# Optimizing a Trainium2 kernel written in Bass

```python
import numpy as np
import jax
import jax.numpy as jnp

def _softmax(x, axis=-1):
    return jax.nn.softmax(x, axis=axis)

def _gelu(x):
    return jax.nn.gelu(x, approximate=True)

def _silu(x):
    return jax.nn.silu(x)

def _sigmoid(x):
    return jax.nn.sigmoid(x)

def _layernorm(x, axis=-1, eps=1e-05):
    m = jnp.mean(x, axis=axis, keepdims=True)
    v = jnp.var(x, axis=axis, keepdims=True)
    return (x - m) / jnp.sqrt(v + eps)

def _scatter_add(tgt, idx, src, axis=0):
    return tgt.at[idx].add(src)

def _segment_sum(src, seg, n):
    return jax.ops.segment_sum(src, seg, n)
kernel_name = 'mk_lm_tower_d1_tok_ids512_r4_09cfe0'

def setup_inputs(seed: int=0):
    np.random.seed(seed)
    _w = jnp.asarray

    def _rec_inputs():
        import jax
        import jax.numpy as jnp
        _rk = jax.random.key(seed)
        x = jax.random.randint(jax.random.fold_in(_rk, 1), (16, 256), 0, 50257, jnp.int32)
        return x
    x = _rec_inputs()

    def _L0_tok_setup():
        import jax, jax.numpy as jnp
        import numpy as np
        VOCAB = 50257
        FEAT = 128
        EPS = 1e-12
        key = jax.random.key(seed)
        k1, k2, k3 = jax.random.split(key, 3)
        token_ids = jax.random.randint(k1, (32, 1024), 0, VOCAB)
        W = jax.random.normal(k2, (FEAT, VOCAB), dtype=jnp.float32) * 0.02
        b = jax.random.normal(k3, (FEAT,), dtype=jnp.float32) * 0.02
        return {'token_ids': token_ids, 'W': W, 'b': b}
    _L0_tok_all = _L0_tok_setup()
    _L0_tok_in = {k: v for k, v in _L0_tok_all.items() if k in ('W', 'b')}
    del _L0_tok_all

    def _L0_attn_setup():
        import jax, jax.numpy as jnp
        import numpy as np
        B_, L_, D_, NB_, MP_ = (8, 512, 128, 4, 8)
        key = jax.random.key(seed)
        ks = jax.random.split(key, 12)

        def rn(k, shape, s=0.02):
            return (jax.random.normal(k, shape) * s).astype(jnp.float32)
        n = jnp.arange(D_, dtype=jnp.float32)
        f = jnp.sqrt(2.0 * n + 1.0)
        f = f / f.max()
        omega = jnp.exp(-f * np.float32(np.log(10000.0)))
        b0 = jnp.sqrt(2.0 * n + 1.0)
        b0 = b0 / b0.max()
        b0_inv = jnp.log(jnp.exp(jnp.clip(b0, 1e-06, None)) - 1.0)
        band_idx = jnp.argsort(-omega).reshape(NB_, D_ // NB_).astype(jnp.int32)
        G = D_ // MP_
        mimo_w = (jnp.eye(MP_, dtype=jnp.float32)[None] + 0.02 * jax.random.normal(ks[8], (G, MP_, MP_))).astype(jnp.float32)
        return {'x': jax.random.normal(ks[0], (B_, L_, D_), jnp.float32), 'omega': omega, 'log_gamma': (jax.random.normal(ks[1], (D_,)) - 3.0).astype(jnp.float32), 'dt': jnp.float32(0.1), 'W_psi': rn(ks[2], (2 * D_, D_)), 'b_psi': jnp.zeros(2 * D_, jnp.float32), 'W_phi': rn(ks[3], (2 * D_, D_)), 'b_phi': jnp.zeros(2 * D_, jnp.float32), 'W_bs': rn(ks[4], (D_, D_)), 'b_bs': b0_inv, 'W_btx': rn(ks[5], (D_, D_)), 'b_btx': b0_inv, 'W_bth': rn(ks[6], (D_, 2 * D_)), 'b_bth': jnp.zeros(D_, jnp.float32), 'w_gate': rn(ks[7], (1, D_)), 'b_gate': jnp.zeros(1, jnp.float32), 'tau': jnp.ones(1, jnp.float32), 'beta': jnp.full((1,), 0.1, jnp.float32), 'mimo_w': mimo_w, 'band_idx': band_idx}
    _L0_attn_all = _L0_attn_setup()
    _L0_attn_in = {k: v for k, v in _L0_attn_all.items() if k in ('omega', 'log_gamma', 'dt', 'W_psi', 'b_psi', 'W_phi', 'b_phi', 'W_bs', 'b_bs', 'W_btx', 'b_btx', 'W_bth', 'b_bth', 'w_gate', 'b_gate', 'tau', 'beta', 'mimo_w', 'band_idx')}
    del _L0_attn_all

    def _L0_ffn_setup():
        import jax, jax.numpy as jnp
        import numpy as np
        B, S, D, F, E = (4, 512, 128, 512, 8)
        key = jax.random.key(seed)
        k = jax.random.split(key, 5)
        x = jax.random.normal(k[0], (B, S, D), dtype=jnp.float32)
        Ws = jax.random.normal(k[1], (D, E), dtype=jnp.float32) * 0.02
        bs = jnp.zeros((E,), dtype=jnp.float32)
        W1 = jax.random.normal(k[2], (E, D, F), dtype=jnp.float32) * 0.02
        b1 = jnp.zeros((E, F), dtype=jnp.float32)
        W2 = jax.random.normal(k[3], (E, F, D), dtype=jnp.float32) * 0.02
        b2 = jnp.zeros((E, D), dtype=jnp.float32)
        return {'x': x, 'Ws': Ws, 'bs': bs, 'W1': W1, 'b1': b1, 'W2': W2, 'b2': b2}
    _L0_ffn_all = _L0_ffn_setup()
    _L0_ffn_in = {k: v for k, v in _L0_ffn_all.items() if k in ('Ws', 'bs', 'W1', 'b1', 'W2', 'b2')}
    del _L0_ffn_all
    return {'x': x, 'L0_tok_W': _L0_tok_in['W'], 'L0_tok_b': _L0_tok_in['b'], 'L0_attn_omega': _L0_attn_in['omega'], 'L0_attn_log_gamma': _L0_attn_in['log_gamma'], 'L0_attn_dt': _L0_attn_in['dt'], 'L0_attn_W_psi': _L0_attn_in['W_psi'], 'L0_attn_b_psi': _L0_attn_in['b_psi'], 'L0_attn_W_phi': _L0_attn_in['W_phi'], 'L0_attn_b_phi': _L0_attn_in['b_phi'], 'L0_attn_W_bs': _L0_attn_in['W_bs'], 'L0_attn_b_bs': _L0_attn_in['b_bs'], 'L0_attn_W_btx': _L0_attn_in['W_btx'], 'L0_attn_b_btx': _L0_attn_in['b_btx'], 'L0_attn_W_bth': _L0_attn_in['W_bth'], 'L0_attn_b_bth': _L0_attn_in['b_bth'], 'L0_attn_w_gate': _L0_attn_in['w_gate'], 'L0_attn_b_gate': _L0_attn_in['b_gate'], 'L0_attn_tau': _L0_attn_in['tau'], 'L0_attn_beta': _L0_attn_in['beta'], 'L0_attn_mimo_w': _L0_attn_in['mimo_w'], 'L0_attn_band_idx': _L0_attn_in['band_idx'], 'L0_ffn_Ws': _L0_ffn_in['Ws'], 'L0_ffn_bs': _L0_ffn_in['bs'], 'L0_ffn_W1': _L0_ffn_in['W1'], 'L0_ffn_b1': _L0_ffn_in['b1'], 'L0_ffn_W2': _L0_ffn_in['W2'], 'L0_ffn_b2': _L0_ffn_in['b2']}

def reference(x, L0_tok_W, L0_tok_b, L0_attn_omega, L0_attn_log_gamma, L0_attn_dt, L0_attn_W_psi, L0_attn_b_psi, L0_attn_W_phi, L0_attn_b_phi, L0_attn_W_bs, L0_attn_b_bs, L0_attn_W_btx, L0_attn_b_btx, L0_attn_W_bth, L0_attn_b_bth, L0_attn_w_gate, L0_attn_b_gate, L0_attn_tau, L0_attn_beta, L0_attn_mimo_w, L0_attn_band_idx, L0_ffn_Ws, L0_ffn_bs, L0_ffn_W1, L0_ffn_b1, L0_ffn_W2, L0_ffn_b2):
    import jax
    import jax.numpy as jnp

    def _L0_tok_ref(token_ids, W, b):
        import jax, jax.numpy as jnp
        import numpy as np
        VOCAB = 50257
        FEAT = 128
        EPS = 1e-12
        feats = W.T[token_ids] + b
        norm = jnp.sqrt(jnp.sum(feats * feats, axis=-1, keepdims=True))
        return feats / jnp.maximum(norm, EPS)

    def _L0_attn_ref(x, omega, log_gamma, dt, W_psi, b_psi, W_phi, b_phi, W_bs, b_bs, W_btx, b_btx, W_bth, b_bth, w_gate, b_gate, tau, beta, mimo_w, band_idx):
        import jax, jax.numpy as jnp
        import numpy as np
        B_, L_, D_, NB_, MP_ = (8, 512, 128, 4, 8)
        B, L, D = x.shape
        K = band_idx.shape[0]
        bsz = D // K
        psi_raw = x @ W_psi.T + b_psi
        psi = jax.lax.complex(psi_raw[..., :D], psi_raw[..., D:])
        phi_raw = x @ W_phi.T + b_phi
        phi = jax.lax.complex(phi_raw[..., :D], phi_raw[..., D:])
        gate = jax.nn.sigmoid(x @ w_gate.T + b_gate)
        dta = jnp.abs(dt)
        lam = jax.lax.complex(-jnp.exp(log_gamma), omega)
        t = jnp.arange(L, dtype=jnp.float32)
        kernel = jnp.exp(lam[None, :] * (t[:, None] * dta))
        n_fft = 2 * L
        K_freq = jnp.fft.fft(kernel.T, n=n_fft, axis=1)

        def causal_fft_conv(U):
            Uf = jnp.fft.fft(jnp.swapaxes(U, 1, 2), n=n_fft, axis=2)
            H = jnp.fft.ifft(Uf * K_freq[None], axis=2)[:, :, :L]
            return jnp.swapaxes(H, 1, 2)
        b_scout = jax.nn.softplus(x @ W_bs.T + b_bs)
        U_scout = gate * b_scout * psi
        H_scout = causal_fft_conv(U_scout)
        H_prev = jnp.pad(H_scout, ((0, 0), (1, 0), (0, 0)))[:, :-1]
        H_prev_flat = jnp.concatenate([H_prev.real, H_prev.imag], axis=-1)
        b_true = jax.nn.softplus(x @ W_btx.T + b_btx + H_prev_flat @ W_bth.T + b_bth)
        U_raw = gate * b_true * psi

        def shift(u, k):
            return jnp.pad(u, ((0, 0), (k, 0), (0, 0)))[:, :L]
        U_s = U_raw * (1.0 / 6.0) + shift(U_raw, 1) * (4.0 / 6.0) + shift(U_raw, 2) * (1.0 / 6.0)
        H = causal_fft_conv(U_s)

        def ln(v):
            m = v.mean(-1, keepdims=True)
            var = v.var(-1, keepdims=True)
            return (v - m) / jnp.sqrt(var + 1e-05)
        H_proj = jax.lax.complex(ln(H.real), ln(H.imag))
        Hb = H_proj[:, :, band_idx]
        Pb = phi[:, :, band_idx]
        alpha = (jnp.conj(Hb) * Pb).sum(-1, keepdims=True) / bsz
        c_k = jax.nn.softmax(jnp.abs(alpha) / jnp.clip(tau, 0.0001, None), axis=2)
        alpha_ig = alpha * c_k * K
        density = (Hb.real ** 2 + Hb.imag ** 2).mean(-1, keepdims=True)
        alpha_fin = alpha_ig + beta * density
        out_bands = (Hb * alpha_fin).real
        out = jnp.zeros((B, L, D), x.dtype).at[:, :, band_idx.reshape(-1)].set(out_bands.reshape(B, L, D))
        G, P = (mimo_w.shape[0], mimo_w.shape[1])
        out = jnp.einsum('gpq,blgq->blgp', mimo_w, out.reshape(B, L, G, P)).reshape(B, L, D)
        return out

    def _L0_ffn_ref(x, Ws, bs, W1, b1, W2, b2):
        import jax, jax.numpy as jnp
        import numpy as np
        B, S, D, F, E = (4, 512, 128, 512, 8)
        Bb, Ss, Dd = x.shape
        xt = x.reshape(-1, Dd)
        logits = xt @ Ws + bs
        probs = jax.nn.softmax(logits, axis=-1)
        prob_max = jnp.max(probs, axis=-1)
        routes = jnp.argmax(probs, axis=-1)
        onehot = jax.nn.one_hot(routes, W1.shape[0], dtype=xt.dtype)

        def expert_ffn(w1, bb1, w2, bb2):
            h = jax.nn.gelu(xt @ w1 + bb1, approximate=False)
            return h @ w2 + bb2
        y = jax.vmap(expert_ffn)(W1, b1, W2, b2)
        out = jnp.einsum('te,etd->td', onehot, y)
        out = out * prob_max[:, None]
        return out.reshape(Bb, Ss, Dd)
    h = _L0_tok_ref(x, L0_tok_W, L0_tok_b)
    h = h + _L0_attn_ref(_layernorm(h, axis=-1), L0_attn_omega, L0_attn_log_gamma, L0_attn_dt, L0_attn_W_psi, L0_attn_b_psi, L0_attn_W_phi, L0_attn_b_phi, L0_attn_W_bs, L0_attn_b_bs, L0_attn_W_btx, L0_attn_b_btx, L0_attn_W_bth, L0_attn_b_bth, L0_attn_w_gate, L0_attn_b_gate, L0_attn_tau, L0_attn_beta, L0_attn_mimo_w, L0_attn_band_idx)
    h = h + _L0_ffn_ref(_layernorm(h, axis=-1), L0_ffn_Ws, L0_ffn_bs, L0_ffn_W1, L0_ffn_b1, L0_ffn_W2, L0_ffn_b2)
    return h

_drawn_inputs = setup_inputs


def setup_inputs(seed=0):
    import zlib

    import numpy as np

    out = dict(_drawn_inputs(seed))
    spreads = {'L0_attn_b_psi': (0.0, 0.1),
     'L0_attn_b_phi': (0.0, 0.1),
     'L0_attn_b_bth': (0.0, 0.1),
     'L0_ffn_bs': (0.0, 0.599),
     'L0_ffn_b1': (0.0, 0.723),
     'L0_ffn_b2': (0.0, 0.1)}
    factors = {}
    for name, (base, spread) in spreads.items():
        noise = np.random.default_rng([zlib.crc32(name.encode()), seed]).standard_normal(out[name].shape)
        drawn = base * np.exp(spread * noise) if base else spread * noise
        out[name] = jnp.asarray(drawn.astype(out[name].dtype))
    for name, factor in factors.items():
        out[name] = (out[name] * factor).astype(out[name].dtype)
    return out
```

```python
from contextlib import ExitStack

import numpy as np

import concourse.bass as bass
from concourse import mybir

ALU = mybir.AluOpType
ACT = mybir.ActivationFunctionType
AX = mybir.AxisListType
F32 = mybir.dt.float32
I32 = mybir.dt.int32

P = 128
BATCH, SEQ, D = 16, 256, 128
T = BATCH * SEQ
TILES = T // P
GT = 4
GN = GT * P
GB = GN // SEQ
G = T // GN
BANDS = 4
BW = D // BANDS
E = 8
F = 512
FC = F // P
REGION = T + P
DUMMY = E * REGION
SLOTS = TILES + E
RC = D + 4
LN_EPS = 1e-5
NORM_EPS2 = 1e-24
TWO_PI = 2.0 * np.pi
PI_A = 6.28125
PI_B = float(np.float32(TWO_PI - PI_A))
PI_C = float(TWO_PI - PI_A - PI_B)
ROUND = 12582912.0

W_PSI, W_PHI, W_BS, W_BTX, W_BTH, W_GATE, W_MIMO, W_PHIN = 0, 2, 4, 5, 6, 8, 9, 10
NW = 12
(C_BPSI, C_BPHI, C_BBS, C_BBTX, C_BBTH, C_OMEGA, C_LGAM, C_DT, C_BGATE, C_TAU, C_BETA) = (0, 2, 4, 5, 6, 7, 8, 9, 10, 11, 12)
NC = 13
K_ADT, K_NR, K_R, K_NBG, K_BT, K_TINV, K_BETA, K_RL, K_T = range(9)


def lm_tower(nc, ids, emb, emb_b, wcat, vecs, band, gate_ws, gate_bs, w1, b1, w2, b2, out):
    sorted_rows = nc.dram_tensor("sorted_rows", [DUMMY + P, RC], F32, kind="Internal").ap()
    out_rows = out.rearrange("b l d -> (b l) d")

    with ExitStack() as ctx:
        def sb(name, shape, dt=F32):
            return ctx.enter_context(nc.sbuf_tensor(name, shape, dt))

        def sem(name):
            return ctx.enter_context(nc.semaphore(name))

        bank = [ctx.enter_context(nc.psum_tensor(f"bank{i}", [P, 512], F32)) for i in range(8)]

        idx = sb("idx", [P, TILES], I32)
        embb = sb("embb", [P, D])
        W = sb("W", [P, NW, P])
        vec = sb("vec", [P, NC])
        bandi = sb("bandi", [P, P], I32)
        bandf = sb("bandf", [P, P])
        gws = sb("gws", [P, E])
        gbs = sb("gbs", [P, E])
        w1s = sb("w1s", [P, E, F])
        w2s = sb("w2s", [P, E, FC * D])
        b1s = sb("b1s", [P, E, F])
        b2s = sb("b2s", [P, E, D])
        kv = sb("kv", [P, 9])
        ident = sb("ident", [P, P])
        upper = sb("upper", [P, P])
        ones = sb("ones", [P, P])
        iota_p = sb("iota_p", [P, 1])
        iota_t = sb("iota_t", [P, SEQ])
        ang = sb("ang", [P, 2, SEQ])
        rnd = sb("rnd", [P, 2, SEQ])
        tab = sb("tab", [P, 3, SEQ])
        decay = sb("decay", [P, 2 * GB, SEQ])
        selz = sb("selz", [P, 3, 3 * BANDS])
        sel5 = sb("sel5", [P, BANDS + 1])
        selT = sb("selT", [3 * BANDS, 2, P])
        mimoC = sb("mimoC", [3 * BANDS, P])
        wq = sb("wq", [P, 2, BANDS + 1])
        bq = sb("bq", [P, 2, BANDS])
        bphib = sb("bphib", [P, 2, P])
        tokid = sb("tokid", [P, TILES])
        expb = sb("expb", [P, E])
        eights = sb("eights", [P, E])
        padrow = sb("padrow", [P, RC])

        rows_buf = sb("rows_buf", [P, SLOTS * RC])
        feat = rows_buf[:, 0:TILES * D].rearrange("p (a b) -> p a b", b=D)
        xr = rows_buf[:, :].rearrange("p (a b) -> p a b", b=RC)
        bnz = sb("bnz", [P, 2, GT, 6])
        mvz = sb("mvz", [P, 2, GT, 2])
        zs = sb("zs", [P, 4, 2, GT])
        zout = sb("zout", [P, 2, 3, GT])
        xn = sb("xn", [P, GT, D])
        xT = sb("xT", [P, 2, GN])

        rot = sb("rot", [P, 4, GN])
        psi = sb("psi", [P, 2, 2, GN])
        gate = sb("gate", [P, 2, GN])
        sp_a = sb("sp_a", [P, 2, GN])
        sp_m = sb("sp_m", [P, 2, GN])
        sp_l = sb("sp_l", [P, 2, GN])
        ga = sb("ga", [P, GN])
        wg = sb("wg", [P, GN])
        u = sb("u", [P, 2, GN])
        g_s = sb("g_s", [P, 2, GN])
        hprev = sb("hprev", [P, 2 * GB, SEQ + 1])
        hpad = sb("hpad", [P, 2 * GB, SEQ + 2])
        fir = sb("fir", [P, 2, GN])
        H = sb("H", [P, 2, 2, GN])
        hsq = sb("hsq", [P, 2, GN])
        xp = sb("xp", [P, 4, GN])

        NSTAT = 10
        st = sb("st", [P, GT, NSTAT, BANDS + 1])
        bt_ = sb("bnd_t", [P, 20, GT, 2, BANDS])
        t12 = sb("t12", [P, GT, 3 * BANDS])
        t12T = sb("t12T", [3 * BANDS, GN])
        e4 = sb("e4", [P, 2, GT, BANDS])
        uu = sb("uu", [P, 2, GN])

        row = sb("row", [P, 2, GT, RC])
        hf = sb("hf", [P, GT, D])
        bnd = sb("bnd", [P, GT, 6])
        mvd = sb("mvd", [P, GT, 2])
        ds_ = sb("ds_", [P, 4, GT])
        x2 = sb("x2", [P, GT, D])
        x2T = sb("x2T", [P, 2, GN])
        lg = sb("lg", [P, GT, E])
        lt = sb("lt", [P, 4, GT, E])
        ex = sb("ex", [P, GT, E])
        oh = sb("oh", [P, GT, E])
        lm = sb("lm", [P, 4, GT])
        pos = sb("pos", [P, 3, GT, E])
        posi = sb("posi", [P, 2, GT], I32)
        base = sb("base", [P, 2, E])

        mp = sb("mp", [P, 8, E])
        mcmp = sb("mcmp", [P, E, TILES])
        mcmp2 = sb("mcmp2", [P, SLOTS, E])
        mt = sb("mt", [P, 8, SLOTS])
        iota_s = sb("iota_s", [P, SLOTS])
        plan = sb("plan", [P, 2 * SLOTS + E], I32)
        hb, hg, hT = rot[:, 0:2, :], rot[:, 2:4, :], u[:, :, :]
        y2, y2T, yb, yo = (g_s[:, r, c:c + 2 * P].rearrange("p (a b) -> p a b", b=P)
                           for r in range(2) for c in (0, 2 * P))
        tick = sb("tick", [P, 1])
        yid = sb("yid", [P, 2, 1], I32)


        names = (
            "idx_in embb_in setup_in weights_in gathered0 gathered1 "
            "pads_made consts_made angles_made lgam_exp decay_log tables_made sel_made sel_turned setup_made "
            "z_stats z_factors xn_made xn_turned xT_made "
            "psi_proj psi_read gate_proj gate_exp gate_made bs_proj bs_read sp1_made w1_made hprev_made "
            "bth_proj bth_read sp2_made w2_made H_made hsq_made phi_proj prod_made "
            "stats_sum stats_copied logits4 exps4 t12_made t12_turned t12_copied spread uu_made mixed "
            "h2_stats d_factors x2_made x2_turned x2T_made router_logits shifted8 exps8 onehot_made "
            "ranks_made pos_made scattered0 scattered1 "
            "plan_made padded rows_in0 rows_in1 rows_in2 rows_in3 rows_in4 rows_in5 rows_in6 rows_in7 "
            "y2_made y2_turned y2T_made hidden hidden_b hidden_g hidden_turned hT_made y_sum y_made "
            "put0 put1 put_ticks y_steps rows_ready "
            "pool_steps act_steps dve_steps f_act_steps").split()
        S = {n: sem(n) for n in names}

        class Steps:

            def __init__(self, eng, name):
                self.eng, self.sem, self.n = eng, S[name], 0

            def go(self, ins):
                self.n += 1
                ins.then_inc(self.sem, 1)

            def wait(self):
                self.eng.wait_ge(self.sem, self.n)

            def __call__(self, ins):
                self.go(ins)
                self.wait()

        def bc(ap, axis, shape):
            return ap.unsqueeze(axis).broadcast_to(shape)

        def rsqrt(step, eng, y, v, t):
            step(eng.tensor_scalar(y.bitcast(I32), v.bitcast(I32), -0.5, 1597463007.0, ALU.mult, ALU.add))
            for _ in range(3):
                step(eng.tensor_tensor(t, y, y, ALU.mult))
                step(eng.tensor_tensor(t, t, v, ALU.mult))
                step(eng.tensor_scalar(t, t, -0.5, 1.5, ALU.mult, ALU.add))
                step(eng.tensor_tensor(y, y, t, ALU.mult))

        def tiles(buf, g):
            return buf[:, g * GT:(g + 1) * GT]

        def at(buf, i):
            if isinstance(i, int):
                return buf[:, i, :]
            return buf[:, bass.ds(i, 1), :].rearrange("p a b -> p (a b)")

        def expert(eng, t):
            return eng.value_load(plan[0:1, t:t + 1] if isinstance(t, int) else plan[0:1, bass.ds(t, 1)],
                                  min_val=0, max_val=E - 1)

        def pipeline(eng, stages):
            first, last = 6, SLOTS - 2

            def slot(t, k, whole):
                for lead, stage in stages:
                    if whole or 0 <= t + k + lead < SLOTS:
                        stage(t + k + lead, (k + lead) % 2)

            for t in range(-2, first, 2):
                for k in range(2):
                    slot(t, k, False)
            with eng.Fori(first, last - 1, 2) as t:
                for k in range(2):
                    slot(t, k, True)
            for t in range(last, SLOTS + 4, 2):
                for k in range(2):
                    slot(t, k, False)

        b4 = lambda ap: ap.rearrange("p (b t) -> p b t", b=GB)

        block = ctx.enter_context(nc.Block())

        @block.sync
        def _(sp):
            sp.dma_start(idx[:, :], ids).then_inc(S["idx_in"], 16)
            sp.dma_start(embb[:, :], emb_b).then_inc(S["embb_in"], 16)
            sp.dma_start(vec[:, :], vecs).then_inc(S["setup_in"], 16)
            sp.dma_start(bandi[:, :], band).then_inc(S["setup_in"], 16)
            sp.dma_start(W[:, :, :], wcat).then_inc(S["setup_in"], 16)
            sp.dma_start(gws[:, :], gate_ws).then_inc(S["setup_in"], 16)
            sp.dma_start(gbs[:, :], gate_bs).then_inc(S["setup_in"], 16)
            sp.dma_start(w1s[:, :, :], w1).then_inc(S["weights_in"], 16)
            sp.dma_start(w2s[:, :, :], w2).then_inc(S["weights_in"], 16)
            sp.dma_start(b1s[:, :, :], b1).then_inc(S["weights_in"], 16)
            sp.dma_start(b2s[:, :, :], b2).then_inc(S["weights_in"], 16)
            sp.wait_ge(S["pads_made"], 1)
            sp.dma_start(sorted_rows[DUMMY:DUMMY + P, :], padrow[:, :]).then_inc(S["padded"], 16)
            sp.wait_ge(S["plan_made"], 1)
            for e in range(E):
                r = sp.value_load(plan[0:1, 2 * SLOTS + e:2 * SLOTS + e + 1], min_val=0, max_val=DUMMY - P)
                sp.dma_start(sorted_rows[bass.ds(r, P), :], padrow[:, :]).then_inc(S["padded"], 16)
            sp.wait_ge(S["padded"], 16 * (E + 1))
            for k in range(2):
                sp.wait_ge(S[f"scattered{k}"], 16 * GT * (G // 2))

            def load(t, k):
                r = sp.value_load(plan[0:1, bass.ds(SLOTS + t, 1)], min_val=0, max_val=DUMMY)
                sp.dma_start(at(xr, t), sorted_rows[bass.ds(r, P), :]).then_inc(S[f"rows_in{k}"], 16)

            for k in range(8):
                load(k, k)
            with sp.Fori(8, SLOTS - 7, 8) as t:
                for k in range(8):
                    sp.wait_ge(S[f"rows_in{k}"], 2 * t)
                    sp.sem_inc(S["rows_ready"], 1)
                    load(t + k, k)
            for k in range(8):
                sp.wait_ge(S[f"rows_in{k}"], 2 * SLOTS)
                sp.sem_inc(S["rows_ready"], 1)
            for k in range(2):
                sp.wait_ge(S[f"put{k}"], 16 * SLOTS // 2)

        @block.gpsimd
        def _(pool):
            step = Steps(pool, "pool_steps")
            tt, ts = pool.tensor_tensor, pool.tensor_scalar
            pool.wait_ge(S["idx_in"], 16)

            def gather(g):
                for t in range(g * GT, (g + 1) * GT):
                    pool.indirect_dma_start(
                        out=feat[:, t, :], out_offset=None, in_=emb,
                        in_offset=bass.IndirectOffsetOnAxis(ap=idx[:, t:t + 1], axis=0),
                    ).then_inc(S[f"gathered{g % 2}"], 16)

            gather(0)
            step(pool.memset(padrow[:, :], 0.0))
            pool.memset(padrow[:, D + 3:D + 4], float(T)).then_inc(S["pads_made"], 1)
            kw = dict(allow_small_or_imprecise_dtypes=True)
            step(pool.memset(ones[:, :], 1.0))
            step(pool.memset(ident[:, :], 0.0))
            step(pool.memset(upper[:, :], 1.0))
            step(pool.affine_select(out=ident[:, :], in_=ident[:, :], compare_op=ALU.not_equal, fill=1.0,
                                    base=0, pattern=[[-1, P]], channel_multiplier=1))
            step(pool.affine_select(out=upper[:, :], in_=upper[:, :], compare_op=ALU.is_gt, fill=0.0,
                                    base=0, pattern=[[1, P]], channel_multiplier=-1))
            step(pool.iota(iota_p[:, :], pattern=[[0, 1]], base=0, channel_multiplier=1, **kw))
            step(pool.iota(iota_t[:, :], pattern=[[1, SEQ]], base=0, channel_multiplier=0, **kw))
            step(pool.iota(iota_s[:, :], pattern=[[1, SLOTS]], base=0, channel_multiplier=0, **kw))
            step(pool.iota(tokid[:, :], pattern=[[P, TILES]], base=0, channel_multiplier=1, **kw))
            step(pool.iota(expb[:, :], pattern=[[REGION, E]], base=0, channel_multiplier=0, **kw))
            step(pool.iota(eights[:, :], pattern=[[-1, E]], base=E, channel_multiplier=0, **kw))
            step(pool.memset(hprev[:, :, :], 0.0))
            step(pool.memset(hpad[:, :, :], 0.0))
            step(pool.memset(selz[:, :, :], 0.0))
            step(pool.memset(sel5[:, :], 1.0))
            step(pool.memset(decay[:, :, :], 1.0))
            step(pool.memset(decay[:, :, 0:1], 0.0))
            pool.memset(base[:, 0, :], 0.0).then_inc(S["consts_made"], 1)
            gather(1)

            def z_factors(g):
                p = g % 2
                pool.wait_ge(S["z_stats"], g + 1)
                if g >= 2:
                    pool.wait_ge(S["xn_made"], g - 1)
                mean, var = mvz[:, p, :, 0], mvz[:, p, :, 1]
                a, v, y, t = (zs[:, k, :, :] for k in range(4))
                step(tt(a[:, 0, :], mean, mean, ALU.mult))
                step(tt(a[:, 0, :], a[:, 0, :], var, ALU.add))
                step(ts(v[:, 0, :], a[:, 0, :], float(D), NORM_EPS2, ALU.mult, ALU.max))
                step(ts(v[:, 1, :], v[:, 0, :], LN_EPS, 0.0, ALU.mult, ALU.add))
                step(tt(v[:, 1, :], v[:, 1, :], var, ALU.add))
                rsqrt(step, pool, y, v, t)
                step(tt(a[:, 1, :], mean, y[:, 1, :], ALU.mult))
                step(ts(zout[:, p, 2, :], a[:, 1, :], -1.0, 0.0, ALU.mult, ALU.add))
                pool.tensor_copy(zout[:, p, 0:2, :], y).then_inc(S["z_factors"], 1)

            full = [P, GT, 2, BANDS]
            B = lambda k: bt_[:, k, :, :, :]
            v2 = lambda k: bt_[:, k, :, :, 0]
            v4 = lambda k: bt_[:, k, :, 0, :]
            m, r, al, dens = v2(0), v2(2), B(8), v4(11)
            mB, rB = bc(m, 3, full), bc(r, 3, full)

            def bands_a(g):
                pool.wait_ge(S["stats_copied"], g + 1)
                if g == 0:
                    pool.wait_ge(S["setup_made"], 1)
                s1, s2, x12, x34, q = (st[:, :, 2 * k:2 * k + 2, 0:BANDS] for k in range(5))
                v, t2 = v2(1), v2(3)
                step(ts(m, st[:, :, 0:2, BANDS], 1.0 / D, 0.0, ALU.mult, ALU.add))
                step(ts(v, st[:, :, 2:4, BANDS], 1.0 / D, 0.0, ALU.mult, ALU.add))
                step(tt(t2, m, m, ALU.mult))
                step(tt(v, v, t2, ALU.subtract))
                step(ts(v, v, 0.0, None, ALU.max))
                step(ts(v, v, 36.0 * LN_EPS, None, ALU.add))
                rsqrt(step, pool, r, v, t2)
                Q = B(5)
                step(tt(Q, q, bc(bq[:, :, :], 1, full), ALU.add))
                ta, tb = B(6), B(7)
                step(tt(ta, Q, mB, ALU.mult))
                step(tt(ta, x12, ta, ALU.subtract))
                step(tt(ta, ta, rB, ALU.mult))
                step(tt(tb[:, :, 0, :], Q[:, :, 1, :], mB[:, :, 0, :], ALU.mult))
                step(tt(tb[:, :, 1, :], Q[:, :, 0, :], mB[:, :, 1, :], ALU.mult))
                step(tt(tb, x34, tb, ALU.subtract))
                step(tt(tb, tb, rB, ALU.mult))
                step(tt(al[:, :, 0, :], ta[:, :, 0, :], ta[:, :, 1, :], ALU.add))
                step(tt(al[:, :, 1, :], tb[:, :, 0, :], tb[:, :, 1, :], ALU.subtract))
                d, nm = B(9), B(10)
                step(ts(nm, mB, float(BW), 0.0, ALU.mult, ALU.add))
                step(ts(d, s1, 2.0, 0.0, ALU.mult, ALU.add))
                step(tt(d, d, nm, ALU.subtract))
                step(tt(d, d, mB, ALU.mult))
                step(tt(d, s2, d, ALU.subtract))
                step(tt(d, d, rB, ALU.mult))
                step(tt(d, d, rB, ALU.mult))
                step(tt(dens, d[:, :, 0, :], d[:, :, 1, :], ALU.add))
                sq, a2, ab, t4, vm, mx = B(12), v4(13), v4(14), v4(15), v4(16), v4(17)
                step(tt(sq, al, al, ALU.mult))
                step(tt(a2, sq[:, :, 0, :], sq[:, :, 1, :], ALU.add))
                step(ts(vm, a2, 1e-30, None, ALU.max))
                rsqrt(step, pool, ab, vm, t4)
                step(tt(ab, ab, a2, ALU.mult))
                step(ts(ab, ab, kv[:, K_TINV:K_TINV + 1], None, ALU.mult))
                for o, a, b in ((mx[:, :, 0:2], ab[:, :, 0:2], ab[:, :, 2:4]),
                                (mx[:, :, 2:3], mx[:, :, 0:1], mx[:, :, 1:2])):
                    step(tt(o, a, b, ALU.subtract))
                    step(ts(o, o, 0.0, None, ALU.max))
                    step(tt(o, o, b, ALU.add))
                tt(e4[:, 0, :, :], ab, mx[:, :, 2:3].broadcast_to([P, GT, BANDS]), ALU.subtract)\
                    .then_inc(S["logits4"], 1)

            def bands_b(g):
                pool.wait_ge(S["exps4"], g + 1)
                ex4, sm, ck, fn, mf, yt = e4[:, 1, :, :], v4(18), v4(13), B(12), B(10), v4(19)
                step(tt(sm[:, :, 0:2], ex4[:, :, 0:2], ex4[:, :, 2:4], ALU.add))
                step(tt(sm[:, :, 2:3], sm[:, :, 0:1], sm[:, :, 1:2], ALU.add))
                y_, t_ = yt[:, :, 0:1], yt[:, :, 1:2]
                rsqrt(step, pool, y_, sm[:, :, 2:3], t_)
                step(tt(t_, y_, y_, ALU.mult))
                step(tt(ck, ex4, t_.broadcast_to([P, GT, BANDS]), ALU.mult))
                step(ts(ck, ck, float(BANDS) / BW, None, ALU.mult))
                step(tt(fn, al, bc(ck, 2, full), ALU.mult))
                step(ts(dens, dens, kv[:, K_BETA:K_BETA + 1], None, ALU.mult))
                step(tt(fn[:, :, 0, :], fn[:, :, 0, :], dens, ALU.add))
                step(tt(fn, fn, rB, ALU.mult))
                step(tt(mf, fn, mB, ALU.mult))
                if g >= 1:
                    pool.wait_ge(S["t12_turned"], g)
                step(ts(t12[:, :, 0:BANDS], fn[:, :, 0, :], 1.0, 0.0, ALU.mult, ALU.add))
                step(ts(t12[:, :, BANDS:2 * BANDS], fn[:, :, 1, :], -1.0, 0.0, ALU.mult, ALU.add))
                tt(t12[:, :, 2 * BANDS:], mf[:, :, 1, :], mf[:, :, 0, :], ALU.subtract).then_inc(S["t12_made"], 1)

            def d_factors(g):
                p = g % 2
                pool.wait_ge(S["h2_stats"], g + 1)
                mean, var = mvd[:, :, 0], mvd[:, :, 1]
                v, y, t = (ds_[:, k, :] for k in range(3))
                step(ts(v, var, LN_EPS, None, ALU.add))
                rsqrt(step, pool, y, v, t)
                step(tt(t, mean, y, ALU.mult))
                step(pool.tensor_copy(row[:, p, :, D:D + 1], y.unsqueeze(2)))
                step(ts(row[:, p, :, D + 1:D + 2], t.unsqueeze(2), -1.0, 0.0, ALU.mult, ALU.add))
                pool.tensor_copy(row[:, p, :, D + 3:D + 4], tiles(tokid, g).unsqueeze(2)).then_inc(S["d_factors"], 1)

            def scatter(g):
                p = g % 2
                pool.wait_ge(S["pos_made"], g + 1)
                for j in range(GT):
                    pool.indirect_dma_start(
                        out=sorted_rows, out_offset=bass.IndirectOffsetOnAxis(ap=posi[:, p, j:j + 1], axis=0),
                        in_=row[:, p, j, :], in_offset=None,
                    ).then_inc(S[f"scattered{p}"], 16)

            z_factors(0)
            z_factors(1)
            for i in range(G + 4):
                if i + 2 < G:
                    pool.wait_ge(S[f"gathered{i % 2}"], 16 * GT * (i // 2 + 1))
                    gather(i + 2)
                if 0 <= i - 2 < G:
                    bands_a(i - 2)
                    bands_b(i - 2)
                if 0 <= i - 2 < G:
                    d_factors(i - 2)
                if i + 2 < G:
                    z_factors(i + 2)
                if 0 <= i - 3 < G:
                    scatter(i - 3)

            def put(t, k):
                if not (isinstance(t, int) and t == 0):
                    pool.wait_ge(S["put_ticks"], t)
                pool.wait_ge(S["y_made"], t + 1)
                tt(tick[:, :], ones[:, 0:1], ones[:, 0:1], ALU.mult).then_inc(S["put_ticks"], 1)
                pool.indirect_dma_start(
                    out=out_rows, out_offset=bass.IndirectOffsetOnAxis(ap=yid[:, k, :], axis=0),
                    in_=yo[:, k, :], in_offset=None, bounds_check=T - 1, oob_is_err=False,
                ).then_inc(S[f"put{k}"], 16)

            for k in range(2):
                put(k, k)
            with pool.Fori(2, SLOTS - 1, 2) as t:
                for k in range(2):
                    put(t + k, k)

        @block.scalar
        def _(act):
            A = act.activation
            step = Steps(act, "act_steps")

            act.wait_ge(S["setup_in"], 80)
            A(kv[:, K_T:K_T + 1], vec[:, C_LGAM:C_LGAM + 1], ACT.Exp).then_inc(S["lgam_exp"], 1)
            act.wait_ge(S["decay_log"], 1)
            A(kv[:, K_R:K_R + 1], kv[:, K_RL:K_RL + 1], ACT.Exp).then_inc(S["tables_made"], 1)
            act.wait_ge(S["angles_made"], 1)
            A(tab[:, 0:2, :], ang[:, :, :], ACT.Sin).then_inc(S["tables_made"], 1)
            A(tab[:, 2, :], ang[:, 0, :], ACT.Sin).then_inc(S["tables_made"], 1)

            def xT_copy(g):
                act.wait_ge(S["xn_turned"], g + 1)
                if g >= 2:
                    act.wait_ge(S["stats_sum"], g - 1)
                A(xT[:, g % 2, :], bank[6][:, :], ACT.Copy).then_inc(S["xT_made"], 1)

            def gates(g):
                p = g % 2
                act.wait_ge(S["gate_proj"], g + 1)
                if g == 0:
                    act.wait_ge(S["setup_made"], 1)
                if g >= 2:
                    act.wait_ge(S["w2_made"], g - 1)
                A(ga[:, :], bank[2][:, :], ACT.Exp, bias=kv[:, K_NBG:K_NBG + 1], scale=-1.0)\
                    .then_inc(S["gate_exp"], 1)
                act.wait_ge(S["gate_exp"], g + 1)
                step(A(gate[:, p, :], ga[:, :], ACT.Ln, bias=1.0))
                A(gate[:, p, :], gate[:, p, :], ACT.Exp, scale=-1.0).then_inc(S["gate_made"], 1)

            def softplus(g, k, proj, read, used, done, x, bias):
                act.wait_ge(S[proj], g + 1)
                if g >= 1:
                    act.wait_ge(S[used], g)
                step.go(A(sp_m[:, k, :], x[:, :], ACT.Relu, bias=bias))
                A(sp_a[:, k, :], x[:, :], ACT.Abs, bias=bias).then_inc(S[read], 1)
                act.wait_ge(S[read], g + 1)
                step(A(sp_a[:, k, :], sp_a[:, k, :], ACT.Exp, scale=-1.0))
                A(sp_l[:, k, :], sp_a[:, k, :], ACT.Ln, bias=1.0).then_inc(S[done], 1)

            xT_copy(0)
            for i in range(G + 4):
                if 0 <= i - 1 < G:
                    softplus(i - 1, 1, "bth_proj", "bth_read", "w2_made", "sp2_made", bank[6], kv[:, K_BT:K_BT + 1])
                if 0 <= i < G:
                    gates(i)
                    softplus(i, 0, "bs_proj", "bs_read", "w1_made", "sp1_made", bank[3], vec[:, C_BBS:C_BBS + 1])
                if 0 <= i - 2 < G:
                    g = i - 2
                    act.wait_ge(S["logits4"], g + 1)
                    A(e4[:, 1, :, :], e4[:, 0, :, :], ACT.Exp).then_inc(S["exps4"], 1)
                    act.wait_ge(S["t12_turned"], g + 1)
                    if g >= 1:
                        act.wait_ge(S["mixed"], g)
                    A(t12T[:, :], bank[7][0:3 * BANDS, :], ACT.Copy).then_inc(S["t12_copied"], 1)
                if 0 <= i - 1 < G:
                    g = i - 1
                    act.wait_ge(S["H_made"], g + 1)
                    if g >= 1:
                        act.wait_ge(S["stats_sum"], g)
                    A(hsq[:, :, :], H[:, g % 2, :, :], ACT.Square).then_inc(S["hsq_made"], 1)
                    act.wait_ge(S["stats_sum"], g + 1)
                    if g >= 1:
                        act.wait_ge(S["logits4"], g)
                    A(st[:, :, :, :].rearrange("p a b c -> p (a b c)"),
                      bank[7][:, 0:GT * NSTAT * (BANDS + 1)], ACT.Copy).then_inc(S["stats_copied"], 1)
                if 0 <= i - 2 < G:
                    g = i - 2
                    act.wait_ge(S["x2_turned"], g + 1)
                    A(x2T[:, g % 2, :], bank[3][:, :], ACT.Copy).then_inc(S["x2T_made"], 1)
                if i + 1 < G:
                    xT_copy(i + 1)
                if 0 <= i - 3 < G:
                    g = i - 3
                    act.wait_ge(S["shifted8"], g + 1)
                    A(ex[:, :, :], lt[:, 0, :, :], ACT.Exp).then_inc(S["exps8"], 1)

            def gelu(t, k):
                act.wait_ge(S["hidden_b"], t + 1)
                if not (isinstance(t, int) and t < 2):
                    act.wait_ge(S["hidden_turned"], t - 1)
                A(hg[:, k, :], hb[:, k, :], ACT.Gelu).then_inc(S["hidden_g"], 1)

            def hT_copy(t, k):
                act.wait_ge(S["hidden_turned"], t + 1)
                if not (isinstance(t, int) and t < 2):
                    act.wait_ge(S["y_sum"], t - 1)
                A(hT[:, k, :], bank[4 + k][:, :], ACT.Copy).then_inc(S["hT_made"], 1)

            pipeline(act, ((0, gelu), (-2, hT_copy)))

        @block.tensor
        def _(pe):
            mm = pe.matmul

            pe.wait_ge(S["sel_made"], 1)
            pe.wait_ge(S["setup_in"], 80)
            for s in range(2):
                pe.transpose(bank[0][0:3 * BANDS, s * P:(s + 1) * P], selz[:, s, :], ident[:, :])
            mm(bank[1][0:3 * BANDS, 0:P], selz[:, 2, :], W[:, W_MIMO, :], start=True, stop=True)
            for r in range(2):
                mm(bank[2][:, r * 5:r * 5 + 5], W[:, W_PHIN + r, :], sel5[:, :], start=True, stop=True)
            for r in range(2):
                last = mm(bank[3][:, r * 4:r * 4 + 4], bphib[:, r, :], sel5[:, 0:BANDS], start=True, stop=True)
            last.then_inc(S["sel_turned"], 1)

            def turn(dst, src, done):
                for j in range(GT):
                    last = pe.transpose(dst[:, j * P:(j + 1) * P], src[:, j, :], ident[:, :])
                last.then_inc(S[done], 1)

            def z_turn(g):
                pe.wait_ge(S["xn_made"], g + 1)
                if g >= 2:
                    pe.wait_ge(S["bth_read"], g - 1)
                turn(bank[6], xn, "xn_turned")

            z_turn(0)
            pe.wait_ge(S["setup_made"], 1)
            for i in range(G + 4):
                if 0 <= i - 1 < G:
                    g = i - 1
                    pe.wait_ge(S["hprev_made"], g + 1)
                    if g + 1 < G:
                        pe.wait_ge(S["xT_made"], g + 2)
                    x = xT[:, g % 2, :]
                    mm(bank[6][:, :], W[:, W_BTX, :], x, start=True, stop=False)
                    for r in range(2):
                        last = mm(bank[6][:, :], W[:, W_BTH + r, :], hprev[:, r * GB:(r + 1) * GB, 0:SEQ],
                                  start=False, stop=(r == 1))
                    last.then_inc(S["bth_proj"], 1)
                if 0 <= i < G:
                    pe.wait_ge(S["xT_made"], i + 1)
                    if i >= 3:
                        pe.wait_ge(S["uu_made"], i - 2)
                    x = xT[:, i % 2, :]
                    for r in range(2):
                        last = mm(bank[r][:, :], W[:, W_PSI + r, :], x, start=True, stop=True)
                    last.then_inc(S["psi_proj"], 1)
                    if i >= 3:
                        pe.wait_ge(S["h2_stats"], i - 2)
                    mm(bank[2][:, :], W[:, W_GATE, :], x, start=True, stop=True).then_inc(S["gate_proj"], 1)
                    if i >= 3:
                        pe.wait_ge(S["x2T_made"], i - 2)
                    mm(bank[3][:, :], W[:, W_BS, :], x, start=True, stop=True).then_inc(S["bs_proj"], 1)
                if 0 <= i - 1 < G:
                    g = i - 1
                    if g >= 1:
                        pe.wait_ge(S["prod_made"], g)
                    for r in range(2):
                        last = mm(bank[4 + r][:, :], W[:, W_PHI + r, :], xT[:, g % 2, :], start=True, stop=True)
                    last.then_inc(S["phi_proj"], 1)
                if 0 <= i - 2 < G:
                    g = i - 2
                    pe.wait_ge(S["t12_made"], g + 1)
                    if g >= 2:
                        pe.wait_ge(S["pos_made"], g - 1)
                    for j in range(GT):
                        last = pe.transpose(bank[7][0:3 * BANDS, j * P:(j + 1) * P], t12[:, j, :], ident[:, :])
                    last.then_inc(S["t12_turned"], 1)
                    pe.wait_ge(S["t12_copied"], g + 1)
                    if i < G:
                        pe.wait_ge(S["psi_read"], i + 1)
                    for r in range(2):
                        last = mm(bank[r][:, :], selT[:, r, :], t12T[:, :], start=True, stop=True)
                    last.then_inc(S["spread"], 1)
                    pe.wait_ge(S["uu_made"], g + 1)
                    if i < G:
                        pe.wait_ge(S["gate_exp"], i + 1)
                    for j in range(GT):
                        c = slice(j * P, (j + 1) * P)
                        for r in range(2):
                            mm(bank[2][:, c], uu[:, r, c], W[:, W_MIMO, :], start=(r == 0), stop=False)
                        last = mm(bank[2][:, c], t12T[:, c], mimoC[:, :], start=False, stop=True)
                    last.then_inc(S["mixed"], 1)
                if 0 <= i - 1 < G:
                    g = i - 1
                    pe.wait_ge(S["hsq_made"], g + 1)
                    pe.wait_ge(S["prod_made"], g + 1)
                    if g >= 1:
                        pe.wait_ge(S["t12_copied"], g)
                    for j in range(GT):
                        c = slice(j * P, (j + 1) * P)
                        srcs = [H[:, g % 2, 0, c], H[:, g % 2, 1, c], hsq[:, 0, c], hsq[:, 1, c]]
                        srcs += [xp[:, k, c] for k in range(4)] + [xT[:, g % 2, c]] * 2
                        for k, s in enumerate(srcs):
                            o = (j * NSTAT + k) * (BANDS + 1)
                            rhs = sel5[:, :] if k < 8 else wq[:, k - 8, :]
                            last = mm(bank[7][:, o:o + BANDS + 1], s, rhs, start=True, stop=True)
                    last.then_inc(S["stats_sum"], 1)
                if 0 <= i - 2 < G:
                    g = i - 2
                    pe.wait_ge(S["x2_made"], g + 1)
                    if i < G:
                        pe.wait_ge(S["bs_read"], i + 1)
                    turn(bank[3], x2, "x2_turned")
                if i + 1 < G:
                    z_turn(i + 1)
                if 0 <= i - 3 < G:
                    g = i - 3
                    pe.wait_ge(S["x2T_made"], g + 1)
                    if g + 2 < G:
                        pe.wait_ge(S["stats_copied"], g + 3)
                    if g >= 1:
                        pe.wait_ge(S["pos_made"], g)
                    for j in range(GT):
                        last = mm(bank[7][:, j * E:(j + 1) * E], x2T[:, g % 2, j * P:(j + 1) * P], gws[:, :],
                                  start=True, stop=True)
                    last.then_inc(S["router_logits"], 1)
                    pe.wait_ge(S["onehot_made"], g + 1)
                    for j in range(GT + 1):
                        o = bank[7][:, j * E:(j + 1) * E]
                        for s in range(j):
                            last = mm(o, ones[:, :], oh[:, s, :], start=(s == 0), stop=(s == j - 1 and j == GT))
                        if j < GT:
                            last = mm(o, upper[:, :], oh[:, j, :], start=(j == 0), stop=True)
                    last.then_inc(S["ranks_made"], 1)

            pe.wait_ge(S["weights_in"], 64)
            pe.wait_ge(S["plan_made"], 1)

            def x_turn(t, k):
                pe.wait_ge(S["y2_made"], t + 1)
                if not (isinstance(t, int) and t < 2):
                    pe.wait_ge(S["y2T_made"], t - 1)
                pe.transpose(bank[k][:, 0:P], y2[:, k, :], ident[:, :]).then_inc(S["y2_turned"], 1)

            def up(t, k):
                pe.wait_ge(S["y2T_made"], t + 1)
                if not (isinstance(t, int) and t < 2):
                    pe.wait_ge(S["hidden_b"], t - 1)
                e = expert(pe, t)
                mm(bank[2 + k][:, :], y2T[:, k, :], at(w1s, e), start=True, stop=True).then_inc(S["hidden"], 1)

            def h_turn(t, k):
                pe.wait_ge(S["hidden_g"], t + 1)
                if not (isinstance(t, int) and t < 2):
                    pe.wait_ge(S["hT_made"], t - 1)
                for c in range(FC):
                    last = pe.transpose(bank[4 + k][:, c * P:(c + 1) * P], hg[:, k, c * P:(c + 1) * P], ident[:, :])
                last.then_inc(S["hidden_turned"], 1)

            def down(t, k):
                pe.wait_ge(S["hT_made"], t + 1)
                if not (isinstance(t, int) and t < 2):
                    pe.wait_ge(S["y_made"], t - 1)
                e = expert(pe, t)
                for c in range(FC):
                    w = w2s[:, bass.ds(e, 1), c * D:(c + 1) * D].rearrange("p a b -> p (a b)")
                    last = mm(bank[6 + k][:, 0:D], hT[:, k, c * P:(c + 1) * P], w, start=(c == 0), stop=(c == FC - 1))
                last.then_inc(S["y_sum"], 1)

            pipeline(pe, ((1, x_turn), (0, up), (-2, h_turn), (-3, down)))

        @block.vector
        def _(dve):
            step = Steps(dve, "dve_steps")
            tt, ts, stt, cp = dve.tensor_tensor, dve.tensor_scalar, dve.scalar_tensor_tensor, dve.tensor_copy
            col = lambda c: vec[:, c:c + 1]
            kc = lambda c: kv[:, c:c + 1]

            dve.wait_ge(S["setup_in"], 80)
            dve.wait_ge(S["consts_made"], 1)
            step(ts(kc(K_ADT), col(C_DT), -1.0, None, ALU.mult))
            step.go(tt(kc(K_ADT), kc(K_ADT), col(C_DT), ALU.max))
            step.go(ts(kc(K_NBG), col(C_BGATE), -1.0, None, ALU.mult))
            step.go(tt(kc(K_BT), col(C_BBTX), col(C_BBTH), ALU.add))
            step.go(ts(kc(K_BETA), col(C_BETA), 1.0 / BW, None, ALU.mult))
            step.go(ts(kc(K_TINV), col(C_TAU), 1e-4, None, ALU.max))
            step.wait()
            step(dve.reciprocal(kc(K_TINV), kc(K_TINV)))
            step.go(ts(kc(K_TINV), kc(K_TINV), 1.0 / BW, None, ALU.mult))
            dve.wait_ge(S["lgam_exp"], 1)
            step(tt(kc(K_RL), kc(K_T), kc(K_ADT), ALU.mult))
            ts(kc(K_RL), kc(K_RL), -1.0, None, ALU.mult).then_inc(S["decay_log"], 1)
            step(ts(ang[:, 1, :], iota_t[:, :], kc(K_ADT), col(C_OMEGA), ALU.mult, ALU.mult))
            step.go(cp(ang[:, 0, :], ang[:, 1, :]))
            step.go(ts(rnd[:, 0, :], ang[:, 1, :], 1.0 / TWO_PI, 0.25, ALU.mult, ALU.add))
            step.go(ts(rnd[:, 1, :], ang[:, 1, :], 1.0 / TWO_PI, None, ALU.mult))
            step.wait()
            step(ts(rnd[:, :, :], rnd[:, :, :], ROUND, None, ALU.add))
            step(ts(rnd[:, :, :], rnd[:, :, :], -ROUND, None, ALU.add))
            for part in (PI_A, PI_B, PI_C):
                step(stt(ang[:, :, :], rnd[:, :, :], -part, ang[:, :, :], ALU.mult, ALU.add))
            step(ts(ang[:, 0, :], ang[:, 0, :], np.pi / 2, None, ALU.add))
            ts(ang[:, :, :], ang[:, :, :], 3.1415925, -3.1415925, ALU.min, ALU.max).then_inc(S["angles_made"], 1)
            step(cp(bandf[:, :], bandi[:, :]))
            step(ts(bandf[:, :], bandf[:, :], iota_p[:, 0:1], None, ALU.is_equal))
            step(dve.tensor_reduce(sel5[:, 0:BANDS], bandf[:, :].rearrange("p (k w) -> p k w", k=BANDS), AX.X, ALU.add))
            for r in range(2):
                step.go(ts(bphib[:, r, :], ones[:, :], col(C_BPHI + r), None, ALU.mult))
            for s in range(3):
                step.go(cp(selz[:, s, s * BANDS:(s + 1) * BANDS], sel5[:, 0:BANDS]))
            step.wait()
            cp(kc(K_T), kc(K_BT)).then_inc(S["sel_made"], 1)
            dve.wait_ge(S["sel_turned"], 1)
            step.go(cp(selT[:, :, :], bank[0][0:3 * BANDS, 0:2 * P].rearrange("p (a b) -> p a b", a=2)))
            step.go(cp(mimoC[:, :], bank[1][0:3 * BANDS, 0:P]))
            step.go(cp(wq[:, :, :], bank[2][:, 0:10].rearrange("p (a b) -> p a b", a=2)))
            step.go(cp(bq[:, :, :], bank[3][:, 0:8].rearrange("p (a b) -> p a b", a=2)))
            dve.wait_ge(S["tables_made"], 3)
            step.wait()
            step(ts(decay[:, :, :], decay[:, :, :], kc(K_R), None, ALU.mult))
            cp(kc(K_T), kc(K_R)).then_inc(S["setup_made"], 1)

            def z_stats(g):
                p = g % 2
                dve.wait_ge(S[f"gathered{p}"], 16 * GT * (g // 2 + 1))
                f = tiles(feat, g)
                step(tt(f, f, bc(embb[:, :], 1, [P, GT, D]), ALU.add))
                if g >= 2:
                    dve.wait_ge(S["z_factors"], g - 1)
                for j in range(GT):
                    step.go(dve.bn_stats(bnz[:, p, j, :], f[:, j, :]))
                step.wait()
                for j in range(GT):
                    last = dve.bn_aggr(mvz[:, p, j, :], bnz[:, p, j, :])
                    if j < GT - 1:
                        step.go(last)
                last.then_inc(S["z_stats"], 1)

            def z_rows(g):
                p = g % 2
                dve.wait_ge(S["z_factors"], g + 1)
                if g >= 1:
                    dve.wait_ge(S["xn_turned"], g)
                f = tiles(feat, g)
                for j in range(GT):
                    last = ts(xn[:, j, :], f[:, j, :], zout[:, p, 1, j:j + 1], zout[:, p, 2, j:j + 1],
                              ALU.mult, ALU.add)
                    step.go(last)
                step.wait()
                for j in range(GT):
                    last = ts(f[:, j, :], f[:, j, :], zout[:, p, 0, j:j + 1], None, ALU.mult)
                    if j < GT - 1:
                        step.go(last)
                last.then_inc(S["xn_made"], 1)

            cs = lambda k: bc(tab[:, k, :], 1, [P, GB, SEQ])
            def cs2(k):
                return bc(tab[:, k:k + 2, :], 2, [P, 2, GB, SEQ])

            def psi_turn(g):
                p = g % 2
                dve.wait_ge(S["psi_proj"], g + 1)
                for k, (r, c) in enumerate(((0, 0), (1, 1), (1, 0), (0, 1))):
                    last = stt(b4(rot[:, k, :]), b4(bank[r][:, :]), col(C_BPSI + r), cs(c), ALU.add, ALU.mult)
                    if k < 3:
                        step.go(last)
                last.then_inc(S["psi_read"], 1)
                dve.wait_ge(S["psi_read"], g + 1)
                step.wait()
                step.go(tt(psi[:, p, 0, :], rot[:, 0, :], rot[:, 1, :], ALU.add))
                step(tt(psi[:, p, 1, :], rot[:, 2, :], rot[:, 3, :], ALU.subtract))

            def scan(g, k, made, w_made, dst, t0, turned=None):
                p = g % 2
                dve.wait_ge(S[made], g + 1)
                step(tt(wg[:, :], sp_m[:, k, :], sp_l[:, k, :], ALU.add))
                if k == 0:
                    dve.wait_ge(S["gate_made"], g + 1)
                tt(wg[:, :], wg[:, :], gate[:, p, :], ALU.mult).then_inc(S[w_made], 1)
                dve.wait_ge(S[w_made], g + 1)
                step(tt(u[:, :, :], psi[:, p, :, :], bc(wg[:, :], 1, [P, 2, GN]), ALU.mult))
                step(dve.tensor_tensor_scan(g_s[:, :, :].rearrange("p a b -> p (a b)"),
                                            decay[:, :, :].rearrange("p a b -> p (a b)"),
                                            u[:, :, :].rearrange("p a b -> p (a b)"), 0.0, ALU.mult, ALU.add))
                gs = g_s[:, :, :].rearrange("p r (b t) -> p r b t", b=GB)
                for q in range(2):
                    step.go(tt(rot[:, 2 * q:2 * q + 2, :].rearrange("p r (b t) -> p r b t", b=GB), gs, cs2(q), ALU.mult))
                step.wait()
                if k == 0 and g >= 1:
                    dve.wait_ge(S["bth_proj"], g)
                for r in range(2):
                    last = tt(dst[:, r * GB:(r + 1) * GB, t0:t0 + SEQ], b4(rot[:, 2 * r, :]), b4(rot[:, 2 * r + 1, :]),
                              (ALU.subtract, ALU.add)[r])
                    if r == 0 or k == 1:
                        step.go(last)
                return last

            def scout(g):
                scan(g, 0, "sp1_made", "w1_made", hprev, 1).then_inc(S["hprev_made"], 1)

            def main_scan(g):
                scan(g, 1, "sp2_made", "w2_made", hpad, 2)
                step.wait()
                tap = lambda k: hpad[:, :, 2 - k:2 - k + SEQ]
                f4 = fir[:, :, :].rearrange("p r (b t) -> p (r b) t", b=GB)
                h4 = H[:, g % 2, :, :].rearrange("p r (b t) -> p (r b) t", b=GB)
                step(stt(f4, tap(1), 4.0, tap(0), ALU.mult, ALU.add))
                if g >= 2:
                    dve.wait_ge(S["stats_sum"], g - 1)
                tt(h4, f4, tap(2), ALU.add).then_inc(S["H_made"], 1)

            def products(g):
                dve.wait_ge(S["H_made"], g + 1)
                dve.wait_ge(S["phi_proj"], g + 1)
                if g >= 1:
                    dve.wait_ge(S["stats_sum"], g)
                for k, (hr, pr) in enumerate(((0, 0), (1, 1), (0, 1), (1, 0))):
                    last = stt(xp[:, k, :], bank[4 + pr][:, :], col(C_BPHI + pr), H[:, g % 2, hr, :], ALU.add, ALU.mult)
                    if k < 3:
                        step.go(last)
                last.then_inc(S["prod_made"], 1)

            def weigh(g):
                dve.wait_ge(S["spread"], g + 1)
                if g >= 1:
                    dve.wait_ge(S["mixed"], g)
                step.go(tt(uu[:, 0, :], H[:, g % 2, 0, :], bank[0][:, :], ALU.mult))
                tt(uu[:, 1, :], H[:, g % 2, 1, :], bank[1][:, :], ALU.mult).then_inc(S["uu_made"], 1)

            def residual(g):
                p = g % 2
                dve.wait_ge(S["mixed"], g + 1)
                if g >= 2:
                    dve.wait_ge(S[f"scattered{p}"], 16 * GT * (g // 2))
                h2 = row[:, p, :, 0:D]
                step(tt(h2, tiles(feat, g), bank[2][:, :].rearrange("p (a b) -> p a b", a=GT), ALU.add))
                for j in range(GT):
                    step.go(dve.bn_stats(bnd[:, j, :], h2[:, j, :]))
                step.wait()
                if g >= 1:
                    dve.wait_ge(S["d_factors"], g)
                for j in range(GT):
                    last = dve.bn_aggr(mvd[:, j, :], bnd[:, j, :])
                    if j < GT - 1:
                        step.go(last)
                last.then_inc(S["h2_stats"], 1)

            def x2_rows(g):
                p = g % 2
                dve.wait_ge(S["d_factors"], g + 1)
                if g >= 1:
                    dve.wait_ge(S["x2_turned"], g)
                for j in range(GT):
                    last = ts(x2[:, j, :], row[:, p, j, 0:D], row[:, p, j, D:D + 1], row[:, p, j, D + 1:D + 2],
                              ALU.mult, ALU.add)
                    if j < GT - 1:
                        step.go(last)
                last.then_inc(S["x2_made"], 1)

            def route(g):
                p = g % 2
                dve.wait_ge(S["router_logits"], g + 1)
                e3 = [P, GT, E]
                first, pick, best = lt[:, 1, :, :], lt[:, 2, :, :], lt[:, 3, :, :]
                step(tt(lg[:, :, :], bank[7][:, 0:GT * E].rearrange("p (a b) -> p a b", a=GT),
                        bc(gbs[:, :], 1, e3), ALU.add))
                step(dve.tensor_reduce(lm[:, 0, :], lg[:, :, :], AX.X, ALU.max))
                tt(lt[:, 0, :, :], lg[:, :, :], bc(lm[:, 0, :], 2, e3), ALU.subtract).then_inc(S["shifted8"], 1)
                step(tt(pick, lg[:, :, :], bc(lm[:, 0, :], 2, e3), ALU.is_ge))
                step(tt(first, pick, bc(eights[:, :], 1, e3), ALU.mult))
                step(dve.tensor_reduce(lm[:, 1, :], first, AX.X, ALU.max))
                tt(oh[:, :, :], first, bc(lm[:, 1, :], 2, e3), ALU.is_equal).then_inc(S["onehot_made"], 1)
                dve.wait_ge(S["exps8"], g + 1)
                step(dve.tensor_reduce(lm[:, 2, :], ex[:, :, :], AX.X, ALU.add))
                step(dve.reciprocal(row[:, p, :, D + 2:D + 3], lm[:, 2, :].unsqueeze(2)))
                a, b = pos[:, 0, :, :], pos[:, 1, :, :]
                step(tt(base[:, 1, :], base[:, 0, :], expb[:, :], ALU.add))
                dve.wait_ge(S["ranks_made"], g + 1)
                dve.wait_ge(S["onehot_made"], g + 1)
                step.go(tt(a, bank[7][:, 0:GT * E].rearrange("p (a b) -> p a b", a=GT), bc(base[:, 1, :], 1, e3), ALU.add))
                step.wait()
                step.go(tt(base[:, 0, :], base[:, 0, :], bank[7][:, GT * E:(GT + 1) * E], ALU.add))
                step(tt(b, a, oh[:, :, :], ALU.mult))
                step(dve.tensor_reduce(lm[:, 3, :], b, AX.X, ALU.add))
                cp(posi[:, p, :], lm[:, 3, :]).then_inc(S["pos_made"], 1)

            z_stats(0)
            z_stats(1)
            z_rows(0)
            for i in range(G + 4):
                if 0 <= i < G:
                    psi_turn(i)
                if 0 <= i - 1 < G:
                    main_scan(i - 1)
                if 0 <= i - 2 < G:
                    weigh(i - 2)
                if 0 <= i - 1 < G:
                    products(i - 1)
                if 0 <= i - 2 < G:
                    residual(i - 2)
                if 0 <= i < G:
                    scout(i)
                if 0 <= i - 2 < G:
                    x2_rows(i - 2)
                if i + 1 < G:
                    z_rows(i + 1)
                if i + 2 < G:
                    z_stats(i + 2)
                if 0 <= i - 3 < G:
                    route(i - 3)

            n_e = base[:, 0, :]
            begun, ends, starts = (mp[:, k, :] for k in range(3))
            full = [P, E, TILES]
            step.go(cp(mcmp[:, :, :], bc(n_e, 2, full)))
            step.go(ts(mp[:, 4, :], expb[:, :], 0.0, 1.0, ALU.mult, ALU.add))
            step.wait()
            step(ts(mt[:, 7, 0:TILES], iota_s[:, 0:TILES], float(P), None, ALU.mult))
            step(tt(mcmp[:, :, :], mcmp[:, :, :], bc(mt[:, 7, 0:TILES], 1, full), ALU.is_gt))
            step(dve.tensor_reduce(begun, mcmp[:, :, :], AX.X, ALU.add))
            step(dve.tensor_tensor_scan(ends, mp[:, 4, :], begun, 0.0, ALU.mult, ALU.add))
            step(tt(starts, ends, begun, ALU.subtract))
            fs = [P, SLOTS, E]
            step(tt(mcmp2[:, :, :], bc(iota_s[:, :], 2, fs), bc(starts, 1, fs), ALU.is_ge))
            step(dve.tensor_reduce(mt[:, 0, :], mcmp2[:, :, :], AX.X, ALU.add))
            step(ts(mt[:, 0, :], mt[:, 0, :], -1.0, None, ALU.add))
            step(tt(mcmp2[:, :, :], mcmp2[:, :, :], bc(starts, 1, fs), ALU.mult))
            step(dve.tensor_reduce(mt[:, 1, :], mcmp2[:, :, :], AX.X, ALU.max))
            step(tt(mt[:, 2, :], iota_s[:, :], mt[:, 1, :], ALU.subtract))
            step(ts(mt[:, 2, :], mt[:, 2, :], float(P), None, ALU.mult))
            step(stt(mt[:, 3, :], mt[:, 0, :], float(REGION), mt[:, 2, :], ALU.mult, ALU.add))
            step(ts(mt[:, 4, :], iota_s[:, :], ends[:, E - 1:E], None, ALU.is_ge))
            step(ts(mt[:, 5, :], mt[:, 3, :], -1.0, float(DUMMY), ALU.mult, ALU.add))
            step(tt(mt[:, 5, :], mt[:, 5, :], mt[:, 4, :], ALU.mult))
            step(tt(mt[:, 3, :], mt[:, 3, :], mt[:, 5, :], ALU.add))
            step(tt(mp[:, 5, :], n_e, expb[:, :], ALU.add))
            step.go(cp(plan[:, 0:SLOTS], mt[:, 0, :]))
            step.go(cp(plan[:, SLOTS:2 * SLOTS], mt[:, 3, :]))
            step.wait()
            cp(plan[:, 2 * SLOTS:], mp[:, 5, :]).then_inc(S["plan_made"], 1)
            dve.wait_ge(S["plan_made"], 1)
            dve.wait_ge(S["weights_in"], 64)

            def f_in(t, k):
                dve.wait_ge(S["rows_ready"], t + 1)
                if not (isinstance(t, int) and t < 2):
                    dve.wait_ge(S["y2_turned"], t - 1)
                ts(y2[:, k, :], at(xr, t)[:, 0:D], at(xr, t)[:, D:D + 1], at(xr, t)[:, D + 1:D + 2], ALU.mult, ALU.add)\
                    .then_inc(S["y2_made"], 1)

            def f_turned(t, k):
                dve.wait_ge(S["y2_turned"], t + 1)
                if not (isinstance(t, int) and t < 2):
                    dve.wait_ge(S["hidden"], t - 1)
                cp(y2T[:, k, :], bank[k][:, 0:P]).then_inc(S["y2T_made"], 1)

            def f_bias(t, k):
                dve.wait_ge(S["hidden"], t + 1)
                if not (isinstance(t, int) and t < 2):
                    dve.wait_ge(S["hidden_g"], t - 1)
                e = expert(dve, t)
                tt(hb[:, k, :], bank[2 + k][:, :], at(b1s, e), ALU.add).then_inc(S["hidden_b"], 1)

            def f_out(t, k):
                dve.wait_ge(S["y_sum"], t + 1)
                if not (isinstance(t, int) and t < 2):
                    dve.wait_ge(S[f"put{k}"], 8 * (t - k))
                e = expert(dve, t)
                tt(yb[:, k, :], bank[6 + k][:, 0:D], at(b2s, e), ALU.add).then_inc(S["y_steps"], 1)
                cp(yid[:, k, :], at(xr, t)[:, D + 3:D + 4]).then_inc(S["y_steps"], 1)
                dve.wait_ge(S["y_steps"], 2 * t + 2)
                stt(yo[:, k, :], yb[:, k, :], at(xr, t)[:, D + 2:D + 3], at(xr, t)[:, 0:D], ALU.mult, ALU.add)\
                    .then_inc(S["y_made"], 1)

            pipeline(dve, ((2, f_in), (1, f_turned), (0, f_bias), (-3, f_out)))


def kernel(x, L0_tok_W, L0_tok_b, L0_attn_omega, L0_attn_log_gamma, L0_attn_dt, L0_attn_W_psi, L0_attn_b_psi,
           L0_attn_W_phi, L0_attn_b_phi, L0_attn_W_bs, L0_attn_b_bs, L0_attn_W_btx, L0_attn_b_btx, L0_attn_W_bth,
           L0_attn_b_bth, L0_attn_w_gate, L0_attn_b_gate, L0_attn_tau, L0_attn_beta, L0_attn_mimo_w,
           L0_attn_band_idx, L0_ffn_Ws, L0_ffn_bs, L0_ffn_W1, L0_ffn_b1, L0_ffn_W2, L0_ffn_b2):
    import concourse.bacc as bacc
    from concourse.bass_utils import run_bass_kernel_spmd

    lay = np.ascontiguousarray
    n = np.asarray
    every = lambda v: lay(np.broadcast_to(n(v).reshape(1, -1), (P, n(v).size)))
    mimo = n(L0_attn_mimo_w)
    groups, width = mimo.shape[0], mimo.shape[1]
    mimo_t = np.zeros((D, D), mimo.dtype)
    for g in range(groups):
        s = slice(g * width, (g + 1) * width)
        mimo_t[s, s] = mimo[g].T
    w_psi, w_phi, w_bth = n(L0_attn_W_psi), n(L0_attn_W_phi), n(L0_attn_W_bth)
    blocks = [w_psi[:D].T, w_psi[D:].T, w_phi[:D].T, w_phi[D:].T, n(L0_attn_W_bs).T, n(L0_attn_W_btx).T,
              w_bth[:, :D].T, w_bth[:, D:].T, np.broadcast_to(n(L0_attn_w_gate).reshape(D, 1), (D, D)),
              mimo_t, w_phi[:D], w_phi[D:]]
    one = lambda v: np.broadcast_to(n(v).reshape(1), (D,))
    b_psi, b_phi = n(L0_attn_b_psi), n(L0_attn_b_phi)
    cols = [b_psi[:D], b_psi[D:], b_phi[:D], b_phi[D:], n(L0_attn_b_bs), n(L0_attn_b_btx), n(L0_attn_b_bth),
            n(L0_attn_omega), n(L0_attn_log_gamma), one(L0_attn_dt), one(L0_attn_b_gate), one(L0_attn_tau),
            one(L0_attn_beta)]
    arrays = {
        "ids": lay(n(x).reshape(TILES, P).T),
        "emb": lay(n(L0_tok_W).T),
        "emb_b": every(L0_tok_b),
        "wcat": lay(np.stack(blocks, axis=1)),
        "vecs": lay(np.stack(cols, axis=1)),
        "band": every(L0_attn_band_idx),
        "gate_ws": lay(n(L0_ffn_Ws)),
        "gate_bs": every(L0_ffn_bs),
        "w1": lay(n(L0_ffn_W1).transpose(1, 0, 2)),
        "b1": every(L0_ffn_b1).reshape(P, E, F),
        "w2": lay(n(L0_ffn_W2).reshape(E, FC, P, D).transpose(2, 0, 1, 3)).reshape(P, E, FC * D),
        "b2": every(L0_ffn_b2).reshape(P, E, D),
    }
    nc = bacc.Bacc("TRN2", target_bir_lowering=False, num_devices=1)
    args = [nc.dram_tensor(f"in_{k}", a.shape, mybir.dt.from_np(a.dtype), kind="ExternalInput").ap()
            for k, a in arrays.items()]
    out = nc.dram_tensor("out", (BATCH, SEQ, D), F32, kind="ExternalOutput").ap()
    lm_tower(nc, *args, out)
    r = run_bass_kernel_spmd(nc, [{f"in_{k}": a for k, a in arrays.items()}], core_ids=[0])
    return r.results[0]["out"]
```

```python
from contextlib import ExitStack

import numpy as np

import concourse.bass as bass
from concourse import mybir

ALU = mybir.AluOpType
ACT = mybir.ActivationFunctionType
AX = mybir.AxisListType
F32 = mybir.dt.float32
I32 = mybir.dt.int32
BF16 = mybir.dt.bfloat16

P = 128
BATCH, SEQ, D = 16, 256, 128
T = BATCH * SEQ
TILES = T // P
GT = 4
GN = GT * P
GB = GN // SEQ
G = T // GN
BANDS = 4
BW = D // BANDS
E = 8
F = 512
FC = F // P
REGION = T + P
DUMMY = E * REGION
SLOTS = TILES + E
RC = D + 4
LN_EPS = 1e-5
NORM_EPS2 = 1e-24
TWO_PI = 2.0 * np.pi
PI_A = 6.28125
PI_B = float(np.float32(TWO_PI - PI_A))
PI_C = float(TWO_PI - PI_A - PI_B)
ROUND = 12582912.0

NSUM_W = BANDS + 1
NPROD = 8
NROW = (NPROD + 2) * NSUM_W

W_PSI, W_PHI, W_BS, W_BTX, W_BTH, W_GATE, W_MIMO, W_PHIN = 0, 2, 4, 5, 6, 8, 9, 10
NW = 12
(C_BPSI, C_BPHI, C_BBS, C_BBTX, C_BBTH, C_OMEGA, C_LGAM, C_DT, C_BGATE, C_TAU, C_BETA) = (0, 2, 4, 5, 6, 7, 8, 9, 10, 11, 12)
NC = 13
K_ADT, K_NR, K_R, K_NBG, K_BT, K_TINV, K_BETA, K_RL, K_T = range(9)


def lm_tower(nc, ids, emb, emb_b, wcat, vecs, band, gate_ws, gate_bs, w1, b1, w2, b2, out):
    sorted_rows = nc.dram_tensor("sorted_rows", [DUMMY + P, RC], F32, kind="Internal").ap()
    out_rows = out.rearrange("b l d -> (b l) d")

    with ExitStack() as ctx:
        def sb(name, shape, dt=F32):
            return ctx.enter_context(nc.sbuf_tensor(name, shape, dt))

        def sem(name):
            return ctx.enter_context(nc.semaphore(name))

        bank = [ctx.enter_context(nc.psum_tensor(f"bank{i}", [P, 512], F32)) for i in range(8)]

        idx = sb("idx", [P, TILES], I32)
        embb = sb("embb", [P, D])
        W = sb("W", [P, NW, P])
        vec = sb("vec", [P, NC])
        bandi = sb("bandi", [P, P], I32)
        bandf = sb("bandf", [P, P])
        gws = sb("gws", [P, E])
        gbs = sb("gbs", [P, E])
        w1s = sb("w1s", [P, E, F])
        w2s = sb("w2s", [P, E, FC * D])
        b1s = sb("b1s", [P, E, F])
        b2s = sb("b2s", [P, E, D])
        kv = sb("kv", [P, 9])
        ident = sb("ident", [P, P])
        upper = sb("upper", [P, P])
        ones = sb("ones", [P, P])
        upper16 = sb("upper16", [P, P], BF16)
        ones16 = sb("ones16", [P, P], BF16)
        iota_p = sb("iota_p", [P, 1])
        iota_t = sb("iota_t", [P, SEQ])
        tab = sb("tab", [P, 3, SEQ])
        decay = sb("decay", [P, 2 * GB, SEQ])
        selz = sb("selz", [P, 3, 3 * BANDS])
        selw = sb("selw", [P, 2 * NROW - NSUM_W])
        sel5 = selw[:, NROW - NSUM_W:NROW]
        selT = sb("selT", [3 * BANDS, 2, P])
        mimoC = sb("mimoC", [3 * BANDS, P])
        wq = sb("wq", [P, NROW])
        bq = sb("bq", [P, 2, BANDS])
        bphib = sb("bphib", [P, 2, P])
        tokid = sb("tokid", [P, TILES])
        expb = sb("expb", [P, E])
        eights = sb("eights", [P, E])
        padrow = sb("padrow", [P, RC])

        rows_buf = sb("rows_buf", [P, SLOTS * RC])
        feat = rows_buf[:, 0:TILES * D].rearrange("p (a b) -> p a b", b=D)
        xr = rows_buf[:, :].rearrange("p (a b) -> p a b", b=RC)
        bnz = sb("bnz", [P, 2, GT, 6])
        mvz = sb("mvz", [P, 2, GT, 2])
        zs = sb("zs", [P, 4, 2, GT])
        zout = sb("zout", [P, 2, 3, GT])
        xn = sb("xn", [P, GT, D])
        xT = sb("xT", [P, 4, GN])

        rot = sb("rot", [P, 4, GN])
        ang = rot[:, 0, :].rearrange("p (a t) -> p a t", a=2)
        psi = sb("psi", [P, 2, 2, GN])
        gate = sb("gate", [P, 2, GN])
        sp_a = sb("sp_a", [P, 2, GN])
        sp_m = sb("sp_m", [P, 2, GN])
        sp_l = sb("sp_l", [P, 2, GN])
        ga = sb("ga", [P, GN])
        wg = sb("wg", [P, GN])
        u = sb("u", [P, 2, GN])
        g_s = sb("g_s", [P, 2, GN])
        hprev = sb("hprev", [P, 2 * GB, SEQ + 1])
        hpad = sb("hpad", [P, 2 * GB, SEQ + 2])
        fir = sb("fir", [P, 2, GN])
        rnd = fir[:, :, 0:SEQ]
        H = sb("H", [P, 3, 2, GN])
        hsq = sb("hsq", [P, 2, GN])
        xp = sb("xp", [P, 4, GN])

        st = sb("st", [P, GT, NPROD + 2, NSUM_W])
        turned = sb("turned", [NROW, GN])
        bt_ = sb("bnd_t", [P, 20, GT, 2, BANDS])
        t12 = sb("t12", [P, GT, 3 * BANDS])
        t12T = turned[0:3 * BANDS, :]
        e4 = sb("e4", [P, 2, GT, BANDS])
        lns = sb("lns", [P, 2, GT])
        uu = sb("uu", [P, 2, GN])

        row = sb("row", [P, 2, GT, RC])
        bnd = sb("bnd", [P, GT, 6])
        mvd = sb("mvd", [P, GT, 2])
        ds_ = sb("ds_", [P, 4, GT])
        x2 = sb("x2", [P, GT, D])
        x2T = sb("x2T", [P, GN])
        lg = sb("lg", [P, GT, E])
        lt = sb("lt", [P, 4, GT, E])
        ex = sb("ex", [P, GT, E])
        oh = sb("oh", [P, GT, E], BF16)
        lm = sb("lm", [P, 4, GT])
        pos = sb("pos", [P, 3, GT, E])
        posi = sb("posi", [P, 2, GT], I32)
        base = sb("base", [P, 2, E])

        mp = sb("mp", [P, 8, E])
        mcmp = fir[:, 0, 0:E * TILES].rearrange("p (a b) -> p a b", b=TILES)
        mcmp2 = fir[:, 1, 0:SLOTS * E].rearrange("p (a b) -> p a b", b=E)
        mt = sb("mt", [P, 7, SLOTS])
        iota_s = sb("iota_s", [P, SLOTS])
        plan = sb("plan", [P, 2 * SLOTS + E], I32)
        hb, hg, hT = rot[:, 0:2, :], rot[:, 2:4, :], u[:, :, :]
        y2, y2T, yb, yo = (g_s[:, r, c:c + 2 * P].rearrange("p (a b) -> p a b", b=P)
                           for r in range(2) for c in (0, 2 * P))
        tick = sb("tick", [P, 1])
        yid = sb("yid", [P, 2, 1], I32)


        names = (
            "idx_in embb_in setup_in weights_in gathered0 gathered1 "
            "pads_made consts_made angles_made lgam_exp decay_log tables_made sel_made sel_turned setup_made "
            "z_stats z_factors xn_made xn_turned xT_made "
            "psi_proj psi_read gate_proj gate_exp gate_made bs_proj bs_read sp1_made w1_made hprev_made "
            "bth_proj bth_read sp2_made w2_made H_made hsq_made phi_proj prod_made "
            "stats_sum sums_copied stats_turned stats_copied logits4 exps4 sum4 lnsum4 log4 soft4 t12_made t12_turned t12_copied spread uu_made mixed mixed_copied mixed_turned "
            "h2_stats x2_made x2_turned x2T_made router_logits logits_read shifted8 exps8 onehot_made "
            "ranks_made pos_made scattered0 scattered1 "
            "plan_made padded rows_in0 rows_in1 rows_in2 rows_in3 rows_in4 rows_in5 rows_in6 rows_in7 "
            "y2_made y2_turned y2T_made hidden hidden_b hidden_g hidden_turned hT_made y_sum y_made "
            "put0 put1 put_ticks y_steps rows_ready "
            "pool_steps act_steps dve_steps f_act_steps").split()
        S = {n: sem(n) for n in names}

        class Steps:

            def __init__(self, eng, name):
                self.eng, self.sem, self.n = eng, S[name], 0

            def go(self, ins):
                self.n += 1
                ins.then_inc(self.sem, 1)

            def wait(self):
                self.eng.wait_ge(self.sem, self.n)

            def __call__(self, ins):
                self.go(ins)
                self.wait()

        def wait(eng, name, n):
            if n > 0:
                eng.wait_ge(S[name], min(n, G))

        def bc(ap, axis, shape):
            return ap.unsqueeze(axis).broadcast_to(shape)

        def rsqrt(step, eng, y, v, t):
            step(eng.tensor_scalar(y.bitcast(I32), v.bitcast(I32), -0.5, 1597463007.0, ALU.mult, ALU.add))
            for _ in range(3):
                step(eng.tensor_tensor(t, y, y, ALU.mult))
                step(eng.tensor_tensor(t, t, v, ALU.mult))
                step(eng.tensor_scalar(t, t, -0.5, 1.5, ALU.mult, ALU.add))
                step(eng.tensor_tensor(y, y, t, ALU.mult))

        def tiles(buf, g):
            return buf[:, g * GT:(g + 1) * GT]

        def at(buf, i):
            if isinstance(i, int):
                return buf[:, i, :]
            return buf[:, bass.ds(i, 1), :].rearrange("p a b -> p (a b)")

        def expert(eng, t):
            return eng.value_load(plan[0:1, t:t + 1] if isinstance(t, int) else plan[0:1, bass.ds(t, 1)],
                                  min_val=0, max_val=E - 1)

        def pipeline(eng, stages):
            first, last = 6, SLOTS - 2

            def slot(t, k, whole):
                for lead, stage in stages:
                    if whole or 0 <= t + k + lead < SLOTS:
                        stage(t + k + lead, (k + lead) % 2)

            for t in range(-2, first, 2):
                for k in range(2):
                    slot(t, k, False)
            with eng.Fori(first, last - 1, 2) as t:
                for k in range(2):
                    slot(t, k, True)
            for t in range(last, SLOTS + 4, 2):
                for k in range(2):
                    slot(t, k, False)

        b4 = lambda ap: ap.rearrange("p (b t) -> p b t", b=GB)

        block = ctx.enter_context(nc.Block())

        @block.sync
        def _(sp):
            sp.dma_start(idx[:, :], ids).then_inc(S["idx_in"], 16)
            sp.dma_start(embb[:, :], emb_b).then_inc(S["embb_in"], 16)
            sp.dma_start(vec[:, :], vecs).then_inc(S["setup_in"], 16)
            sp.dma_start(bandi[:, :], band).then_inc(S["setup_in"], 16)
            sp.dma_start(W[:, :, :], wcat).then_inc(S["setup_in"], 16)
            sp.dma_start(gws[:, :], gate_ws).then_inc(S["setup_in"], 16)
            sp.dma_start(gbs[:, :], gate_bs).then_inc(S["setup_in"], 16)
            sp.dma_start(w1s[:, :, :], w1).then_inc(S["weights_in"], 16)
            sp.dma_start(w2s[:, :, :], w2).then_inc(S["weights_in"], 16)
            sp.dma_start(b1s[:, :, :], b1).then_inc(S["weights_in"], 16)
            sp.dma_start(b2s[:, :, :], b2).then_inc(S["weights_in"], 16)
            sp.wait_ge(S["pads_made"], 1)
            sp.dma_start(sorted_rows[DUMMY:DUMMY + P, :], padrow[:, :]).then_inc(S["padded"], 16)
            sp.wait_ge(S["plan_made"], 1)
            for e in range(E):
                r = sp.value_load(plan[0:1, 2 * SLOTS + e:2 * SLOTS + e + 1], min_val=0, max_val=DUMMY - P)
                sp.dma_start(sorted_rows[bass.ds(r, P), :], padrow[:, :]).then_inc(S["padded"], 16)
            sp.wait_ge(S["padded"], 16 * (E + 1))
            for k in range(2):
                sp.wait_ge(S[f"scattered{k}"], 16 * GT * (G // 2))

            def load(t, k):
                r = sp.value_load(plan[0:1, bass.ds(SLOTS + t, 1)], min_val=0, max_val=DUMMY)
                sp.dma_start(at(xr, t), sorted_rows[bass.ds(r, P), :]).then_inc(S[f"rows_in{k}"], 16)

            for k in range(8):
                load(k, k)
            with sp.Fori(8, SLOTS - 7, 8) as t:
                for k in range(8):
                    sp.wait_ge(S[f"rows_in{k}"], 2 * t)
                    sp.sem_inc(S["rows_ready"], 1)
                    load(t + k, k)
            for k in range(8):
                sp.wait_ge(S[f"rows_in{k}"], 2 * SLOTS)
                sp.sem_inc(S["rows_ready"], 1)
            for k in range(2):
                sp.wait_ge(S[f"put{k}"], 16 * SLOTS // 2)

        @block.gpsimd
        def _(pool):
            step = Steps(pool, "pool_steps")
            tt, ts = pool.tensor_tensor, pool.tensor_scalar
            pool.wait_ge(S["idx_in"], 16)

            def gather(g):
                for t in range(g * GT, (g + 1) * GT):
                    pool.indirect_dma_start(
                        out=feat[:, t, :], out_offset=None, in_=emb,
                        in_offset=bass.IndirectOffsetOnAxis(ap=idx[:, t:t + 1], axis=0),
                    ).then_inc(S[f"gathered{g % 2}"], 16)

            gather(0)
            step(pool.memset(padrow[:, :], 0.0))
            pool.memset(padrow[:, D + 3:D + 4], float(T)).then_inc(S["pads_made"], 1)
            kw = dict(allow_small_or_imprecise_dtypes=True)
            step(pool.memset(ones[:, :], 1.0))
            step(pool.memset(ident[:, :], 0.0))
            step(pool.memset(upper[:, :], 1.0))
            step(pool.affine_select(out=ident[:, :], in_=ident[:, :], compare_op=ALU.not_equal, fill=1.0,
                                    base=0, pattern=[[-1, P]], channel_multiplier=1))
            step(pool.affine_select(out=upper[:, :], in_=upper[:, :], compare_op=ALU.is_gt, fill=0.0,
                                    base=0, pattern=[[1, P]], channel_multiplier=-1))
            step(pool.tensor_copy(upper16[:, :], upper[:, :]))
            step(pool.tensor_copy(ones16[:, :], ones[:, :]))
            step(pool.iota(iota_p[:, :], pattern=[[0, 1]], base=0, channel_multiplier=1, **kw))
            step(pool.iota(iota_t[:, :], pattern=[[1, SEQ]], base=0, channel_multiplier=0, **kw))
            step(pool.iota(iota_s[:, :], pattern=[[1, SLOTS]], base=0, channel_multiplier=0, **kw))
            step(pool.iota(tokid[:, :], pattern=[[P, TILES]], base=0, channel_multiplier=1, **kw))
            step(pool.iota(expb[:, :], pattern=[[REGION, E]], base=0, channel_multiplier=0, **kw))
            step(pool.iota(eights[:, :], pattern=[[-1, E]], base=E, channel_multiplier=0, **kw))
            step(pool.memset(hprev[:, :, :], 0.0))
            step(pool.memset(hpad[:, :, :], 0.0))
            step(pool.memset(selz[:, :, :], 0.0))
            step(pool.memset(selw[:, :], 0.0))
            step(pool.memset(wq[:, :], 0.0))
            step(pool.memset(sel5[:, BANDS:], 1.0))
            step(pool.memset(decay[:, :, :], 1.0))
            step(pool.memset(decay[:, :, 0:1], 0.0))
            pool.memset(base[:, 0, :], 0.0).then_inc(S["consts_made"], 1)
            gather(1)

            def z_factors(g):
                p = g % 2
                pool.wait_ge(S["z_stats"], g + 1)
                if g >= 2:
                    pool.wait_ge(S["xn_made"], g - 1)
                mean, var = mvz[:, p, :, 0], mvz[:, p, :, 1]
                a, v, y, t = (zs[:, k, :, :] for k in range(4))
                step(tt(a[:, 0, :], mean, mean, ALU.mult))
                step(tt(a[:, 0, :], a[:, 0, :], var, ALU.add))
                step(ts(v[:, 0, :], a[:, 0, :], float(D), NORM_EPS2, ALU.mult, ALU.max))
                step(ts(v[:, 1, :], v[:, 0, :], LN_EPS, 0.0, ALU.mult, ALU.add))
                step(tt(v[:, 1, :], v[:, 1, :], var, ALU.add))
                rsqrt(step, pool, y, v, t)
                step(tt(a[:, 1, :], mean, y[:, 1, :], ALU.mult))
                step(ts(zout[:, p, 2, :], a[:, 1, :], -1.0, 0.0, ALU.mult, ALU.add))
                pool.tensor_copy(zout[:, p, 0:2, :], y).then_inc(S["z_factors"], 1)

            full = [P, GT, 2, BANDS]
            B = lambda k: bt_[:, k, :, :, :]
            v2 = lambda k: bt_[:, k, :, :, 0]
            v4 = lambda k: bt_[:, k, :, 0, :]
            m, r, al, dens = v2(0), v2(2), B(8), v4(11)
            mB, rB = bc(m, 3, full), bc(r, 3, full)

            def bands_a(g):
                pool.wait_ge(S["stats_copied"], g + 1)
                if g == 0:
                    pool.wait_ge(S["setup_made"], 1)
                s1, s2, x12, x34, q = (st[:, :, 2 * k:2 * k + 2, 0:BANDS] for k in range(5))
                v, t2 = v2(1), v2(3)
                step(ts(m, st[:, :, 0:2, BANDS], 1.0 / D, 0.0, ALU.mult, ALU.add))
                step(ts(v, st[:, :, 2:4, BANDS], 1.0 / D, 0.0, ALU.mult, ALU.add))
                step(tt(t2, m, m, ALU.mult))
                step(tt(v, v, t2, ALU.subtract))
                step(ts(v, v, 0.0, None, ALU.max))
                step(ts(v, v, 36.0 * LN_EPS, None, ALU.add))
                rsqrt(step, pool, r, v, t2)
                Q = B(5)
                step(tt(Q, q, bc(bq[:, :, :], 1, full), ALU.add))
                ta, tb = B(6), B(7)
                step(tt(ta, Q, mB, ALU.mult))
                step(tt(ta, x12, ta, ALU.subtract))
                step(tt(ta, ta, rB, ALU.mult))
                step(tt(tb[:, :, 0, :], Q[:, :, 1, :], mB[:, :, 0, :], ALU.mult))
                step(tt(tb[:, :, 1, :], Q[:, :, 0, :], mB[:, :, 1, :], ALU.mult))
                step(tt(tb, x34, tb, ALU.subtract))
                step(tt(tb, tb, rB, ALU.mult))
                step(tt(al[:, :, 0, :], ta[:, :, 0, :], ta[:, :, 1, :], ALU.add))
                step(tt(al[:, :, 1, :], tb[:, :, 0, :], tb[:, :, 1, :], ALU.subtract))
                d, nm = B(9), B(10)
                step(ts(nm, mB, float(BW), 0.0, ALU.mult, ALU.add))
                step(ts(d, s1, 2.0, 0.0, ALU.mult, ALU.add))
                step(tt(d, d, nm, ALU.subtract))
                step(tt(d, d, mB, ALU.mult))
                step(tt(d, s2, d, ALU.subtract))
                step(tt(d, d, rB, ALU.mult))
                step(tt(d, d, rB, ALU.mult))
                step(tt(dens, d[:, :, 0, :], d[:, :, 1, :], ALU.add))
                sq, a2, ab, t4, vm, mx = B(12), v4(13), v4(14), v4(15), v4(16), v4(17)
                step(tt(sq, al, al, ALU.mult))
                step(tt(a2, sq[:, :, 0, :], sq[:, :, 1, :], ALU.add))
                step(ts(vm, a2, 1e-30, None, ALU.max))
                rsqrt(step, pool, ab, vm, t4)
                step(tt(ab, ab, a2, ALU.mult))
                step(ts(ab, ab, kv[:, K_TINV:K_TINV + 1], None, ALU.mult))
                for o, a, b in ((mx[:, :, 0:2], ab[:, :, 0:2], ab[:, :, 2:4]),
                                (mx[:, :, 2:3], mx[:, :, 0:1], mx[:, :, 1:2])):
                    step(tt(o, a, b, ALU.subtract))
                    step(ts(o, o, 0.0, None, ALU.max))
                    step(tt(o, o, b, ALU.add))
                tt(e4[:, 0, :, :], ab, mx[:, :, 2:3].broadcast_to([P, GT, BANDS]), ALU.subtract)\
                    .then_inc(S["logits4"], 1)

            def bands_b(g):
                pool.wait_ge(S["exps4"], g + 1)
                ex4, sm, ck, fn, mf = e4[:, 1, :, :], v4(18), v4(13), B(12), B(10)
                step(tt(sm[:, :, 0:2], ex4[:, :, 0:2], ex4[:, :, 2:4], ALU.add))
                tt(lns[:, 0, :], sm[:, :, 0], sm[:, :, 1], ALU.add).then_inc(S["sum4"], 1)
                pool.wait_ge(S["lnsum4"], g + 1)
                tt(e4[:, 0, :, :], e4[:, 0, :, :], bc(lns[:, 1, :], 2, [P, GT, BANDS]), ALU.subtract)\
                    .then_inc(S["log4"], 1)
                pool.wait_ge(S["soft4"], g + 1)
                step(ts(ck, ex4, float(BANDS) / BW, None, ALU.mult))
                step(tt(fn, al, bc(ck, 2, full), ALU.mult))
                step(ts(dens, dens, kv[:, K_BETA:K_BETA + 1], None, ALU.mult))
                step(tt(fn[:, :, 0, :], fn[:, :, 0, :], dens, ALU.add))
                step(tt(fn, fn, rB, ALU.mult))
                step(tt(mf, fn, mB, ALU.mult))
                if g >= 1:
                    pool.wait_ge(S["t12_turned"], g)
                step(ts(t12[:, :, 0:BANDS], fn[:, :, 0, :], 1.0, 0.0, ALU.mult, ALU.add))
                step(ts(t12[:, :, BANDS:2 * BANDS], fn[:, :, 1, :], -1.0, 0.0, ALU.mult, ALU.add))
                tt(t12[:, :, 2 * BANDS:], mf[:, :, 1, :], mf[:, :, 0, :], ALU.subtract).then_inc(S["t12_made"], 1)

            def scatter(g):
                p = g % 2
                pool.wait_ge(S["pos_made"], g + 1)
                for j in range(GT):
                    pool.indirect_dma_start(
                        out=sorted_rows, out_offset=bass.IndirectOffsetOnAxis(ap=posi[:, p, j:j + 1], axis=0),
                        in_=row[:, p, j, :], in_offset=None,
                    ).then_inc(S[f"scattered{p}"], 16)

            def next_gather(g):
                pool.wait_ge(S[f"gathered{g % 2}"], 16 * GT * (g // 2))
                gather(g)

            z_factors(0)
            next_gather(2)
            z_factors(1)
            next_gather(3)
            z_factors(2)
            for i in range(G + 5):
                if 0 <= i - 2 < G:
                    bands_a(i - 2)
                if 0 <= i - 4 < G:
                    scatter(i - 4)
                if 0 <= i - 2 < G:
                    bands_b(i - 2)
                if i + 4 < G:
                    next_gather(i + 4)
                if i + 3 < G:
                    z_factors(i + 3)

            def put(t, k):
                if not (isinstance(t, int) and t == 0):
                    pool.wait_ge(S["put_ticks"], t)
                pool.wait_ge(S["y_made"], t + 1)
                tt(tick[:, :], ones[:, 0:1], ones[:, 0:1], ALU.mult).then_inc(S["put_ticks"], 1)
                pool.indirect_dma_start(
                    out=out_rows, out_offset=bass.IndirectOffsetOnAxis(ap=yid[:, k, :], axis=0),
                    in_=yo[:, k, :], in_offset=None, bounds_check=T - 1, oob_is_err=False,
                ).then_inc(S[f"put{k}"], 16)

            for k in range(2):
                put(k, k)
            with pool.Fori(2, SLOTS - 1, 2) as t:
                for k in range(2):
                    put(t + k, k)

        @block.scalar
        def _(act):
            A = act.activation
            step = Steps(act, "act_steps")

            act.wait_ge(S["setup_in"], 80)
            A(kv[:, K_T:K_T + 1], vec[:, C_LGAM:C_LGAM + 1], ACT.Exp).then_inc(S["lgam_exp"], 1)
            act.wait_ge(S["decay_log"], 1)
            A(kv[:, K_R:K_R + 1], kv[:, K_RL:K_RL + 1], ACT.Exp).then_inc(S["tables_made"], 1)
            act.wait_ge(S["angles_made"], 1)
            A(tab[:, 0:2, :], ang[:, :, :], ACT.Sin).then_inc(S["tables_made"], 1)
            A(tab[:, 2, :], ang[:, 0, :], ACT.Sin).then_inc(S["tables_made"], 1)

            def xT_copy(g):
                act.wait_ge(S["xn_turned"], g + 1)
                wait(act, "stats_sum", g - 3)
                A(xT[:, g % 4, :], bank[6][:, :], ACT.Copy).then_inc(S["xT_made"], 1)

            def gate_exp(g):
                act.wait_ge(S["gate_proj"], g + 1)
                wait(act, "mixed_turned", g - 3)
                if g == 0:
                    act.wait_ge(S["setup_made"], 1)
                A(ga[:, :], bank[2][:, :], ACT.Exp, bias=kv[:, K_NBG:K_NBG + 1], scale=-1.0)\
                    .then_inc(S["gate_exp"], 1)

            def gate_rest(g):
                p = g % 2
                act.wait_ge(S["gate_exp"], g + 1)
                if g >= 2:
                    act.wait_ge(S["w2_made"], g - 1)
                step(A(gate[:, p, :], ga[:, :], ACT.Ln, bias=1.0))
                A(gate[:, p, :], gate[:, p, :], ACT.Exp, scale=-1.0).then_inc(S["gate_made"], 1)

            def softplus(g, k, proj, read, used, done, x, bias):
                act.wait_ge(S[proj], g + 1)
                if g >= 1:
                    act.wait_ge(S[used], g)
                step.go(A(sp_m[:, k, :], x[:, :], ACT.Relu, bias=bias))
                A(sp_a[:, k, :], x[:, :], ACT.Abs, bias=bias).then_inc(S[read], 1)
                act.wait_ge(S[read], g + 1)
                step(A(sp_a[:, k, :], sp_a[:, k, :], ACT.Exp, scale=-1.0))
                A(sp_l[:, k, :], sp_a[:, k, :], ACT.Ln, bias=1.0).then_inc(S[done], 1)

            def exps4(g):
                act.wait_ge(S["logits4"], g + 1)
                A(e4[:, 1, :, :], e4[:, 0, :, :], ACT.Exp).then_inc(S["exps4"], 1)
                act.wait_ge(S["sum4"], g + 1)
                A(lns[:, 1, :], lns[:, 0, :], ACT.Ln).then_inc(S["lnsum4"], 1)
                act.wait_ge(S["log4"], g + 1)
                A(e4[:, 1, :, :], e4[:, 0, :, :], ACT.Exp).then_inc(S["soft4"], 1)

            xT_copy(0)
            xT_copy(1)
            for i in range(G + 5):
                if 0 <= i - 3 < G:
                    act.wait_ge(S["t12_turned"], i - 2)
                    wait(act, "mixed", i - 3)
                    wait(act, "stats_turned", i - 1)
                    A(t12T[:, :], bank[7][0:3 * BANDS, :], ACT.Copy).then_inc(S["t12_copied"], 1)
                if 0 <= i - 1 < G:
                    softplus(i - 1, 1, "bth_proj", "bth_read", "w2_made", "sp2_made", bank[6], kv[:, K_BT:K_BT + 1])
                if 0 <= i < G:
                    gate_exp(i)
                if 0 <= i - 4 < G:
                    act.wait_ge(S["shifted8"], i - 3)
                    A(ex[:, :, :], lt[:, 0, :, :], ACT.Exp).then_inc(S["exps8"], 1)
                if 0 <= i < G:
                    gate_rest(i)
                    softplus(i, 0, "bs_proj", "bs_read", "w1_made", "sp1_made", bank[3], vec[:, C_BBS:C_BBS + 1])
                if 0 <= i - 3 < G:
                    act.wait_ge(S["mixed"], i - 2)
                    A(ga[:, :], bank[2][:, :], ACT.Copy).then_inc(S["mixed_copied"], 1)
                if 0 <= i - 2 < G:
                    exps4(i - 2)
                if 0 <= i - 1 < G:
                    g = i - 1
                    act.wait_ge(S["H_made"], g + 1)
                    wait(act, "stats_sum", g)
                    A(hsq[:, :, :], H[:, g % 3, :, :], ACT.Square).then_inc(S["hsq_made"], 1)
                if 0 <= i - 1 < G:
                    g = i - 1
                    act.wait_ge(S["stats_sum"], g + 1)
                    A(turned[:, :], bank[7][0:NROW, :], ACT.Copy).then_inc(S["sums_copied"], 1)
                    act.wait_ge(S["stats_turned"], g + 1)
                    wait(act, "logits4", g)
                    A(st[:, :, :, :].rearrange("p a b c -> p (a b c)"), bank[7][:, 0:GT * NROW], ACT.Copy)\
                        .then_inc(S["stats_copied"], 1)
                if 0 <= i - 3 < G:
                    g = i - 3
                    act.wait_ge(S["x2_turned"], g + 1)
                    wait(act, "router_logits", g)
                    A(x2T[:, :], bank[3][:, :], ACT.Copy).then_inc(S["x2T_made"], 1)
                if i + 2 < G:
                    xT_copy(i + 2)

            def gelu(t, k):
                act.wait_ge(S["hidden_b"], t + 1)
                if not (isinstance(t, int) and t < 2):
                    act.wait_ge(S["hidden_turned"], t - 1)
                A(hg[:, k, :], hb[:, k, :], ACT.Gelu).then_inc(S["hidden_g"], 1)

            def hT_copy(t, k):
                act.wait_ge(S["hidden_turned"], t + 1)
                if not (isinstance(t, int) and t < 2):
                    act.wait_ge(S["y_sum"], t - 1)
                A(hT[:, k, :], bank[4 + k][:, :], ACT.Copy).then_inc(S["hT_made"], 1)

            pipeline(act, ((0, gelu), (-2, hT_copy)))

        @block.tensor
        def _(pe):
            mm = pe.matmul

            pe.wait_ge(S["sel_made"], 1)
            pe.wait_ge(S["setup_in"], 80)
            for s in range(2):
                pe.transpose(bank[0][0:3 * BANDS, s * P:(s + 1) * P], selz[:, s, :], ident[:, :])
            mm(bank[1][0:3 * BANDS, 0:P], selz[:, 2, :], W[:, W_MIMO, :], start=True, stop=True)
            for r in range(2):
                mm(bank[2][:, r * 5:r * 5 + 5], W[:, W_PHIN + r, :], sel5[:, :], start=True, stop=True)
            for r in range(2):
                last = mm(bank[3][:, r * 4:r * 4 + 4], bphib[:, r, :], sel5[:, 0:BANDS], start=True, stop=True)
            last.then_inc(S["sel_turned"], 1)

            def turn(dst, src, done):
                for j in range(GT):
                    last = pe.transpose(dst[:, j * P:(j + 1) * P], src[:, j, :], ident[:, :])
                last.then_inc(S[done], 1)

            def z_turn(g):
                pe.wait_ge(S["xn_made"], g + 1)
                wait(pe, "xT_made", g)
                wait(pe, "bth_read", g - 2)
                turn(bank[6], xn, "xn_turned")

            def psi_project(g):
                pe.wait_ge(S["xT_made"], g + 1)
                wait(pe, "psi_read", g)
                for r in range(2):
                    last = mm(bank[r][:, :], W[:, W_PSI + r, :], xT[:, g % 4, :], start=True, stop=True)
                last.then_inc(S["psi_proj"], 1)

            z_turn(0)
            z_turn(1)
            pe.wait_ge(S["setup_made"], 1)
            psi_project(0)
            for i in range(G + 5):
                if 0 <= i - 3 < G:
                    pe.wait_ge(S["t12_made"], i - 2)
                    wait(pe, "stats_copied", i - 1)
                    wait(pe, "pos_made", i - 4)
                    for j in range(GT):
                        last = pe.transpose(bank[7][0:3 * BANDS, j * P:(j + 1) * P], t12[:, j, :], ident[:, :])
                    last.then_inc(S["t12_turned"], 1)
                if 0 <= i - 1 < G:
                    g = i - 1
                    pe.wait_ge(S["hprev_made"], g + 1)
                    wait(pe, "xT_made", i + 2)
                    mm(bank[6][:, :], W[:, W_BTX, :], xT[:, g % 4, :], start=True, stop=False)
                    for r in range(2):
                        last = mm(bank[6][:, :], W[:, W_BTH + r, :], hprev[:, r * GB:(r + 1) * GB, 0:SEQ],
                                  start=False, stop=(r == 1))
                    last.then_inc(S["bth_proj"], 1)
                if 0 <= i - 3 < G:
                    pe.wait_ge(S["t12_copied"], i - 2)
                    wait(pe, "prod_made", i - 1)
                    for r in range(2):
                        last = mm(bank[4 + r][:, :], selT[:, r, :], t12T[:, :], start=True, stop=True)
                    last.then_inc(S["spread"], 1)
                if 0 <= i - 4 < G:
                    g = i - 4
                    pe.wait_ge(S["x2T_made"], g + 1)
                    wait(pe, "t12_copied", i - 2)
                    wait(pe, "stats_copied", i - 1)
                    wait(pe, "pos_made", g)
                    for j in range(GT):
                        last = mm(bank[7][:, j * E:(j + 1) * E], x2T[:, j * P:(j + 1) * P], gws[:, :],
                                  start=True, stop=True)
                    last.then_inc(S["router_logits"], 1)
                if 0 <= i < G:
                    x = xT[:, i % 4, :]
                    wait(pe, "h2_stats", i - 3)
                    mm(bank[2][:, :], W[:, W_GATE, :], x, start=True, stop=True).then_inc(S["gate_proj"], 1)
                    wait(pe, "x2T_made", i - 3)
                    mm(bank[3][:, :], W[:, W_BS, :], x, start=True, stop=True).then_inc(S["bs_proj"], 1)
                if 0 <= i - 4 < G:
                    pe.wait_ge(S["onehot_made"], i - 3)
                    for j in range(GT + 1):
                        o = bank[7][:, j * E:(j + 1) * E]
                        for s in range(j):
                            last = mm(o, ones16[:, :], oh[:, s, :], start=(s == 0), stop=(s == j - 1 and j == GT))
                        if j < GT:
                            last = mm(o, upper16[:, :], oh[:, j, :], start=(j == 0), stop=True)
                    last.then_inc(S["ranks_made"], 1)
                if 0 <= i - 3 < G:
                    g = i - 3
                    pe.wait_ge(S["uu_made"], g + 1)
                    wait(pe, "gate_exp", i + 1)
                    wait(pe, "h2_stats", g)
                    for r in range(2):
                        mm(bank[2][:, :], W[:, W_MIMO, :], uu[:, r, :], start=(r == 0), stop=False)
                    mm(bank[2][:, :], mimoC[:, :], t12T[:, :], start=False, stop=True).then_inc(S["mixed"], 1)
                if 0 <= i - 1 < G:
                    g = i - 1
                    wait(pe, "prod_made", g)
                    wait(pe, "uu_made", i - 2)
                    for r in range(2):
                        last = mm(bank[4 + r][:, :], W[:, W_PHI + r, :], xT[:, g % 4, :], start=True, stop=True)
                    last.then_inc(S["phi_proj"], 1)
                if 0 <= i - 3 < G:
                    pe.wait_ge(S["mixed_copied"], i - 2)
                    for j in range(GT):
                        c = slice(j * P, (j + 1) * P)
                        last = pe.transpose(bank[2][:, c], ga[:, c], ident[:, :])
                    last.then_inc(S["mixed_turned"], 1)
                if i + 1 < G:
                    psi_project(i + 1)
                if 0 <= i - 1 < G:
                    g = i - 1
                    pe.wait_ge(S["H_made"], g + 1)
                    wait(pe, "stats_copied", g)
                    wait(pe, "t12_copied", i - 2)
                    wait(pe, "pos_made", i - 3)
                    mm(bank[7][0:NROW, :], wq[:, :], xT[:, g % 4, :], start=True, stop=False)
                    for k in range(2):
                        o = NROW - NSUM_W * (k + 1)
                        mm(bank[7][0:NROW, :], selw[:, o:o + NROW], H[:, g % 3, k, :], start=False, stop=False)
                    pe.wait_ge(S["hsq_made"], g + 1)
                    pe.wait_ge(S["prod_made"], g + 1)
                    srcs = [hsq[:, 0, :], hsq[:, 1, :], xp[:, 0, :], xp[:, 1, :], xp[:, 2, :], xp[:, 3, :]]
                    for k, x in enumerate(srcs):
                        o = NROW - NSUM_W * (k + 3)
                        last = mm(bank[7][0:NROW, :], selw[:, o:o + NROW], x, start=False, stop=(k == len(srcs) - 1))
                    last.then_inc(S["stats_sum"], 1)
                    pe.wait_ge(S["sums_copied"], g + 1)
                    for j in range(GT):
                        last = pe.transpose(bank[7][:, j * NROW:(j + 1) * NROW], turned[:, j * P:(j + 1) * P],
                                            ident[0:NROW, 0:NROW])
                    last.then_inc(S["stats_turned"], 1)
                if 0 <= i - 3 < G:
                    pe.wait_ge(S["x2_made"], i - 2)
                    wait(pe, "bs_read", i + 1)
                    wait(pe, "x2T_made", i - 3)
                    turn(bank[3], x2, "x2_turned")
                if i + 2 < G:
                    z_turn(i + 2)

            pe.wait_ge(S["weights_in"], 64)
            pe.wait_ge(S["plan_made"], 1)

            def x_turn(t, k):
                pe.wait_ge(S["y2_made"], t + 1)
                if not (isinstance(t, int) and t < 2):
                    pe.wait_ge(S["y2T_made"], t - 1)
                pe.transpose(bank[k][:, 0:P], y2[:, k, :], ident[:, :]).then_inc(S["y2_turned"], 1)

            def up(t, k):
                pe.wait_ge(S["y2T_made"], t + 1)
                if not (isinstance(t, int) and t < 2):
                    pe.wait_ge(S["hidden_b"], t - 1)
                e = expert(pe, t)
                mm(bank[2 + k][:, :], y2T[:, k, :], at(w1s, e), start=True, stop=True).then_inc(S["hidden"], 1)

            def h_turn(t, k):
                pe.wait_ge(S["hidden_g"], t + 1)
                if not (isinstance(t, int) and t < 2):
                    pe.wait_ge(S["hT_made"], t - 1)
                for c in range(FC):
                    last = pe.transpose(bank[4 + k][:, c * P:(c + 1) * P], hg[:, k, c * P:(c + 1) * P], ident[:, :])
                last.then_inc(S["hidden_turned"], 1)

            def down(t, k):
                pe.wait_ge(S["hT_made"], t + 1)
                if not (isinstance(t, int) and t < 2):
                    pe.wait_ge(S["y_made"], t - 1)
                e = expert(pe, t)
                for c in range(FC):
                    w = w2s[:, bass.ds(e, 1), c * D:(c + 1) * D].rearrange("p a b -> p (a b)")
                    last = mm(bank[6 + k][:, 0:D], hT[:, k, c * P:(c + 1) * P], w, start=(c == 0), stop=(c == FC - 1))
                last.then_inc(S["y_sum"], 1)

            pipeline(pe, ((1, x_turn), (0, up), (-2, h_turn), (-3, down)))

        @block.vector
        def _(dve):
            step = Steps(dve, "dve_steps")
            tt, ts, stt, cp = dve.tensor_tensor, dve.tensor_scalar, dve.scalar_tensor_tensor, dve.tensor_copy
            col = lambda c: vec[:, c:c + 1]
            kc = lambda c: kv[:, c:c + 1]

            dve.wait_ge(S["setup_in"], 80)
            dve.wait_ge(S["consts_made"], 1)
            step(ts(kc(K_ADT), col(C_DT), -1.0, None, ALU.mult))
            step.go(tt(kc(K_ADT), kc(K_ADT), col(C_DT), ALU.max))
            step.go(ts(kc(K_NBG), col(C_BGATE), -1.0, None, ALU.mult))
            step.go(tt(kc(K_BT), col(C_BBTX), col(C_BBTH), ALU.add))
            step.go(ts(kc(K_BETA), col(C_BETA), 1.0 / BW, None, ALU.mult))
            step.go(ts(kc(K_TINV), col(C_TAU), 1e-4, None, ALU.max))
            step.wait()
            step(dve.reciprocal(kc(K_TINV), kc(K_TINV)))
            step.go(ts(kc(K_TINV), kc(K_TINV), 1.0 / BW, None, ALU.mult))
            dve.wait_ge(S["lgam_exp"], 1)
            step(tt(kc(K_RL), kc(K_T), kc(K_ADT), ALU.mult))
            ts(kc(K_RL), kc(K_RL), -1.0, None, ALU.mult).then_inc(S["decay_log"], 1)
            step(ts(ang[:, 1, :], iota_t[:, :], kc(K_ADT), col(C_OMEGA), ALU.mult, ALU.mult))
            step.go(cp(ang[:, 0, :], ang[:, 1, :]))
            step.go(ts(rnd[:, 0, :], ang[:, 1, :], 1.0 / TWO_PI, 0.25, ALU.mult, ALU.add))
            step.go(ts(rnd[:, 1, :], ang[:, 1, :], 1.0 / TWO_PI, None, ALU.mult))
            step.wait()
            step(ts(rnd[:, :, :], rnd[:, :, :], ROUND, None, ALU.add))
            step(ts(rnd[:, :, :], rnd[:, :, :], -ROUND, None, ALU.add))
            for part in (PI_A, PI_B, PI_C):
                step(stt(ang[:, :, :], rnd[:, :, :], -part, ang[:, :, :], ALU.mult, ALU.add))
            step(ts(ang[:, 0, :], ang[:, 0, :], np.pi / 2, None, ALU.add))
            ts(ang[:, :, :], ang[:, :, :], 3.1415925, -3.1415925, ALU.min, ALU.max).then_inc(S["angles_made"], 1)
            step(cp(bandf[:, :], bandi[:, :]))
            step(ts(bandf[:, :], bandf[:, :], iota_p[:, 0:1], None, ALU.is_equal))
            step(dve.tensor_reduce(sel5[:, 0:BANDS], bandf[:, :].rearrange("p (k w) -> p k w", k=BANDS), AX.X, ALU.add))
            for r in range(2):
                step.go(ts(bphib[:, r, :], ones[:, :], col(C_BPHI + r), None, ALU.mult))
            for s in range(3):
                step.go(cp(selz[:, s, s * BANDS:(s + 1) * BANDS], sel5[:, 0:BANDS]))
            step.wait()
            cp(kc(K_T), kc(K_BT)).then_inc(S["sel_made"], 1)
            dve.wait_ge(S["sel_turned"], 1)
            step.go(cp(selT[:, :, :], bank[0][0:3 * BANDS, 0:2 * P].rearrange("p (a b) -> p a b", a=2)))
            step.go(cp(mimoC[:, :], bank[1][0:3 * BANDS, 0:P]))
            step.go(cp(wq[:, NPROD * NSUM_W:], bank[2][:, 0:10]))
            step.go(cp(bq[:, :, :], bank[3][:, 0:8].rearrange("p (a b) -> p a b", a=2)))
            dve.wait_ge(S["tables_made"], 3)
            step.wait()
            step(ts(decay[:, :, :], decay[:, :, :], kc(K_R), None, ALU.mult))
            cp(kc(K_T), kc(K_R)).then_inc(S["setup_made"], 1)

            def rsqrt_v(y, v, t):
                step(ts(y.bitcast(I32), v.bitcast(I32), -0.5, 1597463007.0, ALU.mult, ALU.add))
                for _ in range(3):
                    step(tt(t, y, y, ALU.mult))
                    step(stt(t, t, -0.5, v, ALU.mult, ALU.mult))
                    step(stt(y, t, 1.5, y, ALU.add, ALU.mult))

            def z_stats(g):
                p = g % 2
                dve.wait_ge(S[f"gathered{p}"], 16 * GT * (g // 2 + 1))
                f = tiles(feat, g)
                step(tt(f, f, bc(embb[:, :], 1, [P, GT, D]), ALU.add))
                if g >= 2:
                    dve.wait_ge(S["z_factors"], g - 1)
                for j in range(GT):
                    step.go(dve.bn_stats(bnz[:, p, j, :], f[:, j, :]))
                step.wait()
                for j in range(GT):
                    last = dve.bn_aggr(mvz[:, p, j, :], bnz[:, p, j, :])
                    if j < GT - 1:
                        step.go(last)
                last.then_inc(S["z_stats"], 1)

            def z_rows(g):
                p = g % 2
                dve.wait_ge(S["z_factors"], g + 1)
                if g >= 1:
                    dve.wait_ge(S["xn_turned"], g)
                f = tiles(feat, g)
                for j in range(GT):
                    last = ts(xn[:, j, :], f[:, j, :], zout[:, p, 1, j:j + 1], zout[:, p, 2, j:j + 1],
                              ALU.mult, ALU.add)
                    step.go(last)
                step.wait()
                for j in range(GT):
                    last = ts(f[:, j, :], f[:, j, :], zout[:, p, 0, j:j + 1], None, ALU.mult)
                    if j < GT - 1:
                        step.go(last)
                last.then_inc(S["xn_made"], 1)

            cs = lambda k: bc(tab[:, k, :], 1, [P, GB, SEQ])
            def cs2(k):
                return bc(tab[:, k:k + 2, :], 2, [P, 2, GB, SEQ])

            def psi_turn(g):
                p = g % 2
                dve.wait_ge(S["psi_proj"], g + 1)
                step.wait()
                wait(dve, "hprev_made", g)
                for k, (r, c) in enumerate(((0, 0), (1, 1), (1, 0), (0, 1))):
                    last = stt(b4(rot[:, k, :]), b4(bank[r][:, :]), col(C_BPSI + r), cs(c), ALU.add, ALU.mult)
                    if k < 3:
                        step.go(last)
                last.then_inc(S["psi_read"], 1)
                dve.wait_ge(S["psi_read"], g + 1)
                step.wait()
                step.go(tt(psi[:, p, 0, :], rot[:, 0, :], rot[:, 1, :], ALU.add))
                step(tt(psi[:, p, 1, :], rot[:, 2, :], rot[:, 3, :], ALU.subtract))

            def scan(g, k, made, w_made, dst, t0, turned=None):
                p = g % 2
                dve.wait_ge(S[made], g + 1)
                step(tt(wg[:, :], sp_m[:, k, :], sp_l[:, k, :], ALU.add))
                if k == 0:
                    dve.wait_ge(S["gate_made"], g + 1)
                tt(wg[:, :], wg[:, :], gate[:, p, :], ALU.mult).then_inc(S[w_made], 1)
                dve.wait_ge(S[w_made], g + 1)
                step(tt(u[:, :, :], psi[:, p, :, :], bc(wg[:, :], 1, [P, 2, GN]), ALU.mult))
                step(dve.tensor_tensor_scan(g_s[:, :, :].rearrange("p a b -> p (a b)"),
                                            decay[:, :, :].rearrange("p a b -> p (a b)"),
                                            u[:, :, :].rearrange("p a b -> p (a b)"), 0.0, ALU.mult, ALU.add))
                gs = g_s[:, :, :].rearrange("p r (b t) -> p r b t", b=GB)
                for q in range(2):
                    step.go(tt(rot[:, 2 * q:2 * q + 2, :].rearrange("p r (b t) -> p r b t", b=GB), gs, cs2(q), ALU.mult))
                step.wait()
                if k == 0 and g >= 1:
                    dve.wait_ge(S["bth_proj"], g)
                for r in range(2):
                    last = tt(dst[:, r * GB:(r + 1) * GB, t0:t0 + SEQ], b4(rot[:, 2 * r, :]), b4(rot[:, 2 * r + 1, :]),
                              (ALU.subtract, ALU.add)[r])
                    if r == 0 or k == 1:
                        step.go(last)
                return last

            def scout(g):
                scan(g, 0, "sp1_made", "w1_made", hprev, 1).then_inc(S["hprev_made"], 1)

            def main_scan(g):
                scan(g, 1, "sp2_made", "w2_made", hpad, 2)
                step.wait()
                tap = lambda k: hpad[:, :, 2 - k:2 - k + SEQ]
                f4 = fir[:, :, :].rearrange("p r (b t) -> p (r b) t", b=GB)
                h4 = H[:, g % 3, :, :].rearrange("p r (b t) -> p (r b) t", b=GB)
                step(stt(f4, tap(1), 4.0, tap(0), ALU.mult, ALU.add))
                if g >= 3:
                    dve.wait_ge(S["stats_sum"], g - 2)
                tt(h4, f4, tap(2), ALU.add).then_inc(S["H_made"], 1)

            def products(g):
                dve.wait_ge(S["H_made"], g + 1)
                dve.wait_ge(S["phi_proj"], g + 1)
                if g >= 1:
                    dve.wait_ge(S["stats_sum"], g)
                for k, (hr, pr) in enumerate(((0, 0), (1, 1), (0, 1), (1, 0))):
                    last = stt(xp[:, k, :], bank[4 + pr][:, :], col(C_BPHI + pr), H[:, g % 3, hr, :], ALU.add, ALU.mult)
                    if k < 3:
                        step.go(last)
                last.then_inc(S["prod_made"], 1)

            def weigh(g):
                dve.wait_ge(S["spread"], g + 1)
                if g >= 1:
                    dve.wait_ge(S["mixed"], g)
                step.go(tt(uu[:, 0, :], H[:, g % 3, 0, :], bank[4][:, :], ALU.mult))
                tt(uu[:, 1, :], H[:, g % 3, 1, :], bank[5][:, :], ALU.mult).then_inc(S["uu_made"], 1)

            def residual(g):
                p = g % 2
                dve.wait_ge(S["mixed_turned"], g + 1)
                if g >= 2:
                    dve.wait_ge(S[f"scattered{p}"], 16 * GT * (g // 2))
                h2 = row[:, p, :, 0:D]
                step(tt(h2, tiles(feat, g), bank[2][:, :].rearrange("p (a b) -> p a b", a=GT), ALU.add))
                for j in range(GT):
                    step.go(dve.bn_stats(bnd[:, j, :], h2[:, j, :]))
                step.wait()
                for j in range(GT):
                    last = dve.bn_aggr(mvd[:, j, :], bnd[:, j, :])
                    if j < GT - 1:
                        step.go(last)
                    else:
                        last.then_inc(S["h2_stats"], 1)
                dve.wait_ge(S["h2_stats"], g + 1)
                v, y, t = (ds_[:, k, :] for k in range(3))
                step(ts(v, mvd[:, :, 1], LN_EPS, None, ALU.add))
                rsqrt_v(y, v, t)
                step.go(cp(row[:, p, :, D:D + 1], y.unsqueeze(2)))
                step.go(cp(row[:, p, :, D + 3:D + 4], tiles(tokid, g).unsqueeze(2)))
                step(stt(row[:, p, :, D + 1:D + 2], mvd[:, :, 0:1], -1.0, y.unsqueeze(2), ALU.mult, ALU.mult))

            def x2_rows(g):
                p = g % 2
                if g >= 1:
                    dve.wait_ge(S["x2_turned"], g)
                for j in range(GT):
                    last = ts(x2[:, j, :], row[:, p, j, 0:D], row[:, p, j, D:D + 1], row[:, p, j, D + 1:D + 2],
                              ALU.mult, ALU.add)
                    if j < GT - 1:
                        step.go(last)
                last.then_inc(S["x2_made"], 1)

            def route(g):
                dve.wait_ge(S["router_logits"], g + 1)
                e3 = [P, GT, E]
                first, pick, best = lt[:, 1, :, :], lt[:, 2, :, :], lt[:, 3, :, :]
                tt(lg[:, :, :], bank[7][:, 0:GT * E].rearrange("p (a b) -> p a b", a=GT),
                   bc(gbs[:, :], 1, e3), ALU.add).then_inc(S["logits_read"], 1)
                dve.wait_ge(S["logits_read"], g + 1)
                step(dve.tensor_reduce(lm[:, 0, :], lg[:, :, :], AX.X, ALU.max))
                tt(lt[:, 0, :, :], lg[:, :, :], bc(lm[:, 0, :], 2, e3), ALU.subtract).then_inc(S["shifted8"], 1)
                step(tt(pick, lg[:, :, :], bc(lm[:, 0, :], 2, e3), ALU.is_ge))
                step(tt(first, pick, bc(eights[:, :], 1, e3), ALU.mult))
                step(dve.tensor_reduce(lm[:, 1, :], first, AX.X, ALU.max))
                tt(oh[:, :, :], first, bc(lm[:, 1, :], 2, e3), ALU.is_equal).then_inc(S["onehot_made"], 1)

            def place(g):
                p = g % 2
                e3 = [P, GT, E]
                dve.wait_ge(S["exps8"], g + 1)
                step(dve.tensor_reduce(lm[:, 2, :], ex[:, :, :], AX.X, ALU.add))
                step(dve.reciprocal(row[:, p, :, D + 2:D + 3], lm[:, 2, :].unsqueeze(2)))
                a, b = pos[:, 0, :, :], pos[:, 1, :, :]
                step(tt(base[:, 1, :], base[:, 0, :], expb[:, :], ALU.add))
                dve.wait_ge(S["ranks_made"], g + 1)
                dve.wait_ge(S["onehot_made"], g + 1)
                step.go(tt(a, bank[7][:, 0:GT * E].rearrange("p (a b) -> p a b", a=GT), bc(base[:, 1, :], 1, e3), ALU.add))
                step.wait()
                step.go(tt(base[:, 0, :], base[:, 0, :], bank[7][:, GT * E:(GT + 1) * E], ALU.add))
                step(tt(b, a, oh[:, :, :], ALU.mult))
                step(dve.tensor_reduce(lm[:, 3, :], b, AX.X, ALU.add))
                cp(posi[:, p, :], lm[:, 3, :]).then_inc(S["pos_made"], 1)

            z_stats(0)
            z_stats(1)
            z_rows(0)
            z_stats(2)
            z_rows(1)
            for i in range(G + 5):
                if 0 <= i < G:
                    psi_turn(i)
                if 0 <= i - 3 < G:
                    weigh(i - 3)
                if 0 <= i - 4 < G:
                    route(i - 4)
                if 0 <= i - 1 < G:
                    main_scan(i - 1)
                if 0 <= i - 4 < G:
                    place(i - 4)
                if 0 <= i - 1 < G:
                    products(i - 1)
                if i + 3 < G:
                    z_stats(i + 3)
                if 0 <= i - 3 < G:
                    residual(i - 3)
                    x2_rows(i - 3)
                if i + 2 < G:
                    z_rows(i + 2)
                if 0 <= i < G:
                    scout(i)

            n_e = base[:, 0, :]
            begun, ends, starts = (mp[:, k, :] for k in range(3))
            full = [P, E, TILES]
            step.go(cp(mcmp[:, :, :], bc(n_e, 2, full)))
            step.go(ts(mp[:, 4, :], expb[:, :], 0.0, 1.0, ALU.mult, ALU.add))
            step.wait()
            step(ts(mt[:, 6, 0:TILES], iota_s[:, 0:TILES], float(P), None, ALU.mult))
            step(tt(mcmp[:, :, :], mcmp[:, :, :], bc(mt[:, 6, 0:TILES], 1, full), ALU.is_gt))
            step(dve.tensor_reduce(begun, mcmp[:, :, :], AX.X, ALU.add))
            step(dve.tensor_tensor_scan(ends, mp[:, 4, :], begun, 0.0, ALU.mult, ALU.add))
            step(tt(starts, ends, begun, ALU.subtract))
            fs = [P, SLOTS, E]
            step(tt(mcmp2[:, :, :], bc(iota_s[:, :], 2, fs), bc(starts, 1, fs), ALU.is_ge))
            step(dve.tensor_reduce(mt[:, 0, :], mcmp2[:, :, :], AX.X, ALU.add))
            step(ts(mt[:, 0, :], mt[:, 0, :], -1.0, None, ALU.add))
            step(tt(mcmp2[:, :, :], mcmp2[:, :, :], bc(starts, 1, fs), ALU.mult))
            step(dve.tensor_reduce(mt[:, 1, :], mcmp2[:, :, :], AX.X, ALU.max))
            step(tt(mt[:, 2, :], iota_s[:, :], mt[:, 1, :], ALU.subtract))
            step(ts(mt[:, 2, :], mt[:, 2, :], float(P), None, ALU.mult))
            step(stt(mt[:, 3, :], mt[:, 0, :], float(REGION), mt[:, 2, :], ALU.mult, ALU.add))
            step(ts(mt[:, 4, :], iota_s[:, :], ends[:, E - 1:E], None, ALU.is_ge))
            step(ts(mt[:, 5, :], mt[:, 3, :], -1.0, float(DUMMY), ALU.mult, ALU.add))
            step(tt(mt[:, 5, :], mt[:, 5, :], mt[:, 4, :], ALU.mult))
            step(tt(mt[:, 3, :], mt[:, 3, :], mt[:, 5, :], ALU.add))
            step(tt(mp[:, 5, :], n_e, expb[:, :], ALU.add))
            step.go(cp(plan[:, 0:SLOTS], mt[:, 0, :]))
            step.go(cp(plan[:, SLOTS:2 * SLOTS], mt[:, 3, :]))
            step.wait()
            cp(plan[:, 2 * SLOTS:], mp[:, 5, :]).then_inc(S["plan_made"], 1)
            dve.wait_ge(S["plan_made"], 1)
            dve.wait_ge(S["weights_in"], 64)

            def f_in(t, k):
                dve.wait_ge(S["rows_ready"], t + 1)
                if not (isinstance(t, int) and t < 2):
                    dve.wait_ge(S["y2_turned"], t - 1)
                ts(y2[:, k, :], at(xr, t)[:, 0:D], at(xr, t)[:, D:D + 1], at(xr, t)[:, D + 1:D + 2], ALU.mult, ALU.add)\
                    .then_inc(S["y2_made"], 1)

            def f_turned(t, k):
                dve.wait_ge(S["y2_turned"], t + 1)
                if not (isinstance(t, int) and t < 2):
                    dve.wait_ge(S["hidden"], t - 1)
                cp(y2T[:, k, :], bank[k][:, 0:P]).then_inc(S["y2T_made"], 1)

            def f_bias(t, k):
                dve.wait_ge(S["hidden"], t + 1)
                if not (isinstance(t, int) and t < 2):
                    dve.wait_ge(S["hidden_g"], t - 1)
                e = expert(dve, t)
                tt(hb[:, k, :], bank[2 + k][:, :], at(b1s, e), ALU.add).then_inc(S["hidden_b"], 1)

            def f_out(t, k):
                dve.wait_ge(S["y_sum"], t + 1)
                if not (isinstance(t, int) and t < 2):
                    dve.wait_ge(S[f"put{k}"], 8 * (t - k))
                e = expert(dve, t)
                tt(yb[:, k, :], bank[6 + k][:, 0:D], at(b2s, e), ALU.add).then_inc(S["y_steps"], 1)
                cp(yid[:, k, :], at(xr, t)[:, D + 3:D + 4]).then_inc(S["y_steps"], 1)
                dve.wait_ge(S["y_steps"], 2 * t + 2)
                stt(yo[:, k, :], yb[:, k, :], at(xr, t)[:, D + 2:D + 3], at(xr, t)[:, 0:D], ALU.mult, ALU.add)\
                    .then_inc(S["y_made"], 1)

            pipeline(dve, ((2, f_in), (1, f_turned), (0, f_bias), (-3, f_out)))


def kernel(x, L0_tok_W, L0_tok_b, L0_attn_omega, L0_attn_log_gamma, L0_attn_dt, L0_attn_W_psi, L0_attn_b_psi,
           L0_attn_W_phi, L0_attn_b_phi, L0_attn_W_bs, L0_attn_b_bs, L0_attn_W_btx, L0_attn_b_btx, L0_attn_W_bth,
           L0_attn_b_bth, L0_attn_w_gate, L0_attn_b_gate, L0_attn_tau, L0_attn_beta, L0_attn_mimo_w,
           L0_attn_band_idx, L0_ffn_Ws, L0_ffn_bs, L0_ffn_W1, L0_ffn_b1, L0_ffn_W2, L0_ffn_b2):
    import concourse.bacc as bacc
    from concourse.bass_utils import run_bass_kernel_spmd

    lay = np.ascontiguousarray
    n = np.asarray
    every = lambda v: lay(np.broadcast_to(n(v).reshape(1, -1), (P, n(v).size)))
    mimo = n(L0_attn_mimo_w)
    groups, width = mimo.shape[0], mimo.shape[1]
    mimo_t = np.zeros((D, D), mimo.dtype)
    for g in range(groups):
        s = slice(g * width, (g + 1) * width)
        mimo_t[s, s] = mimo[g].T
    w_psi, w_phi, w_bth = n(L0_attn_W_psi), n(L0_attn_W_phi), n(L0_attn_W_bth)
    blocks = [w_psi[:D].T, w_psi[D:].T, w_phi[:D].T, w_phi[D:].T, n(L0_attn_W_bs).T, n(L0_attn_W_btx).T,
              w_bth[:, :D].T, w_bth[:, D:].T, np.broadcast_to(n(L0_attn_w_gate).reshape(D, 1), (D, D)),
              mimo_t, w_phi[:D], w_phi[D:]]
    one = lambda v: np.broadcast_to(n(v).reshape(1), (D,))
    b_psi, b_phi = n(L0_attn_b_psi), n(L0_attn_b_phi)
    cols = [b_psi[:D], b_psi[D:], b_phi[:D], b_phi[D:], n(L0_attn_b_bs), n(L0_attn_b_btx), n(L0_attn_b_bth),
            n(L0_attn_omega), n(L0_attn_log_gamma), one(L0_attn_dt), one(L0_attn_b_gate), one(L0_attn_tau),
            one(L0_attn_beta)]
    arrays = {
        "ids": lay(n(x).reshape(TILES, P).T),
        "emb": lay(n(L0_tok_W).T),
        "emb_b": every(L0_tok_b),
        "wcat": lay(np.stack(blocks, axis=1)),
        "vecs": lay(np.stack(cols, axis=1)),
        "band": every(L0_attn_band_idx),
        "gate_ws": lay(n(L0_ffn_Ws)),
        "gate_bs": every(L0_ffn_bs),
        "w1": lay(n(L0_ffn_W1).transpose(1, 0, 2)),
        "b1": every(L0_ffn_b1).reshape(P, E, F),
        "w2": lay(n(L0_ffn_W2).reshape(E, FC, P, D).transpose(2, 0, 1, 3)).reshape(P, E, FC * D),
        "b2": every(L0_ffn_b2).reshape(P, E, D),
    }
    nc = bacc.Bacc("TRN2", target_bir_lowering=False, num_devices=1)
    args = [nc.dram_tensor(f"in_{k}", a.shape, mybir.dt.from_np(a.dtype), kind="ExternalInput").ap()
            for k, a in arrays.items()]
    out = nc.dram_tensor("out", (BATCH, SEQ, D), F32, kind="ExternalOutput").ap()
    lm_tower(nc, *args, out)
    r = run_bass_kernel_spmd(nc, [{f"in_{k}": a for k, a in arrays.items()}], core_ids=[0])
    return r.results[0]["out"]
```

```python
from contextlib import ExitStack

import numpy as np

import concourse.bass as bass
from concourse import mybir

ALU = mybir.AluOpType
ACT = mybir.ActivationFunctionType
AX = mybir.AxisListType
F32 = mybir.dt.float32
I32 = mybir.dt.int32
BF16 = mybir.dt.bfloat16

P = 128
BATCH, SEQ, D = 16, 256, 128
T = BATCH * SEQ
TILES = T // P
GT = 4
GN = GT * P
GB = GN // SEQ
G = T // GN
BANDS = 4
BW = D // BANDS
E = 8
F = 512
FC = F // P
REGION = T + P
DUMMY = E * REGION
SLOTS = TILES + E
RC = D + 4
DEPTH = 4
LN_EPS = 1e-5
NORM_EPS2 = 1e-24
TWO_PI = 2.0 * np.pi
PI_A = 6.28125
PI_B = float(np.float32(TWO_PI - PI_A))
PI_C = float(TWO_PI - PI_A - PI_B)
ROUND = 12582912.0

NSUM_W = BANDS + 1
NPROD = 8
NROW = (NPROD + 2) * NSUM_W

W_PSI, W_PHI, W_BS, W_BTX, W_BTH, W_GATE, W_MIMO, W_PHIN = 0, 2, 4, 5, 6, 8, 9, 10
NW = 12
(C_BPSI, C_BPHI, C_BBS, C_BBTX, C_BBTH, C_OMEGA, C_LGAM, C_DT, C_BGATE, C_TAU, C_BETA) = (0, 2, 4, 5, 6, 7, 8, 9, 10, 11, 12)
NC = 13
K_ADT, K_NR, K_R, K_NBG, K_BT, K_TINV, K_BETA, K_RL, K_T = range(9)


def lm_tower(nc, ids, emb, emb_b, wcat, vecs, band, gate_ws, gate_bs, w1, b1, w2, b2, out):
    sorted_rows = nc.dram_tensor("sorted_rows", [DUMMY + P, RC], F32, kind="Internal").ap()
    out_rows = out.rearrange("b l d -> (b l) d")

    with ExitStack() as ctx:
        def sb(name, shape, dt=F32):
            return ctx.enter_context(nc.sbuf_tensor(name, shape, dt))

        def sem(name):
            return ctx.enter_context(nc.semaphore(name))

        bank = [ctx.enter_context(nc.psum_tensor(f"bank{i}", [P, 512], F32)) for i in range(8)]

        idx = sb("idx", [P, TILES], I32)
        embb = sb("embb", [P, D])
        W = sb("W", [P, NW, P])
        bth_neg = sb("bth_neg", [P, P])
        eps1 = sb("eps1", [P, 1])
        vec = sb("vec", [P, NC])
        gws = sb("gws", [P, E])
        gbs = sb("gbs", [P, E])
        w1s = sb("w1s", [P, E, F])
        w2s = sb("w2s", [P, E, FC * D])
        b1s = sb("b1s", [P, E, F])
        b2s = sb("b2s", [P, E, D])
        kv = sb("kv", [P, 9])
        ident = sb("ident", [P, P])
        upper = sb("upper", [P, P])
        ones = sb("ones", [P, P])
        upper16 = sb("upper16", [P, P], BF16)
        ones16 = sb("ones16", [P, P], BF16)
        iota_p = sb("iota_p", [P, 1])
        iota_t = sb("iota_t", [P, SEQ])
        tab = sb("tab", [P, 3, SEQ])
        decay = sb("decay", [P, 2 * GB, SEQ])
        selz = sb("selz", [P, 3, 3 * BANDS])
        selw = sb("selw", [P, 2 * NROW - NSUM_W])
        sel5 = selw[:, NROW - NSUM_W:NROW]
        selT = sb("selT", [3 * BANDS, 2, P])
        mimoC = sb("mimoC", [3 * BANDS, P])
        wq = sb("wq", [P, NROW])
        bq = sb("bq", [P, 2, BANDS])
        tokid = sb("tokid", [P, TILES])
        expb = sb("expb", [P, E])
        eights = sb("eights", [P, E])
        padrow = sb("padrow", [P, RC])

        rows_buf = sb("rows_buf", [P, SLOTS * RC])
        feat = rows_buf[:, 0:TILES * D].rearrange("p (a b) -> p a b", b=D)
        xr = rows_buf[:, :].rearrange("p (a b) -> p a b", b=RC)
        bnz = sb("bnz", [P, 2, GT, 6])
        mvz = sb("mvz", [P, 2, GT, 2])
        zs = sb("zs", [P, 4, 2, GT])
        zout = sb("zout", [P, 2, 3, GT])
        xn = sb("xn", [P, GT, D])
        xT = sb("xT", [P, 4, GN])

        rot = sb("rot", [P, 4, GN])
        ang = rot[:, 0, :].rearrange("p (a t) -> p a t", a=2)
        psi = sb("psi", [P, 2, 2, GN])
        gate = sb("gate", [P, 2, GN])
        sp_m = sb("sp_m", [P, 2, GN])
        sp_l = sb("sp_l", [P, 2, GN])
        ga = sb("ga", [P, GN])
        wg = sb("wg", [P, GN])
        u = sb("u", [P, 2, GN])
        g_s = sb("g_s", [P, 2, GN])
        spun = sb("spun", [P, 4, GN])
        hpad = sb("hpad", [P, 2 * GB, SEQ + 2])
        fir = sb("fir", [P, 2, GN])
        rnd = fir[:, :, 0:SEQ]
        H = sb("H", [P, 3, 2, GN])
        hsq = sb("hsq", [P, 2, GN])
        bandi, bandf = hsq[:, 0, 0:P].bitcast(I32), hsq[:, 0, P:2 * P]
        bphib = hsq[:, 1, 0:2 * P].rearrange("p (a b) -> p a b", a=2)
        xp = sb("xp", [P, 4, GN])

        st = sb("st", [P, GT, NPROD + 2, NSUM_W])
        turned = sb("turned", [NROW, GN])
        bt_ = sb("bnd_t", [P, 20, GT, 2, BANDS])
        t12 = sb("t12", [P, GT, 3 * BANDS])
        t12T = turned[0:3 * BANDS, :]
        e4 = sb("e4", [P, 2, GT, BANDS])
        lns = sb("lns", [P, 2, GT])
        uu = sb("uu", [P, 2, GN])

        row = sb("row", [P, 3, GT, RC])
        bnd = sb("bnd", [P, GT, 6])
        mvd = sb("mvd", [P, GT, 2])
        ds_ = sb("ds_", [P, 4, GT])
        x2 = sb("x2", [P, GT, D])
        x2T = sb("x2T", [P, GN])
        lg = sb("lg", [P, GT, E])
        lt = sb("lt", [P, 4, GT, E])
        ex = sb("ex", [P, GT, E])
        oh = sb("oh", [P, GT, E], BF16)
        lm = sb("lm", [P, 4, GT])
        pos = sb("pos", [P, 2, GT, E])
        posi = sb("posi", [P, 3, GT], I32)
        base = sb("base", [P, 2, E])

        mp = sb("mp", [P, 8, E])
        mcmp = fir[:, 0, 0:E * TILES].rearrange("p (a b) -> p a b", b=TILES)
        mcmp2 = fir[:, 1, 0:SLOTS * E].rearrange("p (a b) -> p a b", b=E)
        mt = sb("mt", [P, 7, SLOTS])
        iota_s = sb("iota_s", [P, SLOTS])
        plan = sb("plan", [P, 2 * SLOTS + E], I32)
        hb, hg, hT = rot[:, 0:2, :], rot[:, 2:4, :], u[:, :, :]
        y2, y2T, yb, yo = (g_s[:, r, c:c + 2 * P].rearrange("p (a b) -> p a b", b=P)
                           for r in range(2) for c in (0, 2 * P))
        yid = sb("yid", [P, 2, 1], I32)

        names = (
            "idx_in embb_in vecs_in setup_in weights_in gathered0 gathered1 "
            "pads_made iotas_made consts_made angles_made lgam_exp decay_log tables_made sel_made sel_turned setup_made "
            "biased z_stats z_var z_seed z_factors xn_made h_made xn_turned xT_made "
            "psi_proj psi_read gate_proj gate_exp gate_made bs_proj bs_read sp1_made w1_made spun_made "
            "bth_proj bth_read sp2_made w2_made H_made hsq_made phi_proj prod_made "
            "stats_sum sums_copied stats_turned stats_copied h_var h_seed a_var a_seed "
            "logits4 exps4 sum4 lnsum4 log4 soft4 t12_made t12_turned t12_copied spread uu_made mixed mixed_copied mixed_turned "
            "h2_stats h2_seed row_made x2_made x2_turned x2T_made router_logits logits_read shifted8 exps8 onehot_made "
            "ranks_made pos_made scattered0 scattered1 scattered2 "
            "pads_planned plan_made padded rows_in0 rows_in1 rows_in2 rows_in3 "
            "y2_made y2_turned y2T_made hidden hidden_b hidden_g hidden_turned hT_made y_sum y_made "
            "put0 put1 y_steps "
            "pool_steps act_steps dve_steps").split()
        S = {n: sem(n) for n in names}

        class Steps:

            def __init__(self, eng, name):
                self.eng, self.sem, self.n = eng, S[name], 0

            def go(self, ins):
                self.n += 1
                ins.then_inc(self.sem, 1)

            def wait(self):
                self.eng.wait_ge(self.sem, self.n)

            def __call__(self, ins):
                self.go(ins)
                self.wait()

        def wait(eng, name, n):
            if n > 0:
                eng.wait_ge(S[name], min(n, G))

        def bc(ap, axis, shape):
            return ap.unsqueeze(axis).broadcast_to(shape)

        def newton(step, eng, y, v, t):
            step(eng.tensor_tensor(t, y, y, ALU.mult))
            step(eng.tensor_tensor(t, t, v, ALU.mult))
            step(eng.tensor_scalar(t, t, -0.5, 1.5, ALU.mult, ALU.add))
            step(eng.tensor_tensor(y, y, t, ALU.mult))

        def tiles(buf, g):
            return buf[:, g * GT:(g + 1) * GT]

        def at(buf, i):
            if isinstance(i, int):
                return buf[:, i, :]
            return buf[:, bass.ds(i, 1), :].rearrange("p a b -> p (a b)")

        def expert(eng, t):
            return eng.value_load(plan[0:1, t:t + 1], min_val=0, max_val=E - 1)

        def pipeline(stages):
            for t in range(-2, SLOTS + 4):
                for lead, stage in stages:
                    if 0 <= t + lead < SLOTS:
                        stage(t + lead, (t + lead) % 2)

        b4 = lambda ap: ap.rearrange("p (b t) -> p b t", b=GB)

        block = ctx.enter_context(nc.Block())

        @block.sync
        def _(sp):
            sp.dma_start(idx[:, :], ids).then_inc(S["idx_in"], 16)
            sp.dma_start(embb[:, :], emb_b).then_inc(S["embb_in"], 16)
            sp.dma_start(vec[:, :], vecs).then_inc(S["vecs_in"], 16)
            sp.dma_start(bandi[:, :], band).then_inc(S["vecs_in"], 16)
            sp.dma_start(W[:, :, :], wcat).then_inc(S["setup_in"], 16)
            sp.dma_start(gws[:, :], gate_ws).then_inc(S["setup_in"], 16)
            sp.dma_start(gbs[:, :], gate_bs).then_inc(S["setup_in"], 16)
            for g, (to, src) in enumerate(((w1s, w1), (w2s, w2), (b1s, b1), (b2s, b2))):
                sp.wait_ge(S["H_made"], g + 1)
                sp.dma_start(to[:, :, :], src).then_inc(S["weights_in"], 16)
            sp.wait_ge(S["pads_made"], 1)
            sp.dma_start(sorted_rows[DUMMY:DUMMY + P, :], padrow[:, :]).then_inc(S["padded"], 16)
            sp.wait_ge(S["pads_planned"], 1)
            for e in range(E):
                r = sp.value_load(plan[0:1, 2 * SLOTS + e:2 * SLOTS + e + 1], min_val=0, max_val=DUMMY - P)
                sp.dma_start(sorted_rows[bass.ds(r, P), :], padrow[:, :]).then_inc(S["padded"], 16)
            sp.wait_ge(S["plan_made"], 1)
            sp.wait_ge(S["padded"], 16 * (E + 1))
            for k in range(3):
                sp.wait_ge(S[f"scattered{k}"], 16 * GT * len(range(k, G, 3)))

            def load(t, k):
                r = sp.value_load(plan[0:1, bass.ds(SLOTS + t, 1)], min_val=0, max_val=DUMMY)
                sp.dma_start(at(xr, t), sorted_rows[bass.ds(r, P), :]).then_inc(S[f"rows_in{k}"], 16)

            for k in range(DEPTH):
                load(k, k)
            with sp.Fori(DEPTH, SLOTS - DEPTH + 1, DEPTH) as t:
                for k in range(DEPTH):
                    sp.wait_ge(S[f"rows_in{k}"], (16 // DEPTH) * t)
                    load(t + k, k)
            for k in range(2):
                sp.wait_ge(S[f"put{k}"], 16 * SLOTS // 2)

        @block.gpsimd
        def _(pool):
            step = Steps(pool, "pool_steps")
            tt, ts = pool.tensor_tensor, pool.tensor_scalar
            pool.wait_ge(S["idx_in"], 16)

            def gather(g):
                for t in range(g * GT, (g + 1) * GT):
                    pool.indirect_dma_start(
                        out=feat[:, t, :], out_offset=None, in_=emb,
                        in_offset=bass.IndirectOffsetOnAxis(ap=idx[:, t:t + 1], axis=0),
                    ).then_inc(S[f"gathered{g % 2}"], 16)

            gather(0)
            kw = dict(allow_small_or_imprecise_dtypes=True)
            step(pool.memset(eps1[:, :], LN_EPS))
            step(pool.memset(ones[:, :], 1.0))
            step(pool.iota(iota_p[:, :], pattern=[[0, 1]], base=0, channel_multiplier=1, **kw))
            step(pool.memset(ident[:, :], 0.0))
            step(pool.memset(selz[:, :, :], 0.0))
            step(pool.memset(selw[:, :], 0.0))
            step(pool.memset(wq[:, :], 0.0))
            step(pool.memset(sel5[:, BANDS:], 1.0))
            step(pool.affine_select(out=ident[:, :], in_=ident[:, :], compare_op=ALU.not_equal, fill=1.0,
                                    base=0, pattern=[[-1, P]], channel_multiplier=1))
            pool.iota(iota_t[:, :], pattern=[[1, SEQ]], base=0, channel_multiplier=0, **kw)\
                .then_inc(S["iotas_made"], 1)
            gather(1)

            def bias(g):
                pool.wait_ge(S[f"gathered{g % 2}"], 16 * GT * (g // 2 + 1))
                tt(tiles(feat, g), tiles(feat, g), bc(embb[:, :], 1, [P, GT, D]), ALU.add).then_inc(S["biased"], 1)

            mean = lambda g: mvz[:, g % 2, :, 0]
            var = lambda g: mvz[:, g % 2, :, 1]
            za, zv, zy, zt = (zs[:, k, :, :] for k in range(4))

            def z_squares(g):
                pool.wait_ge(S["z_stats"], g + 1)
                step(tt(za[:, 0, :], mean(g), mean(g), ALU.mult))
                step(tt(za[:, 0, :], za[:, 0, :], var(g), ALU.add))
                step(ts(zv[:, 0, :], za[:, 0, :], float(D), NORM_EPS2, ALU.mult, ALU.max))
                step(ts(zv[:, 1, :], zv[:, 0, :], LN_EPS, 0.0, ALU.mult, ALU.add))
                tt(zv[:, 1, :], zv[:, 1, :], var(g), ALU.add).then_inc(S["z_var"], 1)

            def z_factors(g):
                p = g % 2
                pool.wait_ge(S["z_seed"], g + 1)
                newton(step, pool, zy, zv, zt)
                if g >= 2:
                    pool.wait_ge(S["h_made"], g - 1)
                step(tt(za[:, 1, :], mean(g), zy[:, 1, :], ALU.mult))
                step(ts(zout[:, p, 2, :], za[:, 1, :], -1.0, 0.0, ALU.mult, ALU.add))
                pool.tensor_copy(zout[:, p, 0:2, :], zy).then_inc(S["z_factors"], 1)

            full = [P, GT, 2, BANDS]
            B = lambda k: bt_[:, k, :, :, :]
            v2 = lambda k: bt_[:, k, :, :, 0]
            v4 = lambda k: bt_[:, k, :, 0, :]
            m, r, al, dens = v2(0), v2(2), B(8), v4(11)
            mB, rB = bc(m, 3, full), bc(r, 3, full)

            s1, s2, x12, x34, q = (st[:, :, 2 * k:2 * k + 2, 0:BANDS] for k in range(5))
            v, t2 = v2(1), v2(3)
            Q, ta, tb, d, nm = B(5), B(6), B(7), B(9), B(10)
            sq, a2, ab, t4, vm, mx, at_ = B(12), v4(13), v4(14), v4(15), v4(16), v4(17), v4(19)

            def bands_a(g):
                pool.wait_ge(S["stats_copied"], g + 1)
                if g == 0:
                    pool.wait_ge(S["setup_made"], 1)
                step.go(ts(m, st[:, :, 0:2, BANDS], 1.0 / D, 0.0, ALU.mult, ALU.add))
                step(ts(v, st[:, :, 2:4, BANDS], 1.0 / D, 0.0, ALU.mult, ALU.add))
                step.go(tt(t2, m, m, ALU.mult))
                step.go(tt(Q, q, bc(bq[:, :, :], 1, full), ALU.add))
                step.go(ts(nm, mB, float(BW), 0.0, ALU.mult, ALU.add))
                step(ts(d, s1, 2.0, 0.0, ALU.mult, ALU.add))
                step(tt(v, v, t2, ALU.subtract))
                step(ts(v, v, 0.0, None, ALU.max))
                ts(v, v, 36.0 * LN_EPS, None, ALU.add).then_inc(S["h_var"], 1)
                step.go(tt(ta, Q, mB, ALU.mult))
                step.go(tt(tb[:, :, 0, :], Q[:, :, 1, :], mB[:, :, 0, :], ALU.mult))
                step.go(tt(tb[:, :, 1, :], Q[:, :, 0, :], mB[:, :, 1, :], ALU.mult))
                step(tt(d, d, nm, ALU.subtract))
                step.go(tt(ta, x12, ta, ALU.subtract))
                step.go(tt(tb, x34, tb, ALU.subtract))
                step(tt(d, d, mB, ALU.mult))
                step.go(tt(d, s2, d, ALU.subtract))
                pool.wait_ge(S["h_seed"], g + 1)
                newton(step, pool, r, v, t2)
                step.go(tt(ta, ta, rB, ALU.mult))
                step.go(tt(tb, tb, rB, ALU.mult))
                step(tt(d, d, rB, ALU.mult))
                step.go(tt(al[:, :, 0, :], ta[:, :, 0, :], ta[:, :, 1, :], ALU.add))
                step.go(tt(al[:, :, 1, :], tb[:, :, 0, :], tb[:, :, 1, :], ALU.subtract))
                step(tt(d, d, rB, ALU.mult))
                step(tt(sq, al, al, ALU.mult))
                step(tt(a2, sq[:, :, 0, :], sq[:, :, 1, :], ALU.add))
                ts(vm, a2, 1e-30, None, ALU.max).then_inc(S["a_var"], 1)
                step.go(ts(at_, a2, kv[:, K_TINV:K_TINV + 1], None, ALU.mult))
                step.go(tt(al, al, rB, ALU.mult))
                step(tt(dens, d[:, :, 0, :], d[:, :, 1, :], ALU.add))
                step.go(ts(al, al, float(BANDS) / BW, 0.0, ALU.mult, ALU.add))
                step.go(ts(dens, dens, kv[:, K_BETA:K_BETA + 1], None, ALU.mult))
                pool.wait_ge(S["a_seed"], g + 1)
                newton(step, pool, ab, vm, t4)
                step(tt(ab, ab, at_, ALU.mult))
                for o, a, b in ((mx[:, :, 0:2], ab[:, :, 0:2], ab[:, :, 2:4]),
                                (mx[:, :, 2:3], mx[:, :, 0:1], mx[:, :, 1:2])):
                    step(tt(o, a, b, ALU.subtract))
                    step(ts(o, o, 0.0, None, ALU.max))
                    step(tt(o, o, b, ALU.add))
                tt(e4[:, 0, :, :], ab, mx[:, :, 2:3].broadcast_to([P, GT, BANDS]), ALU.subtract)\
                    .then_inc(S["logits4"], 1)
                step(tt(dens, dens, rB[:, :, 0, :], ALU.mult))

            def bands_b(g):
                pool.wait_ge(S["exps4"], g + 1)
                ex4, sm, fn, mf = e4[:, 1, :, :], v4(18), B(12), B(10)
                step(tt(sm[:, :, 0:2], ex4[:, :, 0:2], ex4[:, :, 2:4], ALU.add))
                tt(lns[:, 0, :], sm[:, :, 0], sm[:, :, 1], ALU.add).then_inc(S["sum4"], 1)
                pool.wait_ge(S["lnsum4"], g + 1)
                tt(e4[:, 0, :, :], e4[:, 0, :, :], bc(lns[:, 1, :], 2, [P, GT, BANDS]), ALU.subtract)\
                    .then_inc(S["log4"], 1)
                pool.wait_ge(S["soft4"], g + 1)
                step(tt(fn, al, bc(ex4, 2, full), ALU.mult))
                if g >= 1:
                    pool.wait_ge(S["t12_turned"], g)
                step.go(ts(t12[:, :, BANDS:2 * BANDS], fn[:, :, 1, :], -1.0, 0.0, ALU.mult, ALU.add))
                step(tt(fn[:, :, 0, :], fn[:, :, 0, :], dens, ALU.add))
                step.go(ts(t12[:, :, 0:BANDS], fn[:, :, 0, :], 1.0, 0.0, ALU.mult, ALU.add))
                step(tt(mf, fn, mB, ALU.mult))
                tt(t12[:, :, 2 * BANDS:], mf[:, :, 1, :], mf[:, :, 0, :], ALU.subtract).then_inc(S["t12_made"], 1)

            def scatter(g):
                p = g % 2
                pool.wait_ge(S["pos_made"], g + 1)
                for j in range(GT):
                    pool.indirect_dma_start(
                        out=sorted_rows, out_offset=bass.IndirectOffsetOnAxis(ap=posi[:, g % 3, j:j + 1], axis=0),
                        in_=row[:, g % 3, j, :], in_offset=None,
                    ).then_inc(S[f"scattered{g % 3}"], 16)

            def next_gather(g):
                pool.wait_ge(S[f"gathered{g % 2}"], 16 * GT * (g // 2))
                gather(g)

            z_squares(0)
            next_gather(2)
            step(pool.memset(decay[:, :, :], 1.0))
            pool.memset(decay[:, :, 0:1], 0.0).then_inc(S["consts_made"], 1)
            z_factors(0)
            z_squares(1)
            step(pool.memset(hpad[:, :, :], 0.0))
            z_factors(1)
            step(pool.memset(upper[:, :], 1.0))
            step(pool.affine_select(out=upper[:, :], in_=upper[:, :], compare_op=ALU.is_gt, fill=0.0,
                                    base=0, pattern=[[1, P]], channel_multiplier=-1))
            step(pool.tensor_copy(upper16[:, :], upper[:, :]))
            step(pool.tensor_copy(ones16[:, :], ones[:, :]))
            step(pool.iota(iota_s[:, :], pattern=[[1, SLOTS]], base=0, channel_multiplier=0, **kw))
            step(pool.iota(tokid[:, :], pattern=[[P, TILES]], base=0, channel_multiplier=1, **kw))
            step(pool.iota(expb[:, :], pattern=[[REGION, E]], base=0, channel_multiplier=0, **kw))
            step(pool.iota(eights[:, :], pattern=[[-1, E]], base=E, channel_multiplier=0, **kw))
            step(pool.memset(base[:, 0, :], 0.0))
            step(pool.memset(padrow[:, :], 0.0))
            pool.memset(padrow[:, D + 3:D + 4], float(T)).then_inc(S["pads_made"], 1)
            z_squares(2)
            z_factors(2)
            next_gather(3)
            for i in range(G + 1):
                if 0 <= i - 2 < G:
                    bands_a(i - 2)
                if 0 <= i - 2 < G:
                    bands_b(i - 2)
                if 0 <= i - 5 < G:
                    scatter(i - 5)
                if i + 3 < G:
                    bias(i + 3)
                if i + 4 < G:
                    next_gather(i + 4)
                if i + 3 < G:
                    z_squares(i + 3)
                    z_factors(i + 3)

            bands_a(G - 1)
            bands_b(G - 1)
            for g in range(G - 4, G):
                scatter(g)

            for t in range(SLOTS):
                k = t % 2
                pool.wait_ge(S["y_made"], t + 1)
                pool.indirect_dma_start(
                    out=out_rows, out_offset=bass.IndirectOffsetOnAxis(ap=yid[:, k, :], axis=0),
                    in_=yo[:, k, :], in_offset=None, bounds_check=T - 1, oob_is_err=False,
                ).then_inc(S[f"put{k}"], 16)

        @block.scalar
        def _(act):
            A = act.activation
            step = Steps(act, "act_steps")

            def seed(v, y, asked, done, g, bias=0.0):
                act.wait_ge(S[asked], g + 1)
                step(A(y, v, ACT.Ln, bias=bias))
                A(y, y, ACT.Exp, scale=-0.5).then_inc(S[done], 1)

            def z_seed(g):
                seed(zs[:, 1, :, :], zs[:, 2, :, :], "z_var", "z_seed", g)

            def z_rows(g):
                p = g % 2
                act.wait_ge(S["z_factors"], g + 1)
                wait(act, "xn_turned", g)
                f = tiles(feat, g)
                for j in range(GT):
                    last = A(xn[:, j, :], f[:, j, :], ACT.Identity, bias=zout[:, p, 2, j:j + 1],
                             scale=zout[:, p, 1, j:j + 1])
                    if j < GT - 1:
                        step.go(last)
                last.then_inc(S["xn_made"], 1)
                act.wait_ge(S["xn_made"], g + 1)
                step.wait()
                for j in range(GT):
                    last = A(f[:, j, :], f[:, j, :], ACT.Identity, scale=zout[:, p, 0, j:j + 1])
                    if j < GT - 1:
                        step.go(last)
                last.then_inc(S["h_made"], 1)

            def x2_rows(g):
                p = g % 3
                act.wait_ge(S["row_made"], g + 1)
                wait(act, "x2_turned", g)
                for j in range(GT):
                    last = A(x2[:, j, :], row[:, p, j, 0:D], ACT.Identity, bias=row[:, p, j, D + 1:D + 2],
                             scale=row[:, p, j, D:D + 1])
                    if j < GT - 1:
                        step.go(last)
                last.then_inc(S["x2_made"], 1)

            act.wait_ge(S["vecs_in"], 32)
            A(kv[:, K_T:K_T + 1], vec[:, C_LGAM:C_LGAM + 1], ACT.Exp).then_inc(S["lgam_exp"], 1)
            act.wait_ge(S["decay_log"], 1)
            A(kv[:, K_R:K_R + 1], kv[:, K_RL:K_RL + 1], ACT.Exp).then_inc(S["tables_made"], 1)
            act.wait_ge(S["angles_made"], 1)
            A(tab[:, 0:2, :], ang[:, :, :], ACT.Sin).then_inc(S["tables_made"], 1)
            A(tab[:, 2, :], ang[:, 0, :], ACT.Sin).then_inc(S["tables_made"], 1)

            def xT_copy(g):
                act.wait_ge(S["xn_turned"], g + 1)
                wait(act, "stats_sum", g - 3)
                A(xT[:, g % 4, :], bank[6][:, :], ACT.Copy).then_inc(S["xT_made"], 1)

            def gate_exp(g):
                act.wait_ge(S["gate_proj"], g + 1)
                wait(act, "mixed_turned", g - 3)
                if g == 0:
                    act.wait_ge(S["setup_made"], 1)
                A(ga[:, :], bank[2][:, :], ACT.Exp, bias=kv[:, K_NBG:K_NBG + 1], scale=-1.0)\
                    .then_inc(S["gate_exp"], 1)

            def gate_rest(g):
                p = g % 2
                act.wait_ge(S["gate_exp"], g + 1)
                if g >= 2:
                    act.wait_ge(S["w2_made"], g - 1)
                step(A(gate[:, p, :], ga[:, :], ACT.Ln, bias=1.0))
                A(gate[:, p, :], gate[:, p, :], ACT.Exp, scale=-1.0).then_inc(S["gate_made"], 1)

            def softplus(g, k, proj, read, used, done, x, bias):
                act.wait_ge(S[proj], g + 1)
                if g >= 1:
                    act.wait_ge(S[used], g)
                step.go(A(sp_l[:, k, :], x[:, :], ACT.Abs, bias=bias))
                A(sp_m[:, k, :], x[:, :], ACT.Relu, bias=bias).then_inc(S[read], 1)
                step.wait()
                step(A(sp_l[:, k, :], sp_l[:, k, :], ACT.Exp, scale=-1.0))
                act.wait_ge(S[read], g + 1)
                A(sp_l[:, k, :], sp_l[:, k, :], ACT.Ln, bias=1.0).then_inc(S[done], 1)

            def exps4(g):
                act.wait_ge(S["logits4"], g + 1)
                A(e4[:, 1, :, :], e4[:, 0, :, :], ACT.Exp).then_inc(S["exps4"], 1)
                act.wait_ge(S["sum4"], g + 1)
                A(lns[:, 1, :], lns[:, 0, :], ACT.Ln).then_inc(S["lnsum4"], 1)
                act.wait_ge(S["log4"], g + 1)
                A(e4[:, 1, :, :], e4[:, 0, :, :], ACT.Exp).then_inc(S["soft4"], 1)

            def h_seed(g):
                seed(bt_[:, 1, :, :, 0], bt_[:, 2, :, :, 0], "h_var", "h_seed", g)

            def a_seed(g):
                seed(bt_[:, 16, :, 0, :], bt_[:, 14, :, 0, :], "a_var", "a_seed", g)

            def h2_seed(g):
                seed(mvd[:, :, 1], ds_[:, 1, :], "h2_stats", "h2_seed", g, bias=eps1[:, :])

            def mixed_copy(g):
                act.wait_ge(S["mixed"], g + 1)
                A(ga[:, :], bank[2][:, :], ACT.Copy).then_inc(S["mixed_copied"], 1)

            def x2T_copy(g):
                act.wait_ge(S["x2_turned"], g + 1)
                wait(act, "router_logits", g)
                A(x2T[:, :], bank[3][:, :], ACT.Copy).then_inc(S["x2T_made"], 1)

            def exps8(g):
                act.wait_ge(S["shifted8"], g + 1)
                A(ex[:, :, :], lt[:, 0, :, :], ACT.Exp).then_inc(S["exps8"], 1)

            def t12_copy(g):
                act.wait_ge(S["t12_turned"], g + 1)
                wait(act, "mixed", g)
                A(t12T[:, :], bank[7][0:3 * BANDS, :], ACT.Copy).then_inc(S["t12_copied"], 1)

            act.preload_act_table_set("natural_log_exp_and_others")
            z_seed(0)
            z_rows(0)
            xT_copy(0)
            z_seed(1)
            z_rows(1)
            xT_copy(1)
            z_seed(2)
            for i in range(G + 1):
                if 0 <= i - 2 < G:
                    h_seed(i - 2)
                if 0 <= i - 4 < G:
                    h2_seed(i - 4)
                if 0 <= i - 1 < G:
                    softplus(i - 1, 1, "bth_proj", "bth_read", "w2_made", "sp2_made", bank[6], kv[:, K_BT:K_BT + 1])
                if 0 <= i < G:
                    gate_exp(i)
                if 0 <= i - 2 < G:
                    a_seed(i - 2)
                if 0 <= i - 4 < G:
                    x2_rows(i - 4)
                if 0 <= i < G:
                    gate_rest(i)
                    softplus(i, 0, "bs_proj", "bs_read", "w1_made", "sp1_made", bank[3], vec[:, C_BBS:C_BBS + 1])
                if 0 <= i - 3 < G:
                    mixed_copy(i - 3)
                if 0 <= i - 2 < G:
                    exps4(i - 2)
                if 0 <= i - 4 < G:
                    x2T_copy(i - 4)
                if 0 <= i - 1 < G:
                    g = i - 1
                    act.wait_ge(S["H_made"], g + 1)
                    wait(act, "stats_sum", g)
                    A(hsq[:, :, :], H[:, g % 3, :, :], ACT.Square).then_inc(S["hsq_made"], 1)
                if i + 2 < G:
                    z_rows(i + 2)
                if 0 <= i - 4 < G:
                    exps8(i - 4)
                if i == G:
                    h2_seed(G - 3)
                    x2_rows(G - 3)
                if 0 <= i - 1 < G:
                    g = i - 1
                    act.wait_ge(S["stats_sum"], g + 1)
                    A(turned[:, :], bank[7][0:NROW, :], ACT.Copy).then_inc(S["sums_copied"], 1)
                    act.wait_ge(S["stats_turned"], g + 1)
                    wait(act, "logits4", g)
                    A(st[:, :, :, :].rearrange("p a b c -> p (a b c)"), bank[7][:, 0:GT * NROW], ACT.Copy)\
                        .then_inc(S["stats_copied"], 1)
                if i + 2 < G:
                    xT_copy(i + 2)
                if 0 <= i - 2 < G:
                    t12_copy(i - 2)
                if i + 3 < G:
                    z_seed(i + 3)

            last, left = G - 1, G - 2
            h_seed(last)
            x2T_copy(G - 3)
            a_seed(last)
            exps8(G - 3)
            mixed_copy(left)
            exps4(last)
            h2_seed(left)
            x2_rows(left)
            t12_copy(last)
            x2T_copy(left)
            exps8(left)
            mixed_copy(last)
            h2_seed(last)
            x2_rows(last)
            x2T_copy(last)
            exps8(last)

            def gelu(t, k):
                act.wait_ge(S["hidden_b"], t + 1)
                if t >= 2:
                    act.wait_ge(S["hidden_turned"], t - 1)
                A(hg[:, k, :], hb[:, k, :], ACT.Gelu).then_inc(S["hidden_g"], 1)

            def hT_copy(t, k):
                act.wait_ge(S["hidden_turned"], t + 1)
                if t >= 2:
                    act.wait_ge(S["y_sum"], t - 1)
                A(hT[:, k, :], bank[4 + k][:, :], ACT.Copy).then_inc(S["hT_made"], 1)

            pipeline(((0, gelu), (-2, hT_copy)))

        @block.tensor
        def _(pe):
            mm = pe.matmul

            pe.wait_ge(S["sel_made"], 1)
            pe.wait_ge(S["setup_in"], 48)
            for s in range(2):
                pe.transpose(bank[0][0:3 * BANDS, s * P:(s + 1) * P], selz[:, s, :], ident[:, :])
            mm(bank[1][0:3 * BANDS, 0:P], selz[:, 2, :], W[:, W_MIMO, :], start=True, stop=True)
            for r in range(2):
                mm(bank[2][:, r * 5:r * 5 + 5], W[:, W_PHIN + r, :], sel5[:, :], start=True, stop=True)
            for r in range(2):
                last = mm(bank[3][:, r * 4:r * 4 + 4], bphib[:, r, :], sel5[:, 0:BANDS], start=True, stop=True)
            last.then_inc(S["sel_turned"], 1)

            def turn(dst, src, done):
                for j in range(GT):
                    last = pe.transpose(dst[:, j * P:(j + 1) * P], src[:, j, :], ident[:, :])
                last.then_inc(S[done], 1)

            def z_turn(g):
                pe.wait_ge(S["xn_made"], g + 1)
                wait(pe, "xT_made", g)
                wait(pe, "bth_read", g - 2)
                turn(bank[6], xn, "xn_turned")

            def psi_project(g):
                pe.wait_ge(S["xT_made"], g + 1)
                wait(pe, "psi_read", g)
                for r in range(2):
                    last = mm(bank[r][:, :], W[:, W_PSI + r, :], xT[:, g % 4, :], start=True, stop=True)
                last.then_inc(S["psi_proj"], 1)

            def mix(g):
                pe.wait_ge(S["uu_made"], g + 1)
                wait(pe, "gate_exp", g + 4)
                wait(pe, "h2_stats", g)
                for r in range(2):
                    mm(bank[2][:, :], W[:, W_MIMO, :], uu[:, r, :], start=(r == 0), stop=False)
                mm(bank[2][:, :], mimoC[:, :], t12T[:, :], start=False, stop=True).then_inc(S["mixed"], 1)

            def mix_turn(g):
                pe.wait_ge(S["mixed_copied"], g + 1)
                for j in range(GT):
                    c = slice(j * P, (j + 1) * P)
                    last = pe.transpose(bank[2][:, c], ga[:, c], ident[:, :])
                last.then_inc(S["mixed_turned"], 1)

            def x2_turn(g):
                pe.wait_ge(S["x2_made"], g + 1)
                wait(pe, "bs_read", g + 5)
                wait(pe, "pos_made", g)
                turn(bank[3], x2, "x2_turned")

            def router(g):
                pe.wait_ge(S["x2T_made"], g + 1)
                for j in range(GT):
                    last = mm(bank[3][:, j * E:(j + 1) * E], x2T[:, j * P:(j + 1) * P], gws[:, :],
                              start=True, stop=True)
                last.then_inc(S["router_logits"], 1)

            def ranks(g):
                pe.wait_ge(S["onehot_made"], g + 1)
                for j in range(GT + 1):
                    o = bank[3][:, j * E:(j + 1) * E]
                    for s in range(j):
                        last = mm(o, ones16[:, :], oh[:, s, :], start=(s == 0), stop=(s == j - 1 and j == GT))
                    if j < GT:
                        last = mm(o, upper16[:, :], oh[:, j, :], start=(j == 0), stop=True)
                last.then_inc(S["ranks_made"], 1)

            def factors_turn(g):
                pe.wait_ge(S["t12_made"], g + 1)
                wait(pe, "stats_copied", g + 2)
                for j in range(GT):
                    last = pe.transpose(bank[7][0:3 * BANDS, j * P:(j + 1) * P], t12[:, j, :], ident[:, :])
                last.then_inc(S["t12_turned"], 1)

            def spread(g):
                pe.wait_ge(S["t12_copied"], g + 1)
                wait(pe, "prod_made", g + 2)
                wait(pe, "uu_made", g)
                for r in range(2):
                    last = mm(bank[4 + r][:, :], selT[:, r, :], t12T[:, :], start=True, stop=True)
                last.then_inc(S["spread"], 1)

            z_turn(0)
            z_turn(1)
            pe.wait_ge(S["setup_made"], 1)
            psi_project(0)
            for i in range(G + 1):
                if 0 <= i - 1 < G:
                    g = i - 1
                    later = b4(bank[6][:, :])[:, :, 1:SEQ]
                    for k, w in enumerate((W[:, W_BTH, :], bth_neg[:, :], W[:, W_BTH + 1, :], W[:, W_BTH + 1, :])):
                        pe.wait_ge(S["spun_made"], 2 * g + 1 + k // 2)
                        last = mm(later, w, b4(spun[:, k, :])[:, :, 0:SEQ - 1], start=False, stop=(k == 3))
                    last.then_inc(S["bth_proj"], 1)
                if 0 <= i < G:
                    x = xT[:, i % 4, :]
                    wait(pe, "h2_stats", i - 3)
                    mm(bank[2][:, :], W[:, W_GATE, :], x, start=True, stop=True).then_inc(S["gate_proj"], 1)
                    wait(pe, "pos_made", i - 4)
                    mm(bank[3][:, :], W[:, W_BS, :], x, start=True, stop=True).then_inc(S["bs_proj"], 1)
                if 0 <= i - 1 < G:
                    g = i - 1
                    wait(pe, "uu_made", i - 2)
                    for r in range(2):
                        last = mm(bank[4 + r][:, :], W[:, W_PHI + r, :], xT[:, g % 4, :], start=True, stop=True)
                    last.then_inc(S["phi_proj"], 1)
                if 0 <= i - 3 < G:
                    mix(i - 3)
                if 0 <= i - 3 < G:
                    mix_turn(i - 3)
                if i + 1 < G:
                    psi_project(i + 1)
                if 0 <= i - 4 < G:
                    x2_turn(i - 4)
                    router(i - 4)
                if 0 <= i - 1 < G:
                    g = i - 1
                    pe.wait_ge(S["H_made"], g + 1)
                    wait(pe, "stats_copied", g)
                    wait(pe, "t12_copied", i - 2)
                    mm(bank[7][0:NROW, :], wq[:, :], xT[:, g % 4, :], start=True, stop=False)
                    for k in range(2):
                        o = NROW - NSUM_W * (k + 1)
                        mm(bank[7][0:NROW, :], selw[:, o:o + NROW], H[:, g % 3, k, :], start=False, stop=False)
                    pe.wait_ge(S["hsq_made"], g + 1)
                    pe.wait_ge(S["prod_made"], g + 1)
                    srcs = [hsq[:, 0, :], hsq[:, 1, :], xp[:, 0, :], xp[:, 1, :], xp[:, 2, :], xp[:, 3, :]]
                    for k, x in enumerate(srcs):
                        o = NROW - NSUM_W * (k + 3)
                        last = mm(bank[7][0:NROW, :], selw[:, o:o + NROW], x, start=False, stop=(k == len(srcs) - 1))
                    last.then_inc(S["stats_sum"], 1)
                    pe.wait_ge(S["sums_copied"], g + 1)
                    for j in range(GT):
                        last = pe.transpose(bank[7][:, j * NROW:(j + 1) * NROW], turned[:, j * P:(j + 1) * P],
                                            ident[0:NROW, 0:NROW])
                    last.then_inc(S["stats_turned"], 1)
                if 0 <= i - 4 < G:
                    ranks(i - 4)
                if i + 2 < G:
                    z_turn(i + 2)
                if 0 <= i - 2 < G:
                    factors_turn(i - 2)
                if 0 <= i < G:
                    wait(pe, "xT_made", i + 3)
                    mm(bank[6][:, :], W[:, W_BTX, :], xT[:, i % 4, :], start=True, stop=False)
                if 0 <= i - 2 < G:
                    spread(i - 2)

            last, left = G - 1, G - 2
            x2_turn(G - 3)
            router(G - 3)
            mix(left)
            mix_turn(left)
            ranks(G - 3)
            factors_turn(last)
            x2_turn(left)
            spread(last)
            router(left)
            mix(last)
            ranks(left)
            mix_turn(last)
            x2_turn(last)
            router(last)
            ranks(last)

            pe.wait_ge(S["weights_in"], 64)
            pe.wait_ge(S["plan_made"], 1)

            def x_turn(t, k):
                pe.wait_ge(S["y2_made"], t + 1)
                if t >= 2:
                    pe.wait_ge(S["y2T_made"], t - 1)
                pe.transpose(bank[k][:, 0:P], y2[:, k, :], ident[:, :]).then_inc(S["y2_turned"], 1)

            expert_of = {}

            def up(t, k):
                e = expert_of[t] = expert(pe, t)
                pe.wait_ge(S["y2T_made"], t + 1)
                if t >= 2:
                    pe.wait_ge(S["hidden_b"], t - 1)
                mm(bank[2 + k][:, :], y2T[:, k, :], at(w1s, e), start=True, stop=True).then_inc(S["hidden"], 1)

            def h_turn(t, k):
                pe.wait_ge(S["hidden_g"], t + 1)
                if t >= 2:
                    pe.wait_ge(S["hT_made"], t - 1)
                for c in range(FC):
                    last = pe.transpose(bank[4 + k][:, c * P:(c + 1) * P], hg[:, k, c * P:(c + 1) * P], ident[:, :])
                last.then_inc(S["hidden_turned"], 1)

            def down(t, k):
                e = expert_of.pop(t)
                pe.wait_ge(S["hT_made"], t + 1)
                if t >= 2:
                    pe.wait_ge(S["y_made"], t - 1)
                for c in range(FC):
                    w = w2s[:, bass.ds(e, 1), c * D:(c + 1) * D].rearrange("p a b -> p (a b)")
                    last = mm(bank[6 + k][:, 0:D], hT[:, k, c * P:(c + 1) * P], w, start=(c == 0), stop=(c == FC - 1))
                last.then_inc(S["y_sum"], 1)

            pipeline(((1, x_turn), (0, up), (-2, h_turn), (-3, down)))

        @block.vector
        def _(dve):
            step = Steps(dve, "dve_steps")
            tt, ts, stt, cp = dve.tensor_tensor, dve.tensor_scalar, dve.scalar_tensor_tensor, dve.tensor_copy
            col = lambda c: vec[:, c:c + 1]
            kc = lambda c: kv[:, c:c + 1]

            def z_stats(g):
                p = g % 2
                f = tiles(feat, g)
                if g < 3:
                    dve.wait_ge(S[f"gathered{p}"], 16 * GT * (g // 2 + 1))
                    step(tt(f, f, bc(embb[:, :], 1, [P, GT, D]), ALU.add))
                else:
                    dve.wait_ge(S["biased"], g - 2)
                if g >= 2:
                    dve.wait_ge(S["z_factors"], g - 1)
                for j in range(GT):
                    step.go(dve.bn_stats(bnz[:, p, j, :], f[:, j, :]))
                step.wait()
                for j in range(GT):
                    last = dve.bn_aggr(mvz[:, p, j, :], bnz[:, p, j, :])
                    if j < GT - 1:
                        step.go(last)
                last.then_inc(S["z_stats"], 1)

            dve.wait_ge(S["embb_in"], 16)
            z_stats(0)
            dve.wait_ge(S["vecs_in"], 32)
            dve.wait_ge(S["iotas_made"], 1)
            step(ts(kc(K_ADT), col(C_DT), -1.0, None, ALU.mult))
            step.go(tt(kc(K_ADT), kc(K_ADT), col(C_DT), ALU.max))
            step.go(ts(kc(K_NBG), col(C_BGATE), -1.0, None, ALU.mult))
            step.go(tt(kc(K_BT), col(C_BBTX), col(C_BBTH), ALU.add))
            step.go(ts(kc(K_BETA), col(C_BETA), 1.0 / BW, None, ALU.mult))
            step.go(ts(kc(K_TINV), col(C_TAU), 1e-4, None, ALU.max))
            step.wait()
            step(dve.reciprocal(kc(K_TINV), kc(K_TINV)))
            step.go(ts(kc(K_TINV), kc(K_TINV), 1.0 / BW, None, ALU.mult))
            dve.wait_ge(S["lgam_exp"], 1)
            step(tt(kc(K_RL), kc(K_T), kc(K_ADT), ALU.mult))
            ts(kc(K_RL), kc(K_RL), -1.0, None, ALU.mult).then_inc(S["decay_log"], 1)
            step(ts(ang[:, 1, :], iota_t[:, :], kc(K_ADT), col(C_OMEGA), ALU.mult, ALU.mult))
            step.go(cp(ang[:, 0, :], ang[:, 1, :]))
            step.go(ts(rnd[:, 0, :], ang[:, 1, :], 1.0 / TWO_PI, 0.25, ALU.mult, ALU.add))
            step.go(ts(rnd[:, 1, :], ang[:, 1, :], 1.0 / TWO_PI, None, ALU.mult))
            step.wait()
            step(ts(rnd[:, :, :], rnd[:, :, :], ROUND, None, ALU.add))
            step(ts(rnd[:, :, :], rnd[:, :, :], -ROUND, None, ALU.add))
            for part in (PI_A, PI_B, PI_C):
                step(stt(ang[:, :, :], rnd[:, :, :], -part, ang[:, :, :], ALU.mult, ALU.add))
            step(ts(ang[:, 0, :], ang[:, 0, :], np.pi / 2, None, ALU.add))
            ts(ang[:, :, :], ang[:, :, :], 3.1415925, -3.1415925, ALU.min, ALU.max).then_inc(S["angles_made"], 1)
            step(cp(bandf[:, :], bandi[:, :]))
            step(ts(bandf[:, :], bandf[:, :], iota_p[:, 0:1], None, ALU.is_equal))
            step(dve.tensor_reduce(sel5[:, 0:BANDS], bandf[:, :].rearrange("p (k w) -> p k w", k=BANDS), AX.X, ALU.add))
            for r in range(2):
                step.go(ts(bphib[:, r, :], ones[:, :], col(C_BPHI + r), None, ALU.mult))
            for s in range(3):
                step.go(cp(selz[:, s, s * BANDS:(s + 1) * BANDS], sel5[:, 0:BANDS]))
            step.wait()
            cp(kc(K_T), kc(K_BT)).then_inc(S["sel_made"], 1)
            z_stats(1)
            dve.wait_ge(S["setup_in"], 48)
            step.go(ts(bth_neg[:, :], W[:, W_BTH, :], -1.0, None, ALU.mult))
            dve.wait_ge(S["sel_turned"], 1)
            step.go(cp(selT[:, :, :], bank[0][0:3 * BANDS, 0:2 * P].rearrange("p (a b) -> p a b", a=2)))
            step.go(cp(mimoC[:, :], bank[1][0:3 * BANDS, 0:P]))
            step.go(cp(wq[:, NPROD * NSUM_W:], bank[2][:, 0:10]))
            step.go(cp(bq[:, :, :], bank[3][:, 0:8].rearrange("p (a b) -> p a b", a=2)))
            dve.wait_ge(S["tables_made"], 3)
            dve.wait_ge(S["consts_made"], 1)
            step.wait()
            step(ts(decay[:, :, :], decay[:, :, :], kc(K_R), None, ALU.mult))
            cp(kc(K_T), kc(K_R)).then_inc(S["setup_made"], 1)

            def newton_v(y, v, t):
                step(tt(t, y, y, ALU.mult))
                step(stt(t, t, -0.5, v, ALU.mult, ALU.mult))
                step(stt(y, t, 1.5, y, ALU.add, ALU.mult))

            cs = lambda k: bc(tab[:, k, :], 1, [P, GB, SEQ])
            def cs2(k):
                return bc(tab[:, k:k + 2, :], 2, [P, 2, GB, SEQ])

            def psi_turn(g):
                p = g % 2
                dve.wait_ge(S["psi_proj"], g + 1)
                step.wait()
                for k, (r, c) in enumerate(((0, 0), (1, 1), (1, 0), (0, 1))):
                    last = stt(b4(rot[:, k, :]), b4(bank[r][:, :]), col(C_BPSI + r), cs(c), ALU.add, ALU.mult)
                    if k < 3:
                        step.go(last)
                last.then_inc(S["psi_read"], 1)
                dve.wait_ge(S["psi_read"], g + 1)
                step.wait()
                step.go(tt(psi[:, p, 0, :], rot[:, 0, :], rot[:, 1, :], ALU.add))
                step(tt(psi[:, p, 1, :], rot[:, 2, :], rot[:, 3, :], ALU.subtract))

            def scan(g, k, made, w_made, dst):
                p = g % 2
                dve.wait_ge(S[made], g + 1)
                step(tt(wg[:, :], sp_m[:, k, :], sp_l[:, k, :], ALU.add))
                if k == 0:
                    dve.wait_ge(S["gate_made"], g + 1)
                tt(wg[:, :], wg[:, :], gate[:, p, :], ALU.mult).then_inc(S[w_made], 1)
                dve.wait_ge(S[w_made], g + 1)
                step(tt(u[:, :, :], psi[:, p, :, :], bc(wg[:, :], 1, [P, 2, GN]), ALU.mult))
                step(dve.tensor_tensor_scan(g_s[:, :, :].rearrange("p a b -> p (a b)"),
                                            decay[:, :, :].rearrange("p a b -> p (a b)"),
                                            u[:, :, :].rearrange("p a b -> p (a b)"), 0.0, ALU.mult, ALU.add))
                gs = g_s[:, :, :].rearrange("p r (b t) -> p r b t", b=GB)
                if k == 0:
                    wait(dve, "bth_proj", g)
                for q in range(2):
                    last = tt(dst[:, 2 * q:2 * q + 2, :].rearrange("p r (b t) -> p r b t", b=GB), gs, cs2(q), ALU.mult)
                    if k == 0:
                        last.then_inc(S["spun_made"], 1)
                    else:
                        step.go(last)

            def scout(g):
                scan(g, 0, "sp1_made", "w1_made", spun)

            def main_scan(g):
                scan(g, 1, "sp2_made", "w2_made", rot)
                step.wait()
                for r in range(2):
                    step.go(tt(hpad[:, r * GB:(r + 1) * GB, 2:2 + SEQ], b4(rot[:, 2 * r, :]), b4(rot[:, 2 * r + 1, :]),
                               (ALU.subtract, ALU.add)[r]))
                step.wait()
                tap = lambda k: hpad[:, :, 2 - k:2 - k + SEQ]
                f4 = fir[:, :, :].rearrange("p r (b t) -> p (r b) t", b=GB)
                h4 = H[:, g % 3, :, :].rearrange("p r (b t) -> p (r b) t", b=GB)
                step(stt(f4, tap(1), 4.0, tap(0), ALU.mult, ALU.add))
                if g >= 3:
                    dve.wait_ge(S["stats_sum"], g - 2)
                tt(h4, f4, tap(2), ALU.add).then_inc(S["H_made"], 1)

            def products(g):
                dve.wait_ge(S["H_made"], g + 1)
                dve.wait_ge(S["phi_proj"], g + 1)
                if g >= 1:
                    dve.wait_ge(S["stats_sum"], g)
                for k, (hr, pr) in enumerate(((0, 0), (1, 1), (0, 1), (1, 0))):
                    last = stt(xp[:, k, :], bank[4 + pr][:, :], col(C_BPHI + pr), H[:, g % 3, hr, :], ALU.add, ALU.mult)
                    if k < 3:
                        step.go(last)
                last.then_inc(S["prod_made"], 1)

            def weigh(g):
                dve.wait_ge(S["spread"], g + 1)
                if g >= 1:
                    dve.wait_ge(S["mixed"], g)
                step.go(tt(uu[:, 0, :], H[:, g % 3, 0, :], bank[4][:, :], ALU.mult))
                tt(uu[:, 1, :], H[:, g % 3, 1, :], bank[5][:, :], ALU.mult).then_inc(S["uu_made"], 1)

            def residual(g):
                p = g % 3
                dve.wait_ge(S["mixed_turned"], g + 1)
                dve.wait_ge(S["h_made"], g + 1)
                if g >= 3:
                    dve.wait_ge(S[f"scattered{p}"], 16 * GT * (g // 3))
                h2 = row[:, p, :, 0:D]
                step(tt(h2, tiles(feat, g), bank[2][:, :].rearrange("p (a b) -> p a b", a=GT), ALU.add))
                for j in range(GT):
                    step.go(dve.bn_stats(bnd[:, j, :], h2[:, j, :]))
                step.wait()
                for j in range(GT):
                    last = dve.bn_aggr(mvd[:, j, :], bnd[:, j, :])
                    if j < GT - 1:
                        step.go(last)
                    else:
                        last.then_inc(S["h2_stats"], 1)

            def residual_factors(g):
                p = g % 3
                v, y, t = (ds_[:, k, :] for k in range(3))
                dve.wait_ge(S["h2_stats"], g + 1)
                step.go(cp(row[:, p, :, D + 3:D + 4], tiles(tokid, g).unsqueeze(2)))
                step(ts(v, mvd[:, :, 1], LN_EPS, None, ALU.add))
                dve.wait_ge(S["h2_seed"], g + 1)
                newton_v(y, v, t)
                step.go(cp(row[:, p, :, D:D + 1], y.unsqueeze(2)))
                stt(row[:, p, :, D + 1:D + 2], mvd[:, :, 0:1], -1.0, y.unsqueeze(2), ALU.mult, ALU.mult)\
                    .then_inc(S["row_made"], 1)

            def route(g):
                dve.wait_ge(S["router_logits"], g + 1)
                e3 = [P, GT, E]
                first, pick, best = lt[:, 1, :, :], lt[:, 2, :, :], lt[:, 3, :, :]
                tt(lg[:, :, :], bank[3][:, 0:GT * E].rearrange("p (a b) -> p a b", a=GT),
                   bc(gbs[:, :], 1, e3), ALU.add).then_inc(S["logits_read"], 1)
                dve.wait_ge(S["logits_read"], g + 1)
                step(dve.tensor_reduce(lm[:, 0, :], lg[:, :, :], AX.X, ALU.max))
                tt(lt[:, 0, :, :], lg[:, :, :], bc(lm[:, 0, :], 2, e3), ALU.subtract).then_inc(S["shifted8"], 1)
                step(tt(pick, lg[:, :, :], bc(lm[:, 0, :], 2, e3), ALU.is_ge))
                step(tt(first, pick, bc(eights[:, :], 1, e3), ALU.mult))
                step(dve.tensor_reduce(lm[:, 1, :], first, AX.X, ALU.max))
                tt(oh[:, :, :], first, bc(lm[:, 1, :], 2, e3), ALU.is_equal).then_inc(S["onehot_made"], 1)

            def place(g):
                p = g % 2
                e3 = [P, GT, E]
                dve.wait_ge(S["exps8"], g + 1)
                step(dve.tensor_reduce(lm[:, 2, :], ex[:, :, :], AX.X, ALU.add))
                step(dve.reciprocal(row[:, g % 3, :, D + 2:D + 3], lm[:, 2, :].unsqueeze(2)))
                a, b = pos[:, 0, :, :], pos[:, 1, :, :]
                step(tt(base[:, 1, :], base[:, 0, :], expb[:, :], ALU.add))
                dve.wait_ge(S["ranks_made"], g + 1)
                dve.wait_ge(S["onehot_made"], g + 1)
                step.go(tt(a, bank[3][:, 0:GT * E].rearrange("p (a b) -> p a b", a=GT), bc(base[:, 1, :], 1, e3), ALU.add))
                step.wait()
                step.go(tt(base[:, 0, :], base[:, 0, :], bank[3][:, GT * E:(GT + 1) * E], ALU.add))
                step(tt(b, a, oh[:, :, :], ALU.mult))
                step(dve.tensor_reduce(lm[:, 3, :], b, AX.X, ALU.add))
                cp(posi[:, g % 3, :], lm[:, 3, :]).then_inc(S["pos_made"], 1)

            z_stats(2)
            for i in range(G + 1):
                if 0 <= i < G:
                    psi_turn(i)
                if 0 <= i - 3 < G:
                    weigh(i - 3)
                if 0 <= i - 4 < G:
                    residual(i - 4)
                if 0 <= i - 5 < G:
                    place(i - 5)
                if 0 <= i - 4 < G:
                    residual_factors(i - 4)
                if 0 <= i - 1 < G:
                    main_scan(i - 1)
                    products(i - 1)
                if i + 3 < G:
                    z_stats(i + 3)
                if 0 <= i - 4 < G:
                    route(i - 4)
                if 0 <= i < G:
                    scout(i)

            last, left = G - 1, G - 2
            residual(G - 3)
            residual_factors(G - 3)
            place(G - 4)
            weigh(left)
            route(G - 3)
            residual(left)
            place(G - 3)
            residual_factors(left)
            weigh(last)
            route(left)
            place(left)
            residual(last)
            residual_factors(last)
            route(last)
            place(last)

            n_e = base[:, 0, :]
            begun, ends, starts = (mp[:, k, :] for k in range(3))
            step(tt(mp[:, 5, :], n_e, expb[:, :], ALU.add))
            cp(plan[:, 2 * SLOTS:], mp[:, 5, :]).then_inc(S["pads_planned"], 1)
            full = [P, E, TILES]
            step.go(cp(mcmp[:, :, :], bc(n_e, 2, full)))
            step.go(ts(mp[:, 4, :], expb[:, :], 0.0, 1.0, ALU.mult, ALU.add))
            step.wait()
            step(ts(mt[:, 6, 0:TILES], iota_s[:, 0:TILES], float(P), None, ALU.mult))
            step(tt(mcmp[:, :, :], mcmp[:, :, :], bc(mt[:, 6, 0:TILES], 1, full), ALU.is_gt))
            step(dve.tensor_reduce(begun, mcmp[:, :, :], AX.X, ALU.add))
            step(dve.tensor_tensor_scan(ends, mp[:, 4, :], begun, 0.0, ALU.mult, ALU.add))
            step(tt(starts, ends, begun, ALU.subtract))
            fs = [P, SLOTS, E]
            step(tt(mcmp2[:, :, :], bc(iota_s[:, :], 2, fs), bc(starts, 1, fs), ALU.is_ge))
            step(dve.tensor_reduce(mt[:, 0, :], mcmp2[:, :, :], AX.X, ALU.add))
            step(ts(mt[:, 0, :], mt[:, 0, :], -1.0, None, ALU.add))
            step(tt(mcmp2[:, :, :], mcmp2[:, :, :], bc(starts, 1, fs), ALU.mult))
            step(dve.tensor_reduce(mt[:, 1, :], mcmp2[:, :, :], AX.X, ALU.max))
            step(tt(mt[:, 2, :], iota_s[:, :], mt[:, 1, :], ALU.subtract))
            step(ts(mt[:, 2, :], mt[:, 2, :], float(P), None, ALU.mult))
            step(stt(mt[:, 3, :], mt[:, 0, :], float(REGION), mt[:, 2, :], ALU.mult, ALU.add))
            step(ts(mt[:, 4, :], iota_s[:, :], ends[:, E - 1:E], None, ALU.is_ge))
            step(ts(mt[:, 5, :], mt[:, 3, :], -1.0, float(DUMMY), ALU.mult, ALU.add))
            step(tt(mt[:, 5, :], mt[:, 5, :], mt[:, 4, :], ALU.mult))
            step(tt(mt[:, 3, :], mt[:, 3, :], mt[:, 5, :], ALU.add))
            step.go(cp(plan[:, 0:SLOTS], mt[:, 0, :]))
            cp(plan[:, SLOTS:2 * SLOTS], mt[:, 3, :]).then_inc(S["plan_made"], 1)
            step.wait()
            dve.wait_ge(S["plan_made"], 1)
            dve.wait_ge(S["weights_in"], 64)

            def f_in(t, k):
                dve.wait_ge(S[f"rows_in{t % DEPTH}"], 16 * (t // DEPTH + 1))
                if t >= 2:
                    dve.wait_ge(S["y2_turned"], t - 1)
                ts(y2[:, k, :], at(xr, t)[:, 0:D], at(xr, t)[:, D:D + 1], at(xr, t)[:, D + 1:D + 2], ALU.mult, ALU.add)\
                    .then_inc(S["y2_made"], 1)

            def f_turned(t, k):
                dve.wait_ge(S["y2_turned"], t + 1)
                if t >= 2:
                    dve.wait_ge(S["hidden"], t - 1)
                cp(y2T[:, k, :], bank[k][:, 0:P]).then_inc(S["y2T_made"], 1)

            expert_of = {}

            def f_bias(t, k):
                e = expert_of[t] = expert(dve, t)
                dve.wait_ge(S["hidden"], t + 1)
                if t >= 2:
                    dve.wait_ge(S["hidden_g"], t - 1)
                tt(hb[:, k, :], bank[2 + k][:, :], at(b1s, e), ALU.add).then_inc(S["hidden_b"], 1)

            def f_out(t, k):
                e = expert_of.pop(t)
                dve.wait_ge(S["y_sum"], t + 1)
                if t >= 2:
                    dve.wait_ge(S[f"put{k}"], 8 * (t - k))
                tt(yb[:, k, :], bank[6 + k][:, 0:D], at(b2s, e), ALU.add).then_inc(S["y_steps"], 1)
                cp(yid[:, k, :], at(xr, t)[:, D + 3:D + 4]).then_inc(S["y_steps"], 1)
                dve.wait_ge(S["y_steps"], 2 * t + 2)
                stt(yo[:, k, :], yb[:, k, :], at(xr, t)[:, D + 2:D + 3], at(xr, t)[:, 0:D], ALU.mult, ALU.add)\
                    .then_inc(S["y_made"], 1)

            pipeline(((2, f_in), (1, f_turned), (0, f_bias), (-3, f_out)))


def kernel(x, L0_tok_W, L0_tok_b, L0_attn_omega, L0_attn_log_gamma, L0_attn_dt, L0_attn_W_psi, L0_attn_b_psi,
           L0_attn_W_phi, L0_attn_b_phi, L0_attn_W_bs, L0_attn_b_bs, L0_attn_W_btx, L0_attn_b_btx, L0_attn_W_bth,
           L0_attn_b_bth, L0_attn_w_gate, L0_attn_b_gate, L0_attn_tau, L0_attn_beta, L0_attn_mimo_w,
           L0_attn_band_idx, L0_ffn_Ws, L0_ffn_bs, L0_ffn_W1, L0_ffn_b1, L0_ffn_W2, L0_ffn_b2):
    import concourse.bacc as bacc
    from concourse.bass_utils import run_bass_kernel_spmd

    lay = np.ascontiguousarray
    n = np.asarray
    every = lambda v: lay(np.broadcast_to(n(v).reshape(1, -1), (P, n(v).size)))
    mimo = n(L0_attn_mimo_w)
    groups, width = mimo.shape[0], mimo.shape[1]
    mimo_t = np.zeros((D, D), mimo.dtype)
    for g in range(groups):
        s = slice(g * width, (g + 1) * width)
        mimo_t[s, s] = mimo[g].T
    w_psi, w_phi, w_bth = n(L0_attn_W_psi), n(L0_attn_W_phi), n(L0_attn_W_bth)
    blocks = [w_psi[:D].T, w_psi[D:].T, w_phi[:D].T, w_phi[D:].T, n(L0_attn_W_bs).T, n(L0_attn_W_btx).T,
              w_bth[:, :D].T, w_bth[:, D:].T, np.broadcast_to(n(L0_attn_w_gate).reshape(D, 1), (D, D)),
              mimo_t, w_phi[:D], w_phi[D:]]
    one = lambda v: np.broadcast_to(n(v).reshape(1), (D,))
    b_psi, b_phi = n(L0_attn_b_psi), n(L0_attn_b_phi)
    cols = [b_psi[:D], b_psi[D:], b_phi[:D], b_phi[D:], n(L0_attn_b_bs), n(L0_attn_b_btx), n(L0_attn_b_bth),
            n(L0_attn_omega), n(L0_attn_log_gamma), one(L0_attn_dt), one(L0_attn_b_gate), one(L0_attn_tau),
            one(L0_attn_beta)]
    arrays = {
        "ids": lay(n(x).reshape(TILES, P).T),
        "emb": lay(n(L0_tok_W).T),
        "emb_b": every(L0_tok_b),
        "wcat": lay(np.stack(blocks, axis=1)),
        "vecs": lay(np.stack(cols, axis=1)),
        "band": every(L0_attn_band_idx),
        "gate_ws": lay(n(L0_ffn_Ws)),
        "gate_bs": every(L0_ffn_bs),
        "w1": lay(n(L0_ffn_W1).transpose(1, 0, 2)),
        "b1": every(L0_ffn_b1).reshape(P, E, F),
        "w2": lay(n(L0_ffn_W2).reshape(E, FC, P, D).transpose(2, 0, 1, 3)).reshape(P, E, FC * D),
        "b2": every(L0_ffn_b2).reshape(P, E, D),
    }
    nc = bacc.Bacc("TRN2", target_bir_lowering=False, num_devices=1)
    args = [nc.dram_tensor(f"in_{k}", a.shape, mybir.dt.from_np(a.dtype), kind="ExternalInput").ap()
            for k, a in arrays.items()]
    out = nc.dram_tensor("out", (BATCH, SEQ, D), F32, kind="ExternalOutput").ap()
    lm_tower(nc, *args, out)
    r = run_bass_kernel_spmd(nc, [{f"in_{k}": a for k, a in arrays.items()}], core_ids=[0])
    return r.results[0]["out"]
```
